# Optimizing a Trainium2 kernel written in Bass

```python
import numpy as np
import jax
import jax.numpy as jnp

def _softmax(x, axis=-1):
    return jax.nn.softmax(x, axis=axis)

def _gelu(x):
    return jax.nn.gelu(x, approximate=True)

def _silu(x):
    return jax.nn.silu(x)

def _sigmoid(x):
    return jax.nn.sigmoid(x)

def _layernorm(x, axis=-1, eps=1e-05):
    m = jnp.mean(x, axis=axis, keepdims=True)
    v = jnp.var(x, axis=axis, keepdims=True)
    return (x - m) / jnp.sqrt(v + eps)

def _scatter_add(tgt, idx, src, axis=0):
    return tgt.at[idx].add(src)

def _segment_sum(src, seg, n):
    return jax.ops.segment_sum(src, seg, n)
kernel_name = 'mk_pixart_seq_d2_seqx_r4_8d52cf'

def setup_inputs(seed: int=0):
    np.random.seed(seed)
    _w = jnp.asarray

    def _rec_inputs():
        import jax
        import jax.numpy as jnp
        _rk = jax.random.key(seed)
        x = -0.0003929 + 0.9999 * jax.random.normal(jax.random.fold_in(_rk, 1), (2, 1024, 256), jnp.float32)
        _lenS = 1024 - jax.random.randint(jax.random.fold_in(_rk, 7), (2,), 0, max(1, 1024 // 4) + 1, jnp.int32)
        _lenS2 = 154 - jax.random.randint(jax.random.fold_in(_rk, 8), (2,), 0, max(1, 154 // 4) + 1, jnp.int32)
        _ctx_1024P = jax.random.normal(jax.random.fold_in(_rk, 11), (2, 16, 256), jnp.float32)
        _ctx_1024c = jax.random.dirichlet(jax.random.fold_in(_rk, 511), 0.3 * jnp.ones((16,), jnp.float32), (2, 154))
        _ctx_1024t = jnp.einsum('bsk,bkd->bsd', _ctx_1024c, _ctx_1024P)
        _ctx_1024t = _ctx_1024t * jax.lax.rsqrt(jnp.mean(jnp.square(_ctx_1024t)) + 1e-12) * 0.953939
        ctx_1024 = -1.39393e-06 + 0.999914 * (_ctx_1024t + 0.3 * jax.random.normal(jax.random.fold_in(_rk, 611), (2, 154, 256), jnp.float32))
        cond_1024 = -0.00920427 + 1.00102 * jax.random.normal(jax.random.fold_in(_rk, 12), (2, 256), jnp.float32)
        return (x, ctx_1024, cond_1024)
    x, ctx_1024, cond_1024 = _rec_inputs()

    def _L0_xcond_setup():
        import jax, jax.numpy as jnp
        import numpy as np
        EPS = 1e-05

        def _ada_ln(x, c, W_ss, b_ss):
            mu = jnp.mean(x, axis=-1, keepdims=True)
            var = jnp.mean((x - mu) ** 2, axis=-1, keepdims=True)
            h = (x - mu) / jnp.sqrt(var + EPS)
            ss = jax.nn.silu(c) @ W_ss + b_ss
            scale, bias = jnp.split(ss, 2, axis=-1)
            return (1.0 + scale)[:, None, :] * h + bias[:, None, :]
        key = jax.random.key(seed)
        ks = jax.random.split(key, 12)
        B, Lq, Lkv, H = (8, 512, 128, 256)
        s = 0.02
        return {'x_q': jax.random.normal(ks[0], (B, Lq, H), jnp.float32), 'x_kv': jax.random.normal(ks[1], (B, Lkv, H), jnp.float32), 't_vec': jax.random.normal(ks[2], (B, H), jnp.float32), 'Wq': jax.random.normal(ks[3], (H, H), jnp.float32) * s, 'bq': jnp.zeros((H,), jnp.float32), 'Wkv': jax.random.normal(ks[4], (H, 2 * H), jnp.float32) * s, 'bkv': jnp.zeros((2 * H,), jnp.float32), 'Wp': jax.random.normal(ks[5], (H, H), jnp.float32) * s, 'bp': jnp.zeros((H,), jnp.float32), 'Wss_q': jax.random.normal(ks[6], (H, 2 * H), jnp.float32) * s, 'bss_q': jnp.zeros((2 * H,), jnp.float32), 'Wss_kv': jax.random.normal(ks[7], (H, 2 * H), jnp.float32) * s, 'bss_kv': jnp.zeros((2 * H,), jnp.float32)}
    _L0_xcond_all = _L0_xcond_setup()
    _L0_xcond_in = {k: v for k, v in _L0_xcond_all.items() if k in ('Wq', 'bq', 'Wkv', 'bkv', 'Wp', 'bp', 'Wss_q', 'bss_q', 'Wss_kv', 'bss_kv')}
    del _L0_xcond_all

    def _L1_xcond_setup():
        import jax, jax.numpy as jnp
        import numpy as np
        H = 256
        RH = 2 * H
        E = 3
        B, T, P = (8, 512, 64)
        LN_EPS = 1e-05

        def _layer_norm(x, gamma, beta):
            mu = jnp.mean(x, axis=-1, keepdims=True)
            var = jnp.mean(jnp.square(x - mu), axis=-1, keepdims=True)
            return (x - mu) * jax.lax.rsqrt(var + LN_EPS) * gamma + beta
        key = jax.random.key(seed)
        ks = jax.random.split(key, 24)
        s = lambda fan_in: 1.0 / np.sqrt(fan_in)
        inp = {'mix_hidden_states': jax.random.normal(ks[0], (B, T, H), jnp.float32), 'global_anchor': jax.random.normal(ks[1], (B, H), jnp.float32), 'prototype_bank': jax.random.normal(ks[2], (B, P, H), jnp.float32), 'ln_gamma': jnp.ones((H,), jnp.float32), 'ln_beta': jnp.zeros((H,), jnp.float32), 'Wq': jax.random.normal(ks[3], (H, H), jnp.float32) * s(H), 'Wk': jax.random.normal(ks[4], (H, H), jnp.float32) * s(H), 'Wv': jax.random.normal(ks[5], (H, H), jnp.float32) * s(H), 'router_W': jax.random.normal(ks[6], (3 * H, E), jnp.float32) * s(3 * H), 'router_b': jnp.zeros((E,), jnp.float32), 'e_w1': jax.random.normal(ks[7], (E, 3 * H, RH), jnp.float32) * s(3 * H), 'e_b1': jnp.zeros((E, RH), jnp.float32), 'e_w2': jax.random.normal(ks[8], (E, RH, H), jnp.float32) * s(RH), 'e_b2': jnp.zeros((E, H), jnp.float32), 'gate_w1': jax.random.normal(ks[9], (3 * H, H), jnp.float32) * s(3 * H), 'gate_b1': jnp.zeros((H,), jnp.float32), 'gate_w2': jax.random.normal(ks[10], (H, H), jnp.float32) * s(H), 'gate_b2': jnp.zeros((H,), jnp.float32), 'out_w': jax.random.normal(ks[11], (H, H), jnp.float32) * s(H), 'out_b': jnp.zeros((H,), jnp.float32)}
        return inp
    _L1_xcond_all = _L1_xcond_setup()
    _L1_xcond_in = {k: v for k, v in _L1_xcond_all.items() if k in ('ln_gamma', 'ln_beta', 'Wq', 'Wk', 'Wv', 'router_W', 'router_b', 'e_w1', 'e_b1', 'e_w2', 'e_b2', 'gate_w1', 'gate_b1', 'gate_w2', 'gate_b2', 'out_w', 'out_b')}
    del _L1_xcond_all
    return {'x': x, 'ctx_1024': ctx_1024, 'cond_1024': cond_1024, 'L0_xcond_Wq': _L0_xcond_in['Wq'], 'L0_xcond_bq': _L0_xcond_in['bq'], 'L0_xcond_Wkv': _L0_xcond_in['Wkv'], 'L0_xcond_bkv': _L0_xcond_in['bkv'], 'L0_xcond_Wp': _L0_xcond_in['Wp'], 'L0_xcond_bp': _L0_xcond_in['bp'], 'L0_xcond_Wss_q': _L0_xcond_in['Wss_q'], 'L0_xcond_bss_q': _L0_xcond_in['bss_q'], 'L0_xcond_Wss_kv': _L0_xcond_in['Wss_kv'], 'L0_xcond_bss_kv': _L0_xcond_in['bss_kv'], 'L1_xcond_ln_gamma': _L1_xcond_in['ln_gamma'], 'L1_xcond_ln_beta': _L1_xcond_in['ln_beta'], 'L1_xcond_Wq': _L1_xcond_in['Wq'], 'L1_xcond_Wk': _L1_xcond_in['Wk'], 'L1_xcond_Wv': _L1_xcond_in['Wv'], 'L1_xcond_router_W': _L1_xcond_in['router_W'], 'L1_xcond_router_b': _L1_xcond_in['router_b'], 'L1_xcond_e_w1': _L1_xcond_in['e_w1'], 'L1_xcond_e_b1': _L1_xcond_in['e_b1'], 'L1_xcond_e_w2': _L1_xcond_in['e_w2'], 'L1_xcond_e_b2': _L1_xcond_in['e_b2'], 'L1_xcond_gate_w1': _L1_xcond_in['gate_w1'], 'L1_xcond_gate_b1': _L1_xcond_in['gate_b1'], 'L1_xcond_gate_w2': _L1_xcond_in['gate_w2'], 'L1_xcond_gate_b2': _L1_xcond_in['gate_b2'], 'L1_xcond_out_w': _L1_xcond_in['out_w'], 'L1_xcond_out_b': _L1_xcond_in['out_b']}

def reference(x, ctx_1024, cond_1024, L0_xcond_Wq, L0_xcond_bq, L0_xcond_Wkv, L0_xcond_bkv, L0_xcond_Wp, L0_xcond_bp, L0_xcond_Wss_q, L0_xcond_bss_q, L0_xcond_Wss_kv, L0_xcond_bss_kv, L1_xcond_ln_gamma, L1_xcond_ln_beta, L1_xcond_Wq, L1_xcond_Wk, L1_xcond_Wv, L1_xcond_router_W, L1_xcond_router_b, L1_xcond_e_w1, L1_xcond_e_b1, L1_xcond_e_w2, L1_xcond_e_b2, L1_xcond_gate_w1, L1_xcond_gate_b1, L1_xcond_gate_w2, L1_xcond_gate_b2, L1_xcond_out_w, L1_xcond_out_b):
    import jax
    import jax.numpy as jnp

    def _L0_xcond_ref(x_q, x_kv, t_vec, Wq, bq, Wkv, bkv, Wp, bp, Wss_q, bss_q, Wss_kv, bss_kv):
        import jax, jax.numpy as jnp
        import numpy as np
        EPS = 1e-05

        def _ada_ln(x, c, W_ss, b_ss):
            mu = jnp.mean(x, axis=-1, keepdims=True)
            var = jnp.mean((x - mu) ** 2, axis=-1, keepdims=True)
            h = (x - mu) / jnp.sqrt(var + EPS)
            ss = jax.nn.silu(c) @ W_ss + b_ss
            scale, bias = jnp.split(ss, 2, axis=-1)
            return (1.0 + scale)[:, None, :] * h + bias[:, None, :]
        B, Lq, H = x_q.shape
        Lkv = x_kv.shape[1]
        nh = 16
        dh = H // nh
        xq = _ada_ln(x_q, t_vec, Wss_q, bss_q)
        xkv = _ada_ln(x_kv, t_vec, Wss_kv, bss_kv)
        q = (xq @ Wq + bq).reshape(B, Lq, nh, dh)
        kv = (xkv @ Wkv + bkv).reshape(B, Lkv, 2, nh, dh)
        k = kv[:, :, 0]
        v = kv[:, :, 1]
        scores = jnp.einsum('bqhd,bkhd->bhqk', q, k) / jnp.sqrt(jnp.float32(dh))
        attn = jax.nn.softmax(scores, axis=-1)
        out = jnp.einsum('bhqk,bkhd->bqhd', attn, v).reshape(B, Lq, H)
        return x_q + (out @ Wp + bp)

    def _L1_xcond_ref(mix_hidden_states, global_anchor, prototype_bank, ln_gamma, ln_beta, Wq, Wk, Wv, router_W, router_b, e_w1, e_b1, e_w2, e_b2, gate_w1, gate_b1, gate_w2, gate_b2, out_w, out_b):
        import jax, jax.numpy as jnp
        import numpy as np
        H = 256
        RH = 2 * H
        E = 3
        B, T, P = (8, 512, 64)
        LN_EPS = 1e-05

        def _layer_norm(x, gamma, beta):
            mu = jnp.mean(x, axis=-1, keepdims=True)
            var = jnp.mean(jnp.square(x - mu), axis=-1, keepdims=True)
            return (x - mu) * jax.lax.rsqrt(var + LN_EPS) * gamma + beta
        x = mix_hidden_states
        nx = _layer_norm(x, ln_gamma, ln_beta)
        q = nx @ Wq
        k = prototype_bank @ Wk
        v = prototype_bank @ Wv
        scores = jnp.einsum('bth,bph->btp', q, k) * H ** (-0.5)
        weights = jax.nn.softmax(scores, axis=-1)
        evidence = jnp.einsum('btp,bph->bth', weights, v)
        anchor = jnp.broadcast_to(global_anchor[:, None, :], nx.shape)
        combined = jnp.concatenate([nx, evidence, anchor], axis=-1)
        router_logits = combined @ router_W + router_b
        router_probs = jax.nn.softmax(router_logits, axis=-1)
        h = jax.nn.silu(jnp.einsum('btc,ecr->bter', combined, e_w1) + e_b1)
        expert_out = jnp.einsum('bter,erh->bteh', h, e_w2) + e_b2
        routed = jnp.sum(expert_out * router_probs[..., None], axis=-2)
        g = jax.nn.sigmoid(jax.nn.silu(combined @ gate_w1 + gate_b1) @ gate_w2 + gate_b2)
        refined_delta = g * (routed @ out_w + out_b)
        return x + refined_delta
    x = _L0_xcond_ref(x, ctx_1024, cond_1024, L0_xcond_Wq, L0_xcond_bq, L0_xcond_Wkv, L0_xcond_bkv, L0_xcond_Wp, L0_xcond_bp, L0_xcond_Wss_q, L0_xcond_bss_q, L0_xcond_Wss_kv, L0_xcond_bss_kv)
    x = _L1_xcond_ref(x, cond_1024, ctx_1024, L1_xcond_ln_gamma, L1_xcond_ln_beta, L1_xcond_Wq, L1_xcond_Wk, L1_xcond_Wv, L1_xcond_router_W, L1_xcond_router_b, L1_xcond_e_w1, L1_xcond_e_b1, L1_xcond_e_w2, L1_xcond_e_b2, L1_xcond_gate_w1, L1_xcond_gate_b1, L1_xcond_gate_w2, L1_xcond_gate_b2, L1_xcond_out_w, L1_xcond_out_b)
    return x

_drawn_inputs = setup_inputs


def setup_inputs(seed=0):
    import zlib

    import numpy as np

    out = dict(_drawn_inputs(seed))
    spreads = {'L0_xcond_bq': (0.0, 2.0),
     'L0_xcond_bkv': (0.0, 0.1),
     'L0_xcond_bp': (0.0, 0.1),
     'L0_xcond_bss_q': (0.0, 2.0),
     'L0_xcond_bss_kv': (0.0, 0.65),
     'L1_xcond_ln_gamma': (1.0, 0.588),
     'L1_xcond_ln_beta': (0.0, 0.607),
     'L1_xcond_router_b': (0.0, 0.413),
     'L1_xcond_e_b1': (0.0, 0.419),
     'L1_xcond_e_b2': (0.0, 0.1),
     'L1_xcond_gate_b1': (0.0, 0.8),
     'L1_xcond_gate_b2': (0.0, 0.8),
     'L1_xcond_out_b': (0.0, 0.1)}
    factors = {'L0_xcond_Wq': 8.0, 'L0_xcond_Wss_q': 8.0}
    for name, (base, spread) in spreads.items():
        noise = np.random.default_rng([zlib.crc32(name.encode()), seed]).standard_normal(out[name].shape)
        drawn = base * np.exp(spread * noise) if base else spread * noise
        out[name] = jnp.asarray(drawn.astype(out[name].dtype))
    for name, factor in factors.items():
        out[name] = (out[name] * factor).astype(out[name].dtype)
    return out
```

```python
from contextlib import ExitStack

import numpy as np
import concourse.bass as bass
from concourse import mybir

F32 = mybir.dt.float32
F32R = mybir.dt.float32r
I32 = mybir.dt.int32
ALU = mybir.AluOpType
ACT = mybir.ActivationFunctionType
AXX = mybir.AxisListType.X

P = 128
B, LQ, D = 2, 1024, 256
LK = 154
NH, DH = 16, 16
KC = D // P
CT = 512
NC = B * LQ // CT
CPB = NC // B
TJ = CT // P
GH = 4
NG = NH // GH
NU = NG + 1
GR = NC * NG
KP = 160
KT = LK - P
E, RH = 3, 512
HB = E * RH // P
GB = D // P
M1 = HB + GB
W1N = M1 * P
SC1 = LK + E
EPS = 1e-5
TAIL3 = 96

SM = {}
_at = 0
for _n, _w in (("cond", KC * B), ("bss", 8), ("bq", NG), ("bk", NG), ("gamma", KC), ("beta", KC),
               ("b1", M1), ("rb", E), ("m0", 1), ("m16", 1), ("m26", 1), ("rwn", KC * E),
               ("rwa", KC * E), ("rwe", KC * E), ("eb2", KC * E)):
    SM[_n] = (_at, _at + _w)
    _at += _w
SMW = _at

SHAPES = {
    "x": (P, B * LQ // P, D), "small": (P, SMW), "ident": (P, P), "ctx": (P, 3, D),
    "ctxT": (P, KC, B, KP), "wss": (P, KC, 8, P), "wq": (P, KC, NG, P), "wk": (P, KC, NG, P),
    "wv": (P, KC, D), "bv": (P, D), "wp": (P, KC, D), "bp": (P, D),
    "pwqT": (P, KC, D), "pwk": (P, KC, D), "pwv": (P, KC, D),
    "w1n": (P, KC, W1N), "w1e": (P, KC, W1N), "w1a": (P, KC, W1N),
    "ew2T": (P, KC, E * RH), "outw": (P, KC, D),
    "outb": (P, D), "gw2": (P, KC, D), "gb2": (P, D),
}


def build(nc, dram, out):
    ctx = ExitStack()
    with ctx:
        def sem(name):
            return ctx.enter_context(nc.semaphore(name))

        def sb(name, shape, dt=F32, where=ctx):
            return where.enter_context(nc.sbuf_tensor(name, list(shape), dt))

        pair = ctx.enter_context(nc.psum_tensor("pair", [P, 2, 512], F32))
        bank = [ctx.enter_context(nc.psum_tensor(f"bank{i}", [P, 512], F32)) for i in range(6)]
        B_P, B_S, B_ST, B_U, B_TOK, B_FEAT = bank[0], [pair[:, i, :] for i in range(2)], bank[1:3], bank[3], bank[4], bank[5]
        B_G, B_Y, B_H, B_SC, B_F = bank[0], B_S, bank[1:3], bank[3], bank[4:6]

        x = sb("x_sb", (P, NC * TJ, D))
        small = sb("small_sb", (P, SMW))
        ident = sb("ident_sb", (P, P))
        negI = sb("negI", (P, P), F32R)
        w1h = sb("w1h", (P, KC, W1N), F32R)
        w1l = sb("w1l", (P, KC, W1N), F32R)
        w2 = sb("w2", (P, HB, D))
        b2 = sb("b2", (P, E, D))
        ab1 = sb("ab1", (P, M1, B))
        kq = sb("kq", (P, KC, B, SC1))
        vf = sb("vf", (P, KC, B, KP))
        vt = sb("vt", (P, KC, B, 3, 32))
        mr = sb("mr", (P, B, E, LK))
        cr = sb("cr", (P, B, E))
        stage = [sb("stage0", (P, KC, 512)), sb("stage1", (P, KC, 256))]
        st6 = sb("st6", (P, 6))
        mv = sb("mv", (P, TJ, 2))
        rs = sb("rs", (P, 4, TJ))

        def sm(name, i=0, n=1):
            return small[:, SM[name][0] + i:SM[name][0] + i + n]

        ops = ExitStack()
        ctxT = sb("ctxT_sb", (P, KC, B, KP), F32, ops)
        pw = sb("pw", (P, 3, KC, D), F32, ops)
        pk = sb("pk", (P, KC, B, KP), F32, ops)
        outb = sb("outb_sb", (P, D), F32, ops)
        ops.close()
        w1_ = ExitStack()
        w1e = sb("w1e_sb", (P, KC, W1N), F32, w1_)
        w1_.close()
        late = ExitStack()
        bs = sb("bs", (P, TJ, D), F32, late)
        acc = sb("acc", (P, TJ, D), F32, late)
        gz = sb("gz", (P, 2, D), F32, late)
        th = sb("th", (P, TJ, D), F32, late)
        late.close()
        sb("place", (P, KC, W1N))

        l0 = ExitStack()
        bp = sb("bp_sb", (P, D), F32, l0)
        wp = sb("wp_sb", (P, KC, D), F32, l0)
        wqh = sb("wqh", (P, KC, NG, P), F32R, l0)
        wql = sb("wql", (P, KC, NG, P), F32R, l0)
        ssc = sb("ssc", (P, 8, B), F32, l0)
        ka = sb("ka", (P, B, NG, GH * LK + P), F32R, l0)
        kb = sb("kb", (P, B, NG, GH * P + P), F32R, l0)
        vmain = sb("vmain", (P, B, NH, 32), F32, l0)
        vtail = sb("vtail", (P, B, NG, P), F32, l0)
        lnt = sb("lnt", (P, 2, D), F32, l0)
        xh = sb("xh", (P, KC, CT), F32R, l0)
        xl = sb("xl", (P, KC, CT), F32R, l0)
        nm = sb("nm", (P, 2, TJ, P), F32R, l0)
        rz = sb("rz", (P, NH), F32, l0)
        pre = ExitStack()
        wss = sb("wss_sb", (P, KC, 8, P), F32, pre)
        wk = sb("wk_sb", (P, KC, NG, P), F32, pre)
        wv = sb("wv_sb", (P, KC, D), F32, pre)
        wq = sb("wq_sb", (P, KC, NG, P), F32, pre)
        ctxt = sb("ctx_sb", (P, 3, D), F32, pre)
        xkv = sb("xkv", (P, KC, B, KP), F32, pre)
        xkv4 = sb("xkv4", (P, KC, B, GH, 32), F32, pre)
        kf = sb("kf", (P, B, KP), F32, pre)
        kh = sb("kh", (P, 2, B, KP), F32R, pre)
        kl = sb("kl", (P, B, KP), F32, pre)
        vtf = sb("vtf", (P, D), F32, pre)
        bv = sb("bv_sb", (P, D), F32, pre)
        pre.close()
        qh = sb("qh", (P, 2, CT), F32R, l0)
        ql = sb("ql", (P, 2, CT), F32R, l0)
        z = sb("z", (P, 2, D), F32, l0)
        zt = sb("zt", (P, 2, KC, P), F32, l0)
        pt = sb("pt", (P, GH + 1, CT), F32, l0)
        u = sb("u", (P, NU, CT), F32, l0)
        xf = sb("xf", (P, KC, CT), F32, l0)
        csilu = sb("csilu", (P, KC, B), F32, l0)
        outw = sb("outw_sb", (P, KC, D), F32, l0)
        l0.close()

        l1 = ExitStack()
        gw2 = sb("gw2_sb", (P, KC, D), F32, l1)
        gb2 = sb("gb2_sb", (P, D), F32, l1)
        mh = sb("mh", (P, B, W1N), F32R, l1)
        ml = sb("ml", (P, B, W1N), F32R, l1)
        mt = sb("mt", (TAIL3, B, W1N), F32R, l1)
        hid = sb("hid", (P, 2, 4, CT), F32, l1)
        hg = sb("hg", (P, GB, CT), F32, l1)
        nxf = sb("nxf", (P, KC, CT), F32, l1)
        nxh = sb("nxh", (P, 2, KC, CT), F32R, l1)
        nxl = sb("nxl", (P, 2, KC, CT), F32R, l1)
        wh = sb("wh", (P, 2, CT), F32R, l1)
        wl = sb("wl", (P, 2, CT), F32R, l1)
        wt = sb("wt", (TAIL3, 2, CT), F32R, l1)
        pb = sb("pb", (P, D), F32, l1)
        lnt1 = sb("lnt1", (P, 2, D), F32, l1)
        pe_ = sb("pe_", (P, 2, LK), F32, l1)
        pn = sb("pn", (P, 2, P), F32, l1)
        pn3 = sb("pn3", (P, 2, 3, 32), F32, l1)
        ttr = sb("ttr", (P, LK), F32, l1)
        nmx = sb("nmx", (P, 2), F32, l1)
        sme = sb("sme", (P, 2), F32, l1)
        rec = sb("rec", (P, 2), F32, l1)
        lg = sb("lg", (P, TJ, E), F32, l1)
        lw = sb("lw", (P, TJ, E), F32, l1)
        lx = sb("lx", (P, TJ), F32, l1)
        le = sb("le", (P, TJ, E), F32, l1)
        pr = sb("pr", (P, 2, TJ, E), F32, l1)
        l1.close()

        ld = {n: sem(f"ld_{n}") for n in SHAPES if n not in ("x", "w1n", "w1a", "ew2T")}
        ld_x = [sem(f"ld_x{c}") for c in range(NC)]
        NW1 = W1N // 256
        PE_PIECES = [("w1a", i) for i in range(4)] + [("ew2T", i) for i in range(3)]
        ld_a, ld_b = [sem(f"ld_piece{i}") for i in range(7)], [sem(f"ld_w1n{i}") for i in range(NW1)]
        stored = sem("stored")
        silu_d, ss_mm, ss_r = sem("silu_done"), sem("ss_mm"), sem("ss_ready")
        zeroed, neg_r, wq_r = sem("zeroed"), sem("neg_ready"), sem("wq_split")
        cl_r, cl_t, xkv_r, x4_r = sem("ctx_ln"), sem("ctx_t"), sem("xkv_ready"), sem("xkv4_ready")
        k_mm, kh_r, v_mm, v_r, ka_r, kb_r = sem("k_mm"), sem("kh_ready"), sem("v_mm"), sem("v_ready"), sem("ka_ready"), sem("kb_ready")
        prep_mm, prep_r, w1_r = sem("prep_mm"), sem("prep_ready"), sem("w1_split")
        ln_r, ln_t, xf_r, xh_r, xl_r = sem("ln_ready"), sem("ln_taken"), sem("xf_ready"), sem("xh_ready"), sem("xl_ready")
        pj_d, qh_r, ql_r = sem("proj_done"), sem("qh_ready"), sem("ql_ready")
        s1_d, mx_d, nm_d = sem("rowscores_done"), sem("max_done"), sem("shift_added")
        st_d, ex_d, av_d, u_r = sem("keyscores_done"), sem("exp_done"), sem("av_done"), sem("u_ready")
        uz_d, z_r, zt_d, zt_r = sem("uz_done"), sem("z_ready"), sem("zt_done"), sem("zt_ready")
        wp_d, xb_r, x1_r = sem("wp_done"), sem("xb_ready"), sem("x1_ready")
        m_mm, m_h, m_l = sem("m_mm"), sem("m_hi"), sem("m_lo")
        l_r, l_t, nf_r, nh_r, nl_r = sem("l_ready"), sem("l_taken"), sem("nxf_ready"), sem("nxh_ready"), sem("nxl_ready")
        sc_d, nm1_r, e1_d, pn_r, w_t = sem("sc_done"), sem("nmx_ready"), sem("e1_done"), sem("pn_ready"), sem("w_taken")
        wh_r, w_r, lg_r, le_r, pr_r, bs_r = sem("wh_ready"), sem("w_ready"), sem("lg_ready"), sem("le_ready"), sem("pr_ready"), sem("bs_ready")
        h_mm, h_r, g_mm, gz_r, th_r = sem("h_mm"), sem("h_ready"), sem("g_mm"), sem("gz_ready"), sem("th_ready")
        y_mm, y_r, o_r = sem("y_mm"), sem("y_used"), sem("out_ready")
        dch, pch = sem("vector_chain"), sem("pool_chain")

        OPS = [("pk", 0), ("pk", 1), ("kq", 0), ("kq", 1), ("v", 0), ("v", 1), ("mr", 0), ("mr", 1), ("b2", 0), ("b2", 1), ("cr",)]
        PREP = OPS + [("anchor", i) for i in range(4)] + [("w2", i, hf) for i in range(3) for hf in range(2)]
        PI = {t: n for n, t in enumerate(PREP)}

        def l0_steps():
            yield ("front", 0)
            yield ("proj", 0)
            for q in range(TJ):
                yield ("rows", 0, q)
            yield ("shift", 0)
            prep = 0
            for g in range(GR):
                c, gi = divmod(g, NG)
                n = g + 1
                if n < GR:
                    yield ("proj", n)
                yield ("keys", g, 0)
                a = TJ * (c - 1) + 2 * gi if c > 0 and gi < 2 else None
                if a is not None:
                    yield ("uz", a)
                yield ("keys", g, 1)
                for q in range(TJ):
                    if n < GR:
                        yield ("rows", n, q)
                    if q < 3:
                        yield ("keys", g, q + 2)
                    if a is not None:
                        yield (("zt", a), ("wp", a), ("uz", a + 1), ("zt", a + 1))[q]
                if a is not None:
                    yield ("wp", a + 1)
                yield ("av", g)
                if n < GR:
                    yield ("shift", n)
                if gi == 2 and c + 1 < NC:
                    yield ("front", c + 1)
                for _ in range(2 if c == 0 or g > 12 else 1):
                    if prep < len(PREP):
                        yield ("prep", prep)
                        prep += 1
            assert prep == len(PREP)
            for j in range(TJ):
                n = TJ * (NC - 1) + j
                yield ("uz", n)
                yield ("zt", n)
                yield ("wp", n)

        MP = [(b, tail, i) for b in range(B) for tail in (0, 1) for i in range(4)]

        def front1(c):
            yield ("ln", c)
            yield ("nxt", c)
            for j in range(TJ):
                yield ("score", TJ * c + j)
                if j > 0:
                    yield ("wtr", TJ * c + j - 1)
            yield ("wtr", TJ * c + TJ - 1)
            yield ("router", c)

        def l1_steps():
            first = list(front1(0))
            for n in range(len(MP)):
                if n < len(first):
                    yield first[n]
                yield ("m", n)
            for c in range(NC):
                take = front1(c + 1) if c + 1 < NC else iter(())

                def one():
                    s = next(take, None)
                    return [s] if s is not None else []
                for m in (HB, HB + 1, 0, 1, 2, 3):
                    yield ("hidden", c, m)
                    yield from one()
                for j in range(TJ):
                    yield ("gate", TJ * c + j)
                for m in range(4, 8):
                    yield ("hidden", c, m)
                    yield from one()
                for j in range(TJ):
                    yield ("expert", c, 0, j)
                for m in range(8, 12):
                    yield ("hidden", c, m)
                    yield from one()
                for e in (1, 2):
                    for j in range(TJ):
                        yield ("expert", c, e, j)
                yield from take

        M_BANK = [B_H[0], B_H[1], B_Y[0], B_Y[1]]
        HORD = [HB, HB + 1] + list(range(HB))

        def hid_buf(c, m):
            return hg[:, m - HB, :] if m >= HB else hid[:, (E * c + m // 4) % 2, m % 4, :]

        def walk(steps, parts):
            for s in steps:
                if s[0] in parts:
                    parts[s[0]](*s[1:])

        block = ctx.enter_context(nc.Block())

        @block.sync
        def _(sp):
            def load(dst, name):
                sp.dma_start(dst, dram[name]).then_inc(ld[name], 16)
            load(small[:], "small")
            load(ctxt[:], "ctx")
            load(wss[:], "wss")
            load(wk[:], "wk")
            load(wv[:], "wv")
            load(bv[:], "bv")
            load(wp[:], "wp")
            for c in range(1, NC):
                sp.dma_start(x[:, TJ * c:TJ * c + TJ, :], dram["x"][:, TJ * c:TJ * c + TJ, :]).then_inc(ld_x[c], 16)
            for n, (name, i) in enumerate(PE_PIECES):
                if n:
                    pname, pi = PE_PIECES[n - 1]
                    sp.wait_ge(prep_mm, 1 + PI[("anchor", pi) if pname == "w1a" else ("w2", pi, 1)])
                w = min(512, SHAPES[name][2] - 512 * i)
                sp.dma_start(stage[0][:, :, 0:w], dram[name][:, :, 512 * i:512 * i + w]).then_inc(ld_a[n], 16)
            sp.wait_ge(prep_r, len(OPS))
            load(w1e[:], "w1e")
            sp.wait_ge(x1_r, TJ * NC)
            load(gw2[:], "gw2")
            load(gb2[:], "gb2")
            for c in range(NC):
                sp.wait_ge(o_r, TJ * c + TJ)
                sp.dma_start(out[:, TJ * c:TJ * c + TJ, :], x[:, TJ * c:TJ * c + TJ, :]).then_inc(stored, 16)
            sp.wait_ge(stored, 16 * NC)

        @block.gpsimd
        def _(pool):
            count = [0]

            def link(ins):
                count[0] += 1
                ins.then_inc(pch, 1)
                pool.wait_ge(pch, count[0])

            g_ = nc.gpsimd
            g_.memset(ka[:].bitcast(F32), 0.0).then_inc(zeroed, 1)
            g_.memset(kb[:].bitcast(F32), 0.0).then_inc(zeroed, 1)
            g_.memset(nm[:].bitcast(F32), 0.0).then_inc(zeroed, 1)
            link(g_.memset(vmain[:], 0.0))
            g_.memset(vmain[:, :, :, DH:DH + 1], 1.0).then_inc(zeroed, 1)
            g_.memset(vtail[:], 0.0).then_inc(zeroed, 1)
            pool.wait_ge(ld["small"], 16)
            pool.wait_ge(zeroed, 5)
            for gi in range(NG):
                pool.wait_ge(kh_r, gi + 1)
                for j in range(GH):
                    r = slice(32 * j, 32 * j + 32)
                    for dst, o, w in ((P * j, 0, P), (P * GH + 32 * j, P, KT)):
                        g_.tensor_scalar(kb[r, :, gi, dst:dst + w], kh[r, gi % 2, :, o:o + w], small[r, SM["m0"][0]:SM["m0"][1]],
                                         small[r, SM["m16"][0]:SM["m16"][1]], ALU.mult, ALU.add).then_inc(kb_r, 1)
                        pool.wait_ge(kb_r, 2 * (GH * gi + j) + (1 if dst < P * GH else 2))

            def front(c):
                if c == 0:
                    pool.wait_ge(ld["bp"], 16)
                for j in range(TJ):
                    n = TJ * c + j
                    pool.wait_ge(ln_r, n + 1)
                    g_.tensor_tensor(x[:, n, :], x[:, n, :], bp[:], ALU.add).then_inc(xb_r, 1)

            def piece(i):
                o = slice(256 * i, 256 * i + 256)
                pool.wait_ge(ld_b[i], 16)
                g_.tensor_copy(w1h[:, :, o], stage[1][:]).then_inc(w1_r, 1)
                pool.wait_ge(w1_r, 2 * i + 1)
                g_.tensor_tensor(w1l[:, :, o], stage[1][:], w1h[:, :, o], ALU.subtract).then_inc(w1_r, 1)
                if i + 1 < NW1:
                    pool.wait_ge(w1_r, 2 * i + 2)
                    pool.dma_start(stage[1][:], dram["w1n"][:, :, 256 * (i + 1):256 * (i + 2)]).then_inc(ld_b[i + 1], 16)

            def av(g):
                if g < NW1:
                    piece(g)

            pool.dma_start(stage[1][:], dram["w1n"][:, :, 0:256]).then_inc(ld_b[0], 16)
            walk(l0_steps(), {"front": front, "av": av})

            def router(c):
                pool.wait_ge(pr_r, c + 1)
                if c == 0:
                    pool.wait_ge(prep_r, len(PREP))
                    pool.wait_ge(m_mm, len(MP))
                if c:
                    pool.wait_ge(y_r, 4 * E * (c - 1) + TJ)
                for j in range(TJ):
                    link(g_.tensor_scalar(bs[:, j, :], b2[:, 0, :], pr[:, c % 2, j, 0:1], None, ALU.mult))
                    for e in (1, 2):
                        link(g_.tensor_scalar(pb[:], b2[:, e, :], pr[:, c % 2, j, e:e + 1], None, ALU.mult))
                        ins = g_.tensor_tensor(bs[:, j, :], bs[:, j, :], pb[:], ALU.add)
                        if e == 1:
                            link(ins)
                    ins.then_inc(bs_r, 1)
                    pool.wait_ge(bs_r, TJ * c + j + 1)

            def expert(c, e, j):
                if e < E - 1:
                    return
                n = TJ * c + j
                pool.wait_ge(y_r, TJ * (E * c + e) + j + 1)
                pool.wait_ge(th_r, n + 1)
                link(g_.tensor_scalar(th[:, j, :], th[:, j, :], 1.0, None, ALU.add))
                link(g_.tensor_tensor(acc[:, j, :], th[:, j, :], acc[:, j, :], ALU.mult))
                g_.tensor_tensor(x[:, n, :], x[:, n, :], acc[:, j, :], ALU.add).then_inc(o_r, 1)

            walk(l1_steps(), {"router": router, "expert": expert})

        @block.scalar
        def _(act):
            def load(dst, name):
                act.dma_start(dst, dram[name]).then_inc(ld[name], 16)
            act.dma_start(x[:, 0:TJ, :], dram["x"][:, 0:TJ, :]).then_inc(ld_x[0], 16)
            load(ident[:], "ident")
            load(wq[:], "wq")
            load(bp[:], "bp")
            load(ctxT[:], "ctxT")
            load(pw[:, 0], "pwqT")
            load(pw[:, 1], "pwk")
            load(pw[:, 2], "pwv")
            load(outw[:], "outw")
            load(outb[:], "outb")
            A = nc.scalar.activation
            act.wait_ge(ld["small"], 16)
            A(csilu[:], small[:, 0:KC * B].rearrange("p (k b) -> p k b", k=KC), ACT.Silu).then_inc(silu_d, 1)

            def front(c):
                b = c // CPB
                act.wait_ge(ln_t, TJ * (c + 1))
                if c == 0:
                    act.wait_ge(v_r, 2 * B + 1)
                for k in range(KC):
                    if c:
                        act.wait_ge(xl_r, KC * (c - 1) + k + 1)
                    A(xf[:, k, :], B_S[k], ACT.Identity, bias=ssc[:, 2 + k, b:b + 1], scale=ssc[:, k, b:b + 1]).then_inc(xf_r, 1)

            def proj(g):
                act.wait_ge(pj_d, g + 1)
                if g >= 2:
                    act.wait_ge(st_d, (GH + 1) * (g - 1))
                A(qh[:, g % 2, :], B_P[:, :], ACT.Identity, bias=sm("bq", g % NG)).then_inc(qh_r, 1)

            def keys(g, k):
                n = (GH + 1) * g + k
                act.wait_ge(st_d, n + 1)
                if k == 0 and g:
                    act.wait_ge(av_d, g)
                A(pt[:, k, :], B_ST[n % 2][:, :], ACT.Exp).then_inc(ex_d, 1)

            def av(g):
                c = g // NG
                act.wait_ge(av_d, g + 1)
                if g >= NU:
                    act.wait_ge(uz_d, TJ * ((g - NU) // NG + 1))
                A(u[:, g % NU, :], B_U[:, :], ACT.Copy).then_inc(u_r, 1)

            def ztr(n):
                act.wait_ge(zt_d, n + 1)
                if n >= 2:
                    act.wait_ge(wp_d, n - 1)
                A(zt[:, n % 2, :, :], B_FEAT[:, 0:D].rearrange("p (k n) -> p k n", k=KC), ACT.Copy).then_inc(zt_r, 1)

            walk(l0_steps(), {"front": front, "proj": proj, "keys": keys, "av": av, "zt": ztr})

            def mpiece(n):
                b, tail, i = MP[n]
                w = min(512, W1N - 512 * i)
                act.wait_ge(m_mm, n + 1)
                if n == 0:
                    act.wait_ge(x1_r, TJ * NC)
                src = M_BANK[n % 4]
                o = slice(512 * i, 512 * i + w)
                if tail:
                    A(mt[:, b, o], src[0:TAIL3, 0:w], ACT.Copy).then_inc(m_h, 1)
                else:
                    A(mh[:, b, o], src[:, 0:w], ACT.Copy).then_inc(m_h, 1)

            def nxt(c):
                act.wait_ge(l_t, TJ * (c + 1))
                if c == 0:
                    act.wait_ge(x1_r, TJ * NC)
                if c:
                    act.wait_ge(sc_d, TJ * c)
                for k in range(KC):
                    if c:
                        act.wait_ge(nl_r, KC * (c - 1) + k + 1)
                    A(nxf[:, k, :], B_F[k][:, :], ACT.Identity, bias=sm("beta", k), scale=sm("gamma", k)).then_inc(nf_r, 1)

            def score(n):
                act.wait_ge(nm1_r, n + 1)
                if n >= 2:
                    act.wait_ge(lg_r, n - 1)
                A(pe_[:, n % 2, :], B_SC[:, 0:LK], ACT.Exp, bias=nmx[:, n % 2:n % 2 + 1],
                  accum_out=sme[:, n % 2:n % 2 + 1]).then_inc(e1_d, 1)

            def router(c):
                act.wait_ge(w_t, TJ * (c + 1))
                if c >= 2:
                    act.wait_ge(h_mm, M1 * (c - 1))
                A(wh[:, c % 2, :], B_F[0][:, :], ACT.Copy).then_inc(wh_r, 1)
                A(wt[:, c % 2, :], B_F[1][0:TAIL3, :], ACT.Copy).then_inc(wh_r, 1)
                act.wait_ge(le_r, 2 * c + 1)
                A(le[:], lg[:], ACT.Exp).then_inc(le_r, 1)

            def hidden(c, m):
                n = M1 * c + HORD.index(m)
                act.wait_ge(h_mm, n + 1)
                q = E * c + m // 4
                if m >= HB:
                    if c:
                        act.wait_ge(g_mm, TJ * c)
                elif q >= 2:
                    act.wait_ge(y_mm, TJ * (q - 1))
                A(hid_buf(c, m), B_H[n % 2][:, :], ACT.Silu, bias=ab1[:, m, c // CPB:c // CPB + 1]).then_inc(h_r, 1)

            def gate(n):
                act.wait_ge(gz_r, n + 1)
                if n >= TJ:
                    act.wait_ge(o_r, n - TJ + 1)
                A(th[:, n % TJ, :], gz[:, n % 2, :], ACT.Tanh, scale=0.5).then_inc(th_r, 1)

            walk(l1_steps(), {"m": mpiece, "nxt": nxt, "score": score, "router": router, "hidden": hidden, "gate": gate})

        @block.vector
        def _(dve):
            V = nc.vector
            count = [0]

            def link(ins):
                count[0] += 1
                ins.then_inc(dch, 1)
                dve.wait_ge(dch, count[0])

            def stats(t, src, rows=P):
                link(V.bn_stats(st6[0:rows, :], src))
                link(V.bn_aggr(mv[0:rows, t, :], st6[0:rows, :]))

            def rsqrt():
                y, v, t, guess = rs[:, 0, :], rs[:, 1, :], rs[:, 2, :], rs[:, 3, :]
                link(V.tensor_scalar(v, mv[:, :, 1], EPS, None, ALU.add))
                link(V.tensor_scalar(guess.bitcast(I32), v.bitcast(I32), 1, None, ALU.logical_shift_right))
                link(V.tensor_scalar(y.bitcast(I32), guess.bitcast(I32), -1.0, float(0x5F3759DF), ALU.mult, ALU.add))
                link(V.tensor_scalar(v, v, 0.5, None, ALU.mult))
                for _ in range(4):
                    link(V.tensor_tensor(t, y, y, ALU.mult))
                    link(V.tensor_tensor(t, t, v, ALU.mult))
                    link(V.scalar_tensor_tensor(y, t, 1.5, y, ALU.subtract, ALU.mult))

            def normalised(dst, t, src, rows=P):
                return V.tensor_scalar(dst, src, mv[0:rows, t, 0:1], rs[0:rows, 0, t:t + 1], ALU.subtract, ALU.mult)

            dve.wait_ge(ld["ctx"], 16)
            link(V.memset(mv[:], 1.0))
            for t in range(3):
                w = P if t < 2 else 64
                stats(t, ctxt[0:w, t, :], w)
            rsqrt()
            for t in range(3):
                w = P if t < 2 else 64
                normalised(ctxt[0:w, t, :], t, ctxt[0:w, t, :], w).then_inc(cl_r, 1)
            dve.wait_ge(ld["small"], 16)
            dve.wait_ge(ss_mm, 1)
            link(V.tensor_tensor(ssc[:], B_TOK[:, 0:8 * B].rearrange("p (m b) -> p m b", m=8),
                                 sm("bss", 0, 8).unsqueeze(2).broadcast_to([P, 8, B]), ALU.add))
            link(V.tensor_scalar(ssc[:, 0:2, :], ssc[:, 0:2, :], 1.0, None, ALU.add))
            V.tensor_scalar(ssc[:, 4:6, :], ssc[:, 4:6, :], 1.0, None, ALU.add).then_inc(ss_r, 1)
            dve.wait_ge(ss_r, 1)
            dve.wait_ge(cl_t, 1)
            for k in range(KC):
                for b in range(B):
                    for dst, o, w in ((0, P * b, P), (P, B * P + 32 * b, 32)):
                        ins = V.tensor_scalar(xkv[:, k, b, dst:dst + w], B_S[k][:, o:o + w], ssc[:, 4 + k, b:b + 1],
                                              ssc[:, 6 + k, b:b + 1], ALU.mult, ALU.add)
                        if (k, b, dst) == (KC - 1, B - 1, P):
                            ins.then_inc(xkv_r, 1)
                        else:
                            link(ins)
            dve.wait_ge(xkv_r, 1)
            for k in range(KC):
                ins = V.tensor_copy(xkv4[:, k, :, :, :], xkv[:, k, :, P:KP].unsqueeze(2).broadcast_to([P, B, GH, 32]))
                if k < KC - 1:
                    link(ins)
            ins.then_inc(x4_r, 1)
            dve.wait_ge(zeroed, 1)
            for gi in range(NG):
                dve.wait_ge(k_mm, gi + 1)
                link(V.tensor_scalar(kf[:], B_ST[gi % 2][:, 0:B * KP].rearrange("p (b n) -> p b n", b=B), sm("bk", gi),
                                     DH ** -0.5, ALU.add, ALU.mult))
                if gi >= 2:
                    dve.wait_ge(kb_r, 2 * GH * (gi - 1))
                V.tensor_copy(kh[:, gi % 2], kf[:]).then_inc(kh_r, 1)
                dve.wait_ge(kh_r, gi + 1)
                link(V.tensor_tensor(kl[:], kf[:], kh[:, gi % 2], ALU.subtract))
                link(V.tensor_tensor(kf[:], kh[:, gi % 2], kl[:], ALU.subtract))
                for j in range(GH):
                    r = slice(32 * j, 32 * j + 32)
                    m0 = small[r, SM["m0"][0]:SM["m0"][1]]
                    for dst, o, w in ((LK * j, 0, LK), (LK * GH + 32 * j, P, KT)):
                        V.scalar_tensor_tensor(ka[r, :, gi, dst:dst + w], kf[r, :, o:o + w], m0, kl[r, :, o:o + w],
                                               ALU.mult, ALU.add).then_inc(ka_r, 1)
                dve.wait_ge(ka_r, 2 * GH * (gi + 1))
            dve.wait_ge(ld["wq"], 16)
            V.tensor_copy(wqh[:], wq[:]).then_inc(wq_r, 1)
            dve.wait_ge(wq_r, 1)
            V.tensor_tensor(wql[:], wq[:], wqh[:], ALU.subtract).then_inc(wq_r, 1)
            dve.wait_ge(ld["ident"], 16)
            V.tensor_scalar(negI[:], ident[:], -1.0, None, ALU.mult).then_inc(neg_r, 1)
            dve.wait_ge(ld["bv"], 16)
            dve.wait_ge(zeroed, 5)
            for n in range(2 * B):
                b, tail = n % B, n // B
                src = B_U if n % 2 else B_FEAT
                dve.wait_ge(v_mm, n + 1)
                if not tail:
                    V.tensor_tensor(vmain[:, b, :, 0:DH], src[:, 0:D].rearrange("p (h d) -> p h d", h=NH),
                                    bv[:].rearrange("p (h d) -> p h d", h=NH), ALU.add).then_inc(v_r, 1)
                else:
                    V.tensor_tensor(vtf[:], src[:, 0:D], bv[:], ALU.add).then_inc(v_r, 1)
                    dve.wait_ge(v_r, n + 1)
                    for j in range(GH):
                        r = slice(32 * j, 32 * j + 32)
                        m26 = small[r, SM["m26"][0]:SM["m26"][1]]
                        link(V.tensor_scalar(vtail[r, b, :, 32 * j:32 * j + DH],
                                             vtf[r, :].rearrange("p (g j d) -> p g j d", g=NG, j=GH)[:, :, j, :],
                                             m26, None, ALU.mult))
                        link(V.tensor_copy(vtail[r, b, :, 32 * j + DH:32 * j + DH + 1],
                                           m26.unsqueeze(1).broadcast_to([32, NG, 1])))
            V.tensor_copy(kq[:, :, 0, LK:SC1], sm("rwn", 0, KC * E).rearrange("p (k e) -> p k e", k=KC)).then_inc(v_r, 1)
            link(V.tensor_copy(kq[:, :, 1, LK:SC1], sm("rwn", 0, KC * E).rearrange("p (k e) -> p k e", k=KC)))

            def front(c):
                dve.wait_ge(ld_x[c], 16)
                for j in range(TJ):
                    stats(j, x[:, TJ * c + j, :])
                rsqrt()
                for j in range(TJ):
                    n = TJ * c + j
                    if n >= 2:
                        dve.wait_ge(ln_t, n - 1)
                    normalised(lnt[:, j % 2, :], j, x[:, n, :]).then_inc(ln_r, 1)
                dve.wait_ge(ln_r, TJ * (c + 1))
                for k in range(KC):
                    dve.wait_ge(xf_r, KC * c + k + 1)
                    if c:
                        dve.wait_ge(pj_d, NG * c)
                    V.tensor_copy(xh[:, k, :], xf[:, k, :]).then_inc(xh_r, 1)
                    dve.wait_ge(xh_r, KC * c + k + 1)
                    V.tensor_tensor(xl[:, k, :], xf[:, k, :], xh[:, k, :], ALU.subtract).then_inc(xl_r, 1)

            def rows(g, q):
                n = TJ * g + q
                dve.wait_ge(s1_d, n + 1)
                if g >= 2:
                    dve.wait_ge(nm_d, g - 1)
                V.tensor_reduce(nm[:, g % 2, q, :].rearrange("p (h w) -> p h w", w=32)[:, :, DH:DH + 1],
                                pair[:, :, 0:2 * LK].rearrange("p s (a n) -> p s a n", a=2), AXX, ALU.max).then_inc(mx_d, 1)

            def shift(g):
                dve.wait_ge(nm_d, g + 1)
                dve.wait_ge(qh_r, g + 1)
                if g >= 2:
                    dve.wait_ge(st_d, (GH + 1) * (g - 1))
                V.scalar_tensor_tensor(ql[:, g % 2, :], B_P[:, :], sm("bq", g % NG), qh[:, g % 2, :],
                                       ALU.add, ALU.subtract).then_inc(ql_r, 1)

            def uz(n):
                dve.wait_ge(uz_d, n + 1)
                heads = B_TOK[:, :].rearrange("p (h w) -> p h w", w=32)
                link(V.reciprocal(rz[:], heads[:, :, DH]))
                if n >= 2:
                    dve.wait_ge(zt_d, n - 1)
                V.tensor_tensor(z[:, n % 2, :].rearrange("p (h d) -> p h d", h=NH), heads[:, :, 0:DH],
                                rz[:].unsqueeze(2).broadcast_to([P, NH, DH]), ALU.mult).then_inc(z_r, 1)

            def wproj(n):
                dve.wait_ge(wp_d, n + 1)
                dve.wait_ge(xb_r, n + 1)
                V.tensor_tensor(x[:, n, :], B_TOK[:, 0:D], x[:, n, :], ALU.add).then_inc(x1_r, 1)

            def prep(n):
                t = PREP[n]
                dve.wait_ge(prep_mm, n + 1)
                src = B_FEAT
                if t[0] == "anchor":
                    m0 = 4 * t[1]
                    w = min(4, M1 - m0)
                    ins = V.tensor_tensor(ab1[:, m0:m0 + w, :], src[:, 0:B * w].rearrange("p (m b) -> p m b", m=w),
                                          sm("b1", m0, w).unsqueeze(2).broadcast_to([P, w, B]), ALU.add)
                elif t[0] == "w2":
                    r = 4 * t[1] + 2 * t[2]
                    ins = V.tensor_copy(w2[:, r:r + 2, :], src[:, :].rearrange("p (r n) -> p r n", r=2))
                elif t[0] == "pk":
                    ins = V.tensor_copy(pk[:, t[1]], src[:, 0:B * KP].rearrange("p (b n) -> p b n", b=B))
                elif t[0] == "kq":
                    ins = V.tensor_scalar(kq[:, t[1], :, 0:LK], src[:, 0:B * KP].rearrange("p (b n) -> p b n", b=B)[:, :, 0:LK],
                                          D ** -0.5, None, ALU.mult)
                elif t[0] == "v":
                    v4 = src[:, 0:B * KP].rearrange("p (b n) -> p b n", b=B)
                    link(V.tensor_copy(vf[:, t[1]], v4))
                    ins = V.tensor_copy(vt[:, t[1]], v4[:, :, P:KP].unsqueeze(2).broadcast_to([P, B, 3, 32]))
                elif t[0] == "mr":
                    ins = V.tensor_copy(mr[:, t[1]], src[:, 0:E * LK].rearrange("p (e n) -> p e n", e=E))
                elif t[0] == "b2":
                    w = 2 - t[1]
                    dve.wait_ge(ld["outb"], 16)
                    ins = V.tensor_tensor(b2[:, 2 * t[1]:2 * t[1] + w, :], src[:, 0:w * D].rearrange("p (e n) -> p e n", e=w),
                                          outb[:].unsqueeze(1).broadcast_to([P, w, D]), ALU.add)
                else:
                    ins = V.tensor_tensor(cr[:], src[:, 0:B * E].rearrange("p (b e) -> p b e", b=B),
                                          sm("rb", 0, E).unsqueeze(1).broadcast_to([P, B, E]), ALU.add)
                ins.then_inc(prep_r, 1)

            walk(l0_steps(), {"front": front, "rows": rows, "shift": shift, "uz": uz, "wp": wproj, "prep": prep})

            dve.wait_ge(x1_r, TJ * NC)
            link(V.memset(pn3[:], 0.0))

            def mpiece(n):
                b, tail, i = MP[n]
                w = min(512, W1N - 512 * i)
                o = slice(512 * i, 512 * i + w)
                dve.wait_ge(m_h, n + 1)
                src = M_BANK[n % 4]
                if tail:
                    ins = V.tensor_tensor(mt[32:64, b, o], src[32:64, 0:w], mt[32:64, b, o], ALU.subtract)
                else:
                    ins = V.tensor_tensor(ml[:, b, o], src[:, 0:w], mh[:, b, o], ALU.subtract)
                ins.then_inc(m_l, 1)

            def ln(c):
                for j in range(TJ):
                    stats(j, x[:, TJ * c + j, :])
                rsqrt()
                for j in range(TJ):
                    n = TJ * c + j
                    if n >= 2:
                        dve.wait_ge(l_t, n - 1)
                    normalised(lnt1[:, n % 2, :], j, x[:, n, :]).then_inc(l_r, 1)
                dve.wait_ge(l_r, TJ * (c + 1))

            def nxt(c):
                for k in range(KC):
                    dve.wait_ge(nf_r, KC * c + k + 1)
                    if c >= 2:
                        dve.wait_ge(h_mm, M1 * (c - 1))
                    V.tensor_copy(nxh[:, c % 2, k, :], nxf[:, k, :]).then_inc(nh_r, 1)
                    dve.wait_ge(nh_r, KC * c + k + 1)
                    V.tensor_tensor(nxl[:, c % 2, k, :], nxf[:, k, :], nxh[:, c % 2, k, :], ALU.subtract).then_inc(nl_r, 1)

            def score(n):
                j = n % TJ
                dve.wait_ge(sc_d, n + 1)
                if j == 0 and n:
                    dve.wait_ge(le_r, 2 * (n // TJ))
                link(V.tensor_copy(lg[:, j, :], B_SC[:, LK:SC1]))
                V.tensor_reduce(nmx[:, n % 2:n % 2 + 1], B_SC[:, 0:LK], AXX, ALU.max, negate=True).then_inc(nm1_r, 1)

            def wtr(n):
                j, b, i = n % TJ, n // TJ // CPB, n % 2
                dve.wait_ge(e1_d, n + 1)
                link(V.reciprocal(rec[:, i:i + 1], sme[:, i:i + 1]))
                if n >= 2:
                    dve.wait_ge(w_t, n - 1)
                link(V.tensor_scalar(pn[:, i, :], pe_[:, i, 0:P], rec[:, i:i + 1], None, ALU.mult))
                V.tensor_scalar(pn3[:, i, :, 0:KT], pe_[:, i, P:LK].unsqueeze(1).broadcast_to([P, 3, KT]),
                                rec[:, i:i + 1], None, ALU.mult).then_inc(pn_r, 1)
                for e in range(E):
                    ins = V.tensor_tensor_reduce(out=ttr[:], in0=pe_[:, i, :], in1=mr[:, b, e, :], scale=rec[:, i:i + 1],
                                                 scalar=0.0, op0=ALU.mult, op1=ALU.add, accum_out=lw[:, j, e:e + 1])
                    if e < E - 1:
                        link(ins)
                ins.then_inc(lg_r, 1)

            def router(c):
                b = c // CPB
                dve.wait_ge(wh_r, 2 * c + 1)
                V.tensor_tensor(wl[:, c % 2, :], B_F[0][:, :], wh[:, c % 2, :], ALU.subtract).then_inc(w_r, 1)
                dve.wait_ge(wh_r, 2 * c + 2)
                V.tensor_tensor(wt[64:96, c % 2, :], B_F[1][64:96, :], wt[64:96, c % 2, :], ALU.subtract).then_inc(w_r, 1)
                dve.wait_ge(lg_r, TJ * (c + 1))
                link(V.tensor_tensor(lg[:], lg[:], lw[:], ALU.add))
                link(V.tensor_tensor(lg[:], lg[:], cr[:, b, :].unsqueeze(1).broadcast_to([P, TJ, E]), ALU.add))
                link(V.tensor_reduce(lx[:], lg[:], AXX, ALU.max))
                V.tensor_tensor(lg[:], lg[:], lx[:].unsqueeze(2).broadcast_to([P, TJ, E]), ALU.subtract).then_inc(le_r, 1)
                dve.wait_ge(le_r, 2 * c + 2)
                link(V.tensor_reduce(lx[:], le[:], AXX, ALU.add))
                link(V.reciprocal(lx[:], lx[:]))
                if c >= 2:
                    dve.wait_ge(bs_r, TJ * (c - 1))
                V.scalar_tensor_tensor(pr[:, c % 2], le[:], 0.5, lx[:].unsqueeze(2).broadcast_to([P, TJ, E]),
                                       ALU.mult, ALU.mult).then_inc(pr_r, 1)

            def gate(n):
                if n == 0:
                    dve.wait_ge(ld["gb2"], 16)
                dve.wait_ge(g_mm, n + 1)
                if n >= 2:
                    dve.wait_ge(th_r, n - 1)
                V.tensor_tensor(gz[:, n % 2, :], B_G[:, 0:D], gb2[:], ALU.add).then_inc(gz_r, 1)

            def expert(c, e, j):
                n = TJ * (E * c + e) + j
                dve.wait_ge(y_mm, n + 1)
                if e == 0:
                    dve.wait_ge(bs_r, TJ * c + j + 1)
                    if c:
                        dve.wait_ge(o_r, TJ * (c - 1) + j + 1)
                else:
                    dve.wait_ge(y_r, n - TJ + 1)
                V.scalar_tensor_tensor(acc[:, j, :], B_Y[n % 2][:, 0:D], pr[:, c % 2, j, e:e + 1],
                                       bs[:, j, :] if e == 0 else acc[:, j, :], ALU.mult, ALU.add).then_inc(y_r, 1)

            walk(l1_steps(), {"m": mpiece, "ln": ln, "nxt": nxt, "score": score, "wtr": wtr, "router": router,
                              "gate": gate, "expert": expert})

        @block.tensor
        def _(pe):
            mm = nc.tensor.matmul

            def same(column):
                return column.broadcast_to([P, P])

            def passes(dst, terms, first=True, last=True, free=False):
                for i, (a, b_) in enumerate(terms):
                    ins = mm(dst, a, b_, start=first and i == 0, stop=last and i == len(terms) - 1,
                             skip_group_check=free)
                return ins

            pe.wait_ge(ld["wss"], 16)
            pe.wait_ge(silu_d, 1)
            for m in range(8):
                ins = passes(B_TOK[:, B * m:B * m + B], [(wss[:, k, m, :], csilu[:, k, :]) for k in range(KC)])
            ins.then_inc(ss_mm, 1)
            pe.wait_ge(ld["ident"], 16)
            for t in range(3):
                pe.wait_ge(cl_r, t + 1)
                w = P if t < 2 else 64
                for k in range(KC):
                    ins = nc.tensor.transpose(B_S[k][:, P * t:P * t + w], ctxt[0:w, t, P * k:P * k + P], ident[0:w, 0:w])
            ins.then_inc(cl_t, 1)
            pe.wait_ge(ld["wk"], 16)
            pe.wait_ge(xkv_r, 1)
            for g in range(NG):
                if g >= 2:
                    pe.wait_ge(kh_r, g - 1)
                passes(B_ST[g % 2][:, 0:B * KP],
                       [(wk[:, k, g, :], xkv[:, k, :, :].rearrange("p b n -> p (b n)")) for k in range(KC)]).then_inc(k_mm, 1)
            pe.wait_ge(ld["wv"], 16)
            pe.wait_ge(x4_r, 1)
            for n in range(2 * B):
                b, tail = n % B, n // B
                if n >= 2:
                    pe.wait_ge(v_r, n - 1)
                bk_ = B_U if n % 2 else B_FEAT
                passes(bk_[:, 0:D],
                       [((xkv4[:, k, b, :, :].rearrange("p a n -> p (a n)") if tail else xkv[:, k, b, 0:P]), wv[:, k, :])
                        for k in range(KC)]).then_inc(v_mm, 1)

            def front(c):
                if c:
                    pe.wait_ge(mx_d, TJ * NG * c)
                else:
                    pe.wait_ge(xkv_r, 1)
                for j in range(TJ):
                    pe.wait_ge(ln_r, TJ * c + j + 1)
                    for k in range(KC):
                        ins = nc.tensor.transpose(B_S[k][:, P * j:P * j + P], lnt[:, j % 2, P * k:P * k + P], ident[:])
                    ins.then_inc(ln_t, 1)

            def proj(g):
                c, gi = divmod(g, NG)
                if g == 0:
                    pe.wait_ge(wq_r, 2)
                if g:
                    pe.wait_ge(ql_r, g)
                pe.wait_ge(xl_r, KC * (c + 1))
                h, l = xh, xl
                terms = []
                for k in range(KC):
                    terms += [(wqh[:, k, gi, :], h[:, k, :]), (wqh[:, k, gi, :], l[:, k, :]), (wql[:, k, gi, :], h[:, k, :])]
                passes(B_P[:, :], terms, last=False, free=True).then_inc(pj_d, 1)

            def rows(g, q):
                c, gi = divmod(g, NG)
                n = TJ * g + q
                pe.wait_ge(qh_r, g + 1)
                if gi == 0 and q == 0:
                    pe.wait_ge(xf_r, KC * (c + 1))
                    pe.wait_ge(ka_r, 2 * NG * GH)
                if n:
                    pe.wait_ge(mx_d, n)
                for s in range(2):
                    ins = mm(B_S[s][:, 0:2 * LK], qh[:, g % 2, P * q:P * q + P],
                             ka[:, c // CPB, gi, 2 * LK * s:2 * LK * (s + 1)], start=True, stop=True)
                ins.then_inc(s1_d, 1)

            def shift(g):
                pe.wait_ge(neg_r, 1)
                for q in range(TJ):
                    pe.wait_ge(mx_d, TJ * g + q + 1)
                    ins = mm(B_P[:, P * q:P * q + P], nm[:, g % 2, q, :], negI[:], start=False, stop=q == TJ - 1,
                             skip_group_check=True)
                ins.then_inc(nm_d, 1)

            def keys(g, k):
                c, gi = divmod(g, NG)
                b = c // CPB
                n = (GH + 1) * g + k
                if k == 0:
                    pe.wait_ge(ql_r, g + 1)
                if n == 0:
                    pe.wait_ge(kb_r, 2 * NG * GH)
                if n >= 2:
                    pe.wait_ge(ex_d, n - 1)
                if k < GH:
                    a, b_ = ka[:, b, gi, LK * k:LK * k + P], kb[:, b, gi, P * k:P * k + P]
                else:
                    a, b_ = ka[:, b, gi, LK * GH:LK * GH + P], kb[:, b, gi, P * GH:P * GH + P]
                passes(B_ST[n % 2][:, :], [(a, qh[:, g % 2, :]), (b_, ql[:, g % 2, :])]).then_inc(st_d, 1)

            def av(g):
                c, gi = divmod(g, NG)
                b = c // CPB
                if g == 0:
                    pe.wait_ge(v_r, 2 * B + 1)
                else:
                    pe.wait_ge(u_r, g)
                for j in range(GH):
                    pe.wait_ge(ex_d, (GH + 1) * g + j + 1)
                    mm(B_U[32 * j:32 * j + 32, :], vmain[:, b, GH * gi + j, :], pt[:, j, :], start=True, stop=False,
                       skip_group_check=True)
                pe.wait_ge(ex_d, (GH + 1) * (g + 1))
                mm(B_U[:, :], vtail[:, b, gi, :], pt[:, GH, :], start=False, stop=True,
                   skip_group_check=True).then_inc(av_d, 1)

            def uz(n):
                c, j = divmod(n, TJ)
                pe.wait_ge(u_r, NG * (c + 1))
                if n:
                    pe.wait_ge(x1_r, n)
                for gi in range(NG):
                    ins = nc.tensor.transpose(B_TOK[:, P * gi:P * gi + P], u[:, (NG * c + gi) % NU, P * j:P * j + P], ident[:])
                ins.then_inc(uz_d, 1)

            def ztr(n):
                pe.wait_ge(z_r, n + 1)
                if n:
                    pe.wait_ge(zt_r, n)
                for k in range(KC):
                    ins = nc.tensor.transpose(B_FEAT[:, P * k:P * k + P], z[:, n % 2, P * k:P * k + P], ident[:])
                ins.then_inc(zt_d, 1)

            def wproj(n):
                if n == 0:
                    pe.wait_ge(ld["wp"], 16)
                pe.wait_ge(zt_r, n + 1)
                passes(B_TOK[:, 0:D], [(zt[:, n % 2, k, :], wp[:, k, :]) for k in range(KC)]).then_inc(wp_d, 1)

            issued = {"zt": 0, "prep": 0}

            def zt_step(n):
                pe.wait_ge(prep_r, issued["prep"]) if issued["prep"] else None
                issued["zt"] += 1
                ztr(n)

            def prep(n):
                t = PREP[n]
                if n:
                    pe.wait_ge(prep_r, n)
                if issued["zt"]:
                    pe.wait_ge(zt_r, issued["zt"])
                issued["prep"] += 1
                if n == 0:
                    pe.wait_ge(v_r, 2 * B)
                st, bk_ = stage[0], B_FEAT
                if t[0] == "anchor":
                    i = t[1]
                    pe.wait_ge(ld_a[i], 16)
                    for m in range(4 * i, min(4 * i + 4, M1)):
                        o = P * (m - 4 * i)
                        ins = passes(bk_[:, B * (m - 4 * i):B * (m - 4 * i) + B],
                                     [(st[:, k, o:o + P], sm("cond", B * k, B)) for k in range(KC)])
                elif t[0] == "w2":
                    pe.wait_ge(ld_a[4 + t[1]], 16)
                    pe.wait_ge(ld["outw"], 16)
                    for r in range(2):
                        o = P * (2 * t[2] + r)
                        ins = passes(bk_[:, D * r:D * r + D], [(st[:, k, o:o + P], outw[:, k, :]) for k in range(KC)])
                elif t[0] in ("pk", "v"):
                    pe.wait_ge(ld["ctxT"], 16)
                    w = pw[:, 1 if t[0] == "pk" else 2]
                    pe.wait_ge(ld["pwk" if t[0] == "pk" else "pwv"], 16)
                    ins = passes(bk_[:, 0:B * KP], [(w[:, k, P * t[1]:P * t[1] + P], ctxT[:, k].rearrange("p b n -> p (b n)"))
                                                    for k in range(KC)])
                elif t[0] == "kq":
                    pe.wait_ge(ld["pwqT"], 16)
                    ins = passes(bk_[:, 0:B * KP], [(pw[:, 0, k, P * t[1]:P * t[1] + P], pk[:, k].rearrange("p b n -> p (b n)"))
                                                    for k in range(KC)])
                elif t[0] == "mr":
                    for e in range(E):
                        ins = passes(bk_[:, LK * e:LK * e + LK], [(same(sm("rwe", E * k + e)), vf[:, k, t[1], 0:LK]) for k in range(KC)])
                elif t[0] == "b2":
                    pe.wait_ge(ld["outw"], 16)
                    for e in range(2 * t[1], min(2 * t[1] + 2, E)):
                        o = D * (e - 2 * t[1])
                        ins = passes(bk_[:, o:o + D], [(same(sm("eb2", E * k + e)), outw[:, k, :]) for k in range(KC)])
                else:
                    for b in range(B):
                        ins = passes(bk_[:, E * b:E * b + E], [(same(sm("cond", B * k + b)), sm("rwa", E * k, E)) for k in range(KC)])
                ins.then_inc(prep_mm, 1)

            walk(l0_steps(), {"front": front, "proj": proj, "rows": rows, "shift": shift, "keys": keys, "av": av,
                              "uz": uz, "zt": zt_step, "wp": wproj, "prep": prep})

            pe.wait_ge(x1_r, TJ * NC)
            pe.wait_ge(prep_r, len(PREP))

            def mpiece(n):
                b, tail, i = MP[n]
                w = min(512, W1N - 512 * i)
                if n == 0:
                    pe.wait_ge(ld["w1e"], 16)
                if n >= 4:
                    pe.wait_ge(m_l, n - 3)
                src = M_BANK[n % 4]
                rows_ = TAIL3 if tail else P
                passes(src[0:rows_, 0:w],
                       [((vt[:, k, b, :, :].rearrange("p a n -> p (a n)") if tail else vf[:, k, b, 0:P]),
                         w1e[:, k, 512 * i:512 * i + w]) for k in range(KC)]).then_inc(m_mm, 1)

            def nxt(c):
                if c:
                    pe.wait_ge(w_r, 2 * c)
                for j in range(TJ):
                    n = TJ * c + j
                    pe.wait_ge(l_r, n + 1)
                    for k in range(KC):
                        ins = nc.tensor.transpose(B_F[k][:, P * j:P * j + P], lnt1[:, n % 2, P * k:P * k + P], ident[:])
                    ins.then_inc(l_t, 1)

            def score(n):
                c, j = divmod(n, TJ)
                pe.wait_ge(nf_r, KC * (c + 1))
                if n:
                    pe.wait_ge(e1_d, n)
                passes(B_SC[:, 0:SC1], [(nxf[:, k, P * j:P * j + P], kq[:, k, c // CPB, :]) for k in range(KC)]).then_inc(sc_d, 1)

            def wtr(n):
                j = n % TJ
                pe.wait_ge(pn_r, n + 1)
                nc.tensor.transpose(B_F[0][:, P * j:P * j + P], pn[:, n % 2, :], ident[:])
                nc.tensor.transpose(B_F[1][0:TAIL3, P * j:P * j + P], pn3[:, n % 2].rearrange("p a n -> p (a n)"),
                                    ident[:]).then_inc(w_t, 1)

            def hidden(c, m):
                n = M1 * c + HORD.index(m)
                b = c // CPB
                if n == 0:
                    pe.wait_ge(w1_r, 2 * NW1)
                if m == HB:
                    pe.wait_ge(nl_r, KC * (c + 1))
                    pe.wait_ge(w_r, 2 * (c + 1))
                    pe.wait_ge(m_l, len(MP))
                if n >= 2:
                    pe.wait_ge(h_r, n - 1)
                o = slice(P * m, P * m + P)
                h, l = nxh[:, c % 2], nxl[:, c % 2]
                terms = []
                for k in range(KC):
                    terms += [(w1h[:, k, o], h[:, k, :]), (w1h[:, k, o], l[:, k, :]), (w1l[:, k, o], h[:, k, :])]
                terms += [(mh[:, b, o], wh[:, c % 2, :]), (mh[:, b, o], wl[:, c % 2, :]), (ml[:, b, o], wh[:, c % 2, :]),
                          (mt[:, b, o], wt[:, c % 2, :])]
                passes(B_H[n % 2][:, :], terms).then_inc(h_mm, 1)

            def gate(n):
                c, j = divmod(n, TJ)
                if n == 0:
                    pe.wait_ge(ld["gw2"], 16)
                pe.wait_ge(h_r, M1 * c + GB)
                if n:
                    pe.wait_ge(gz_r, n)
                passes(B_G[:, 0:D], [(hg[:, k, P * j:P * j + P], gw2[:, k, :]) for k in range(KC)]).then_inc(g_mm, 1)

            def expert(c, e, j):
                q = E * c + e
                n = TJ * q + j
                pe.wait_ge(h_r, M1 * c + GB + 4 * (e + 1))
                if n >= 2:
                    pe.wait_ge(y_r, n - 1)
                passes(B_Y[n % 2][:, 0:D], [(hid[:, q % 2, r, P * j:P * j + P], w2[:, 4 * e + r, :]) for r in range(4)]).then_inc(y_mm, 1)

            walk(l1_steps(), {"m": mpiece, "nxt": nxt, "score": score, "wtr": wtr, "hidden": hidden, "gate": gate,
                              "expert": expert})


def laid_out(v):
    f = lambda name: np.ascontiguousarray(v[name])
    chunks = lambda w: w.reshape(w.shape[0] // P, P, -1).transpose(1, 0, 2)
    rep = lambda row, n=P: np.broadcast_to(row, (n,) + row.shape)
    x, ctx_, cond = f("x"), f("ctx_1024"), f("cond_1024")
    zeros = lambda *s: np.zeros(s, x.dtype)
    twice = lambda w: np.repeat(w.reshape(-1, NG, GH, 1, DH), 2, axis=3).reshape(w.shape[0], NG * P)
    wkv, bkv = f("L0_xcond_Wkv"), f("L0_xcond_bkv")
    a = {"x": x.reshape(B * LQ // P, P, D).transpose(1, 0, 2)}
    p = np.arange(P)
    cols = lambda vec: vec.reshape(-1, P).T
    rw, w1 = f("L1_xcond_router_W"), np.concatenate([*f("L1_xcond_e_w1"), f("L1_xcond_gate_w1")], axis=1)
    w1r = np.concatenate([f("L1_xcond_e_b1").ravel(), f("L1_xcond_gate_b1")])
    bss = np.concatenate([f("L0_xcond_bss_q"), f("L0_xcond_bss_kv")])
    a["small"] = np.concatenate([
        chunks(cond.T).reshape(P, -1), cols(bss), cols(twice(f("L0_xcond_bq")[None])[0]), cols(twice(bkv[None, :D])[0]),
        cols(f("L1_xcond_ln_gamma")), cols(f("L1_xcond_ln_beta")), cols(w1r), rep(f("L1_xcond_router_b")),
        (p % 32 < DH).astype(np.float32)[:, None], (p % 32 == DH).astype(np.float32)[:, None],
        (p % 32 < KT).astype(np.float32)[:, None],
        chunks(rw[0:D]).reshape(P, -1), chunks(rw[2 * D:]).reshape(P, -1),
        chunks(rw[D:2 * D]).reshape(P, -1), chunks(f("L1_xcond_e_b2").T).reshape(P, -1)], axis=1)
    a["ident"] = np.eye(P, dtype=np.float32)
    ct = zeros(P, 3, D)
    for b in range(B):
        ct[:, b] = ctx_[b, 0:P]
        ct[32 * b:32 * b + KT, 2] = ctx_[b, P:]
    a["ctx"] = ct
    cT = zeros(P, KC, B, KP)
    for b in range(B):
        cT[:, :, b, 0:LK] = chunks(ctx_[b].T)
    a["ctxT"] = cT
    a["wss"] = chunks(np.concatenate([f("L0_xcond_Wss_q"), f("L0_xcond_Wss_kv")], axis=1)).reshape(P, KC, 8, P)
    a["wq"] = chunks(twice(f("L0_xcond_Wq"))).reshape(P, KC, NG, P)
    a["wk"] = chunks(twice(wkv[:, :D])).reshape(P, KC, NG, P)
    a["wv"], a["bv"] = chunks(wkv[:, D:]), rep(bkv[D:])
    a["wp"], a["bp"] = chunks(f("L0_xcond_Wp")), rep(f("L0_xcond_bp"))
    a["pwqT"], a["pwk"], a["pwv"] = chunks(f("L1_xcond_Wq").T), chunks(f("L1_xcond_Wk")), chunks(f("L1_xcond_Wv"))
    a["w1n"], a["w1e"], a["w1a"] = chunks(w1[0:D]), chunks(w1[D:2 * D]), chunks(w1[2 * D:])
    a["ew2T"] = chunks(f("L1_xcond_e_w2").reshape(E * RH, D).T)
    a["outw"], a["outb"] = chunks(f("L1_xcond_out_w")), rep(f("L1_xcond_out_b"))
    a["gw2"], a["gb2"] = chunks(f("L1_xcond_gate_w2")), rep(f("L1_xcond_gate_b2"))
    return {n: np.ascontiguousarray(a[n].reshape(s)) for n, s in SHAPES.items()}


def kernel(**inputs):
    import concourse.bacc as bacc
    from concourse.bass_utils import run_bass_kernel_spmd

    nc = bacc.Bacc("TRN2", target_bir_lowering=False, num_devices=1)
    arrays = laid_out({k: np.asarray(v) for k, v in inputs.items()})
    dram = {n: nc.dram_tensor(f"in_{n}", s, F32, kind="ExternalInput").ap() for n, s in SHAPES.items()}
    out = nc.dram_tensor("out_x", SHAPES["x"], F32, kind="ExternalOutput").ap()
    build(nc, dram, out)
    r = run_bass_kernel_spmd(nc, [{f"in_{n}": a for n, a in arrays.items()}], core_ids=[0])
    return r.results[0]["out_x"].transpose(1, 0, 2).reshape(B, LQ, D)
```

```python
from contextlib import ExitStack

import numpy as np
import concourse.bass as bass
from concourse import mybir

F32 = mybir.dt.float32
F32R = mybir.dt.float32r
I32 = mybir.dt.int32
ALU = mybir.AluOpType
ACT = mybir.ActivationFunctionType
AXX = mybir.AxisListType.X

P = 128
B, LQ, D = 2, 1024, 256
LK = 154
NH, DH = 16, 16
KC = D // P
CT = 512
NC = B * LQ // CT
CPB = NC // B
TJ = CT // P
GH = 4
NG = NH // GH
NU = NG + 1
GR = NC * NG
KP = 160
KT = LK - P
E, RH = 3, 512
HB = E * RH // P
GB = D // P
M1 = HB + GB
W1N = M1 * P
SC1 = LK + E
EPS = 1e-5
TAIL3 = 96

SM = {}
_at = 0
for _n, _w in (("cond", KC * B), ("bss", 8), ("bq", NG), ("bk", NG), ("gamma", KC), ("beta", KC),
               ("b1", M1), ("rb", E), ("m0", 1), ("m1", 1), ("m16", 1), ("m26", 1), ("rwn", KC * E),
               ("rwa", KC * E), ("rwe", KC * E), ("eb2", KC * E)):
    SM[_n] = (_at, _at + _w)
    _at += _w
SMW = _at

SHAPES = {
    "x": (P, B * LQ // P, D), "small": (P, SMW), "ident": (P, P), "ctx": (P, 3, D),
    "ctxT": (P, KC, B, KP), "wss": (P, KC, 8, P), "wq": (P, KC, NG, P), "wk": (P, KC, NG, P),
    "wv": (P, KC, D), "bv": (P, D), "wp": (P, KC, D), "bp": (P, D),
    "pwqT": (P, KC, D), "pwk": (P, KC, D), "pwv": (P, KC, D),
    "w1n": (P, KC, W1N), "w1e": (P, KC, W1N), "w1a": (P, KC, W1N),
    "ew2T": (P, KC, E * RH), "outw": (P, KC, D),
    "outb": (P, D), "gw2": (P, KC, D), "gb2": (P, D),
}


def build(nc, dram, out):
    ctx = ExitStack()
    with ctx:
        def sem(name):
            return ctx.enter_context(nc.semaphore(name))

        def sb(name, shape, dt=F32, where=ctx):
            return where.enter_context(nc.sbuf_tensor(name, list(shape), dt))

        pair = ctx.enter_context(nc.psum_tensor("pair", [P, 2, 512], F32))
        bank = [ctx.enter_context(nc.psum_tensor(f"bank{i}", [P, 512], F32)) for i in range(6)]
        B_S, B_P, B_ST, B_U, B_TOK = [pair[:, i, :] for i in range(2)], bank[0:2], bank[2:4], bank[4], bank[5]
        B_Y, B_G, B_SC, B_H, B_F = B_S, bank[0], bank[1], bank[2:4], bank[4:6]
        K_BANK = [B_ST[0], B_ST[1], B_P[0], B_P[1]]
        V_BANK = [B_U, B_TOK, B_S[0], B_S[1]]
        M_BANK = [B_H[0], B_H[1], B_U, B_G]

        x = sb("x_sb", (P, NC * TJ, D))
        small = sb("small_sb", (P, SMW))
        ident = sb("ident_sb", (P, P))
        negI = sb("negI", (P, P), F32R)
        w1h = sb("w1h", (P, KC, W1N), F32R)
        w1l = sb("w1l", (P, KC, W1N), F32R)
        pre0 = ExitStack()
        ctxt = sb("ctx_sb", (P, 3, D), F32, pre0)
        vtf = sb("vtf", (P, D), F32, pre0)
        bv = sb("bv_sb", (P, D), F32, pre0)
        xkv = sb("xkv", (P, KC, B, KP), F32, pre0)
        pre0.close()
        w2 = sb("w2", (P, HB, D))
        b2 = sb("b2", (P, E, D))
        ab1 = sb("ab1", (P, M1, B))
        kq = sb("kq", (P, KC, B, SC1))
        vf = sb("vf", (P, KC, B, KP))
        vt = sb("vt", (P, KC, B, 32))
        mr = sb("mr", (P, B, E, LK))
        cr = sb("cr", (P, B, E))
        stage = [sb("stage0", (P, KC, 512)), sb("stage1", (P, KC, 256))]
        st6 = sb("st6", (P, TJ + 3, 6))
        mv = sb("mv", (P, TJ + 3, 2))
        rs = sb("rs", (P, 3, TJ + 3))

        def sm(name, i=0, n=1):
            return small[:, SM[name][0] + i:SM[name][0] + i + n]

        ops = ExitStack()
        ctxT = sb("ctxT_sb", (P, KC, B, KP), F32, ops)
        pw = sb("pw", (P, 3, KC, D), F32, ops)
        pk = sb("pk", (P, KC, B, KP), F32, ops)
        outb = sb("outb_sb", (P, D), F32, ops)
        ops.close()
        w1_ = ExitStack()
        w1e = sb("w1e_sb", (P, KC, W1N), F32, w1_)
        w1_.close()
        late = ExitStack()
        bs = sb("bs", (P, TJ, D), F32, late)
        acc = sb("acc", (P, TJ, D), F32, late)
        gz = sb("gz", (P, 2, D), F32, late)
        th = sb("th", (P, TJ, D), F32, late)
        late.close()
        sb("place", (P, KC, W1N))

        l0 = ExitStack()
        ka = sb("ka", (P, B, NG, GH * LK + P), F32R, l0)
        kb = sb("kb", (P, B, NG, GH * P + P), F32R, l0)
        bp = sb("bp_sb", (P, D), F32, l0)
        wp = sb("wp_sb", (P, KC, D), F32, l0)
        wqh = sb("wqh", (P, KC, NG, P), F32R, l0)
        wql = sb("wql", (P, KC, NG, P), F32R, l0)
        ssc = sb("ssc", (P, 8, B), F32, l0)
        vmain = sb("vmain", (P, B, NH, 32), F32, l0)
        vtail = sb("vtail", (P, B, NG, P), F32, l0)
        lnt = sb("lnt", (P, 2, D), F32, l0)
        xh = sb("xh", (P, KC, CT), F32R, l0)
        xl = sb("xl", (P, KC, CT), F32R, l0)
        xf = sb("xf", (P, KC, CT), F32, l0)
        nm = sb("nm", (P, 2, TJ, P), F32R, l0)
        rz = sb("rz", (P, NH), F32, l0)
        pre = ExitStack()
        wss = sb("wss_sb", (P, KC, 8, P), F32, pre)
        wk = sb("wk_sb", (P, KC, NG, P), F32, pre)
        wv = sb("wv_sb", (P, KC, D), F32, pre)
        wq = sb("wq_sb", (P, KC, NG, P), F32, pre)
        xkv4 = sb("xkv4", (P, KC, B, GH, 32), F32, pre)
        kh = sb("kh", (P, NG, B, KP), F32R, pre)
        kg = sb("kg", (P, NG, B, LK), F32R, pre)
        pre.close()
        qh = sb("qh", (P, 2, CT), F32R, l0)
        ql = sb("ql", (P, 2, CT), F32R, l0)
        z = sb("z", (P, 2, D), F32, l0)
        zt = sb("zt", (P, 2, KC, P), F32, l0)
        pt = sb("pt", (P, GH + 1, CT), F32, l0)
        u = sb("u", (P, NU, CT), F32, l0)
        csilu = sb("csilu", (P, KC, B), F32, l0)
        outw = sb("outw_sb", (P, KC, D), F32, l0)
        l0.close()

        l1 = ExitStack()
        mh = sb("mh", (P, B, W1N), F32R, l1)
        ml = sb("ml", (P, B, W1N), F32R, l1)
        mt = sb("mt", (TAIL3, B, W1N), F32R, l1)
        gw2 = sb("gw2_sb", (P, KC, D), F32, l1)
        gb2 = sb("gb2_sb", (P, D), F32, l1)
        hg = sb("hg", (P, GB, CT), F32, l1)
        wh = sb("wh", (P, 2, CT), F32R, l1)
        wl = sb("wl", (P, 2, CT), F32R, l1)
        wt = sb("wt", (TAIL3, 2, CT), F32R, l1)
        nxf = sb("nxf", (P, KC, CT), F32, l1)
        nxh = sb("nxh", (P, 2, KC, CT), F32R, l1)
        nxl = sb("nxl", (P, 2, KC, CT), F32R, l1)
        lnt1 = sb("lnt1", (P, 2, D), F32, l1)
        pe_ = sb("pe_", (P, 2, LK), F32, l1)
        pn = sb("pn", (P, 2, P), F32, l1)
        pn3 = sb("pn3", (P, 2, 3, 32), F32, l1)
        ttr = sb("ttr", (P, LK), F32, l1)
        nmx = sb("nmx", (P, 2), F32, l1)
        sme = sb("sme", (P, 2), F32, l1)
        rec = sb("rec", (P, 2), F32, l1)
        lg = sb("lg", (P, TJ, E), F32, l1)
        lw = sb("lw", (P, TJ, E), F32, l1)
        lx = sb("lx", (P, TJ), F32, l1)
        le = sb("le", (P, TJ, E), F32, l1)
        pr = sb("pr", (P, 2, TJ, E), F32, l1)
        pb = sb("pb", (P, D), F32, l1)
        hid = sb("hid", (P, 2, 4, CT), F32, l1)
        l1.close()

        ld = {n: sem(f"ld_{n}") for n in SHAPES if n not in ("x", "w1n", "w1a", "ew2T")}
        ld_x = [sem(f"ld_x{c}") for c in range(NC)]
        NW1 = W1N // 256
        PE_PIECES = [("w1a", i) for i in range(4)] + [("ew2T", i) for i in range(3)]
        ld_a, ld_b = [sem(f"ld_piece{i}") for i in range(7)], [sem(f"ld_w1n{i}") for i in range(NW1)]
        stored = sem("stored")
        silu_d, ss_mm, ss_r = sem("silu_done"), sem("ss_mm"), sem("ss_ready")
        zeroed, neg_r, wq_r = sem("zeroed"), sem("neg_ready"), sem("wq_split")
        cl_r, cl_t, xkv_r, x4_r, ones_r = sem("ctx_ln"), sem("ctx_t"), sem("xkv_ready"), sem("xkv4_ready"), sem("ones_ready")
        k_mm, kh_r, kg_r, v_mm, v_r, ka_r, kb_r = sem("k_mm"), sem("kh_ready"), sem("kg_ready"), sem("v_mm"), sem("v_ready"), sem("ka_ready"), sem("kb_ready")
        prep_mm, prep_r, w1_r = sem("prep_mm"), sem("prep_ready"), sem("w1_split")
        ln_r, ln_t, xf_r, xh_r, xl_r = sem("ln_ready"), sem("ln_taken"), sem("xf_ready"), sem("xh_ready"), sem("xl_ready")
        pj_d, qh_r, ql_r = sem("proj_done"), sem("qh_ready"), sem("ql_ready")
        s1_d, mx_d, nm_d = sem("rowscores_done"), sem("max_done"), sem("shift_added")
        st_d, ex_d, av_d, u_r = sem("keyscores_done"), sem("exp_done"), sem("av_done"), sem("u_ready")
        uz_d, z_r, zt_d, zt_r = sem("uz_done"), sem("z_ready"), sem("zt_done"), sem("zt_ready")
        wp_d, xb_r, x1_r = sem("wp_done"), sem("xb_ready"), sem("x1_ready")
        m_mm, m_h, m_l = sem("m_mm"), sem("m_hi"), sem("m_lo")
        l_r, l_t, nf_r, nh_r, nl_r = sem("l_ready"), sem("l_taken"), sem("nxf_ready"), sem("nxh_ready"), sem("nxl_ready")
        sc_d, nm1_r, e1_d, pn_r, w_t = sem("sc_done"), sem("nmx_ready"), sem("e1_done"), sem("pn_ready"), sem("w_taken")
        wh_r, w_r, lg_r, le_r, pr_r, bs_r = sem("wh_ready"), sem("w_ready"), sem("lg_ready"), sem("le_ready"), sem("pr_ready"), sem("bs_ready")
        h_mm, h_r, g_mm, gz_r, th_r = sem("h_mm"), sem("h_ready"), sem("g_mm"), sem("gz_ready"), sem("th_ready")
        y_mm, y_r, o_r = sem("y_mm"), sem("y_used"), sem("out_ready")
        dch, pch = sem("vector_chain"), sem("pool_chain")

        OPS = [("pk", 0), ("pk", 1), ("kq", 0), ("kq", 1), ("v", 0), ("v", 1), ("mr", 0), ("mr", 1), ("b2", 0), ("b2", 1), ("cr",)]
        PREP = OPS + [("anchor", i) for i in range(4)] + [("w2", i, hf) for i in range(3) for hf in range(2)]
        PI = {t: n for n, t in enumerate(PREP)}

        def tile_steps(n):
            return ("uz", n), ("zt", n), ("wp", n)

        def l0_steps():
            yield ("proj", 0)
            for q in range(TJ):
                yield ("rows", 0, q)
            yield ("proj", 1)
            yield ("shift", 0)
            prep = 0
            for g in range(GR):
                c, gi = divmod(g, NG)
                n, m = g + 1, g + 2
                fill = [()] * 6
                if c > 0 and gi < 2:
                    fill = [(s,) for t in (0, 1) for s in tile_steps(TJ * (c - 1) + 2 * gi + t)]
                if c + 1 < NC:
                    if gi < 2:
                        fill[3] += (("stats", c + 1, gi),)
                    elif gi == 2:
                        fill[0] += (("xt", c + 1, 0),)
                        fill[2] += (("xt", c + 1, 1),)
                for i in ((1, 3, 5) if c == 0 else (3, 5) if gi >= 2 else ()):
                    if prep < len(PREP):
                        fill[i] += (("prep", prep),)
                        prep += 1
                yield ("keys", g, 0)
                if n < GR:
                    yield ("rows", n, 0)
                yield ("keys", g, 1)
                yield from fill[0]
                yield ("keys", g, 2)
                if n < GR:
                    yield ("rows", n, 1)
                yield from fill[1]
                yield ("keys", g, 3)
                yield ("keys", g, 4)
                yield from fill[2]
                if n < GR:
                    yield ("rows", n, 2)
                yield from fill[3]
                if n < GR:
                    yield ("rows", n, 3)
                yield from fill[4]
                if m < GR:
                    yield ("proj", m)
                if n < GR:
                    yield ("shift", n)
                yield ("av", g)
                yield from fill[5]
            assert prep == len(PREP)

        MP = [(b, i) for b in range(B) for i in range(4)] + [(None, i) for i in range(4)]

        def m_hi(n):
            return n + 1 if n < 4 * B else 4 * B + 3 * (n + 1 - 4 * B)

        def front1(c):
            n = TJ * c
            yield (("ln_stats", c),)
            yield (("ln", c, 0),)
            yield (("nxt", c, 0), ("ln", c, 1))
            yield (("nxt", c, 1),)
            yield (("nxf", c),)
            yield ()
            yield (("score", n),)
            for j in range(TJ + 1):
                group = ()
                if j > 0:
                    group += (("wtr", n + j - 1),)
                if j < TJ:
                    group += (("weights", n + j),)
                if j + 1 < TJ:
                    group += (("score", n + j + 1),)
                yield group
            yield (("router", c),)

        def between_steps():
            first = front1(0)
            tail = [s for j in range(TJ) for s in tile_steps(TJ * (NC - 1) + j)]
            yield from next(first)
            yield from next(first)
            for n in range(len(MP)):
                yield tail[n]
                yield ("m", n)
                yield from next(first, ())

        def l1_steps():
            for c in range(NC):
                take = front1(c + 1) if c + 1 < NC else iter(())
                experts = iter([("expert", c, e, j) for e in (0, 1) for j in range(TJ)])
                for i, m in enumerate(HORD):
                    yield ("hidden", c, m)
                    if 2 <= i < 6:
                        yield ("gate", TJ * c + i - 2)
                    if i < 4:
                        if c:
                            yield ("expert", c - 1, 2, i)
                    elif i >= 6:
                        yield next(experts)
                    yield from next(take, ())
            for j in range(TJ):
                yield ("expert", NC - 1, 2, j)

        def feat(c):
            return [B_F[0][:, :], B_F[1][:, :]] if c else B_S

        HORD = [HB, HB + 1] + list(range(HB))

        def hid_buf(c, m):
            return hg[:, m - HB, :] if m >= HB else hid[:, (E * c + m // 4) % 2, m % 4, :]

        def walk(steps, parts):
            for s in steps:
                if s[0] in parts:
                    parts[s[0]](*s[1:])

        block = ctx.enter_context(nc.Block())

        @block.sync
        def _(sp):
            def load(dst, name):
                sp.dma_start(dst, dram[name]).then_inc(ld[name], 16)
            load(wss[:], "wss")
            load(small[:], "small")
            load(wk[:], "wk")
            load(wv[:], "wv")
            load(bv[:], "bv")
            load(wp[:], "wp")
            for c in range(1, NC):
                sp.dma_start(x[:, TJ * c:TJ * c + TJ, :], dram["x"][:, TJ * c:TJ * c + TJ, :]).then_inc(ld_x[c], 16)
            for n, (name, i) in enumerate(PE_PIECES):
                if n:
                    pname, pi = PE_PIECES[n - 1]
                    sp.wait_ge(prep_mm, 1 + PI[("anchor", pi) if pname == "w1a" else ("w2", pi, 1)])
                w = min(512, SHAPES[name][2] - 512 * i)
                sp.dma_start(stage[0][:, :, 0:w], dram[name][:, :, 512 * i:512 * i + w]).then_inc(ld_a[n], 16)
            sp.wait_ge(prep_r, len(OPS))
            load(w1e[:], "w1e")
            sp.wait_ge(x1_r, TJ * NC)
            load(gw2[:], "gw2")
            load(gb2[:], "gb2")
            for c in range(NC):
                sp.wait_ge(o_r, TJ * c + TJ)
                sp.dma_start(out[:, TJ * c:TJ * c + TJ, :], x[:, TJ * c:TJ * c + TJ, :]).then_inc(stored, 16)
            sp.wait_ge(stored, 16 * NC)

        @block.gpsimd
        def _(pool):
            count = [0]

            def link(ins):
                count[0] += 1
                ins.then_inc(pch, 1)
                pool.wait_ge(pch, count[0])

            g_ = nc.gpsimd
            g_.memset(ka[:].bitcast(F32), 0.0).then_inc(zeroed, 1)
            g_.memset(kb[:].bitcast(F32), 0.0).then_inc(zeroed, 1)
            g_.memset(nm[:].bitcast(F32), 0.0).then_inc(zeroed, 1)
            link(g_.memset(vmain[:], 0.0))
            g_.memset(vmain[:, :, :, DH:DH + 1], 1.0).then_inc(zeroed, 1)
            g_.memset(vtail[:], 0.0).then_inc(zeroed, 1)
            pool.wait_ge(zeroed, 5)
            pool.wait_ge(ld["small"], 16)
            pool.wait_ge(kh_r, NG)
            for j in range(GH):
                r = slice(32 * j, 32 * j + 32)
                for dst, o, w in ((P * j, 0, P), (P * GH + 32 * j, P, KT)):
                    g_.tensor_scalar(kb[r, :, :, dst:dst + w].rearrange("p b g n -> p g b n"), kh[r, :, :, o:o + w],
                                     small[r, SM["m0"][0]:SM["m0"][1]], small[r, SM["m16"][0]:SM["m16"][1]],
                                     ALU.mult, ALU.add).then_inc(kb_r, 1)
                    pool.wait_ge(kb_r, 2 * j + (1 if w == P else 2))
            for j in range(GH):
                r = slice(32 * j, 32 * j + 32)
                link(g_.tensor_copy(vtail[r, :, :, 32 * j + DH:32 * j + DH + 1].rearrange("p b g o -> p (b g) o"),
                                    small[r, SM["m26"][0]:SM["m26"][1]].unsqueeze(1).broadcast_to([32, B * NG, 1])))
            g_.tensor_copy(kq[:, :, :, LK:SC1], sm("rwn", 0, KC * E).rearrange("p (k e) -> p k e", k=KC)
                           .unsqueeze(2).broadcast_to([P, KC, B, E])).then_inc(ones_r, 1)
            pool.wait_ge(ones_r, 1)

            def xb(c, half):
                if (c, half) == (0, 0):
                    pool.wait_ge(ld["bp"], 16)
                for j in (2 * half, 2 * half + 1):
                    n = TJ * c + j
                    pool.wait_ge(ln_r, n + 1)
                    g_.tensor_tensor(x[:, n, :], x[:, n, :], bp[:], ALU.add).then_inc(xb_r, 1)

            def piece(i):
                o = slice(256 * i, 256 * i + 256)
                pool.wait_ge(ld_b[i], 16)
                g_.tensor_copy(w1h[:, :, o], stage[1][:]).then_inc(w1_r, 1)
                pool.wait_ge(w1_r, 2 * i + 1)
                g_.tensor_tensor(w1l[:, :, o], stage[1][:], w1h[:, :, o], ALU.subtract).then_inc(w1_r, 1)
                if i + 1 < NW1:
                    pool.wait_ge(w1_r, 2 * i + 2)
                    pool.dma_start(stage[1][:], dram["w1n"][:, :, 256 * (i + 1):256 * (i + 2)]).then_inc(ld_b[i + 1], 16)

            def av(g):
                if g < NW1:
                    piece(g)

            pool.dma_start(stage[1][:], dram["w1n"][:, :, 0:256]).then_inc(ld_b[0], 16)
            xb(0, 0)
            xb(0, 1)
            walk(l0_steps(), {"xt": xb, "av": av})

            def router(c):
                pool.wait_ge(pr_r, c + 1)
                if c == 0:
                    pool.wait_ge(prep_r, len(PREP))
                    pool.wait_ge(m_mm, len(MP))
                if c:
                    pool.wait_ge(y_r, 4 * E * (c - 1) + TJ)
                for j in range(TJ):
                    link(g_.tensor_scalar(bs[:, j, :], b2[:, 0, :], pr[:, c % 2, j, 0:1], None, ALU.mult))
                    for e in (1, 2):
                        link(g_.tensor_scalar(pb[:], b2[:, e, :], pr[:, c % 2, j, e:e + 1], None, ALU.mult))
                        ins = g_.tensor_tensor(bs[:, j, :], bs[:, j, :], pb[:], ALU.add)
                        if e == 1:
                            link(ins)
                    ins.then_inc(bs_r, 1)
                    pool.wait_ge(bs_r, TJ * c + j + 1)

            def expert(c, e, j):
                if e < E - 1:
                    return
                n = TJ * c + j
                pool.wait_ge(y_r, TJ * (E * c + e) + j + 1)
                pool.wait_ge(th_r, n + 1)
                link(g_.tensor_scalar(th[:, j, :], th[:, j, :], 1.0, None, ALU.add))
                link(g_.tensor_tensor(acc[:, j, :], th[:, j, :], acc[:, j, :], ALU.mult))
                g_.tensor_tensor(x[:, n, :], x[:, n, :], acc[:, j, :], ALU.add).then_inc(o_r, 1)

            router(0)
            walk(l1_steps(), {"router": router, "expert": expert})

        @block.scalar
        def _(act):
            def load(dst, name):
                act.dma_start(dst, dram[name]).then_inc(ld[name], 16)
            load(ctxt[:], "ctx")
            act.dma_start(x[:, 0:TJ, :], dram["x"][:, 0:TJ, :]).then_inc(ld_x[0], 16)
            load(ident[:], "ident")
            load(wq[:], "wq")
            load(bp[:], "bp")
            load(ctxT[:], "ctxT")
            load(pw[:, 0], "pwqT")
            load(pw[:, 1], "pwk")
            load(pw[:, 2], "pwv")
            load(outw[:], "outw")
            load(outb[:], "outb")
            A = nc.scalar.activation
            act.wait_ge(ld["small"], 16)
            A(csilu[:], small[:, 0:KC * B].rearrange("p (k b) -> p k b", k=KC), ACT.Silu).then_inc(silu_d, 1)

            act.wait_ge(ss_r, 1)
            act.wait_ge(cl_t, 1)
            for k in range(KC):
                for b in range(B):
                    for dst, o, w in ((0, P * b, P), (P, B * P + 32 * b, 32)):
                        A(xkv[:, k, b, dst:dst + w], B_S[k][:, o:o + w], ACT.Identity, bias=ssc[:, 6 + k, b:b + 1],
                          scale=ssc[:, 4 + k, b:b + 1]).then_inc(xkv_r, 1)

            def xt(c, half):
                b = c // CPB
                act.wait_ge(ln_t, 2 * c + half + 1)
                if c:
                    act.wait_ge(xl_r, 2 * (c - 1) + half + 1)
                o = 2 * P * half
                for k in range(KC):
                    A(xf[:, k, o:o + 2 * P], B_TOK[:, 2 * P * k:2 * P * k + 2 * P], ACT.Identity, bias=ssc[:, 2 + k, b:b + 1],
                      scale=ssc[:, k, b:b + 1]).then_inc(xf_r, 1)

            xt(0, 0)
            xt(0, 1)
            for gi in range(NG):
                act.wait_ge(k_mm, gi + 1)
                A(kh[:, gi], K_BANK[gi][:, 0:B * KP].rearrange("p (b n) -> p b n", b=B), ACT.Identity,
                  bias=sm("bk", gi)).then_inc(kh_r, 1)
            act.wait_ge(ld["wq"], 16)
            A(wqh[:], wq[:], ACT.Copy).then_inc(wq_r, 1)

            def proj(g):
                act.wait_ge(pj_d, g + 1)
                if g >= 2:
                    act.wait_ge(st_d, (GH + 1) * (g - 1))
                A(qh[:, g % 2, :], B_P[g % 2][:, :], ACT.Identity, bias=sm("bq", g % NG)).then_inc(qh_r, 1)

            def keys(g, k):
                n = (GH + 1) * g + k
                act.wait_ge(st_d, n + 1)
                if k == 0 and g:
                    act.wait_ge(av_d, g)
                if n == 0:
                    act.wait_ge(v_r, 2 * B)
                A(pt[:, k, :], B_ST[n % 2][:, :], ACT.Exp, scale=DH ** -0.5).then_inc(ex_d, 1)

            def av(g):
                c = g // NG
                act.wait_ge(av_d, g + 1)
                if g >= NU:
                    act.wait_ge(uz_d, TJ * ((g - NU) // NG + 1))
                A(u[:, g % NU, :], B_U[:, :], ACT.Copy).then_inc(u_r, 1)

            def ztr(n):
                act.wait_ge(zt_d, n + 1)
                if n >= 2:
                    act.wait_ge(wp_d, n - 1)
                A(zt[:, n % 2, :, :], B_TOK[:, 0:D].rearrange("p (k n) -> p k n", k=KC), ACT.Copy).then_inc(zt_r, 1)

            walk(l0_steps(), {"xt": xt, "proj": proj, "keys": keys, "av": av, "zt": ztr})

            def mpiece(n):
                b, i = MP[n]
                w = min(512, W1N - 512 * i)
                act.wait_ge(m_mm, n + 1)
                src = M_BANK[n % 4]
                o = slice(512 * i, 512 * i + w)
                if b is None:
                    A(mt[0:32, 0, o], src[0:32, 0:w], ACT.Copy).then_inc(m_h, 1)
                    A(mt[32:64, 1, o], src[32:64, 0:w], ACT.Copy).then_inc(m_h, 1)
                    A(mt[0:32, 1, o], src[32:64, 0:w], ACT.Copy).then_inc(m_h, 1)
                else:
                    A(mh[:, b, o], src[:, 0:w], ACT.Copy).then_inc(m_h, 1)

            def nxf_(c):
                act.wait_ge(l_t, TJ * (c + 1))
                if c:
                    act.wait_ge(sc_d, TJ * c)
                for k in range(KC):
                    if c:
                        act.wait_ge(nl_r, KC * (c - 1) + k + 1)
                    A(nxf[:, k, :], feat(c)[k], ACT.Identity, bias=sm("beta", k), scale=sm("gamma", k)).then_inc(nf_r, 1)

            def score(n):
                act.wait_ge(nm1_r, n + 1)
                if n >= 2:
                    act.wait_ge(lg_r, n - 1)
                A(pe_[:, n % 2, :], B_SC[:, 0:LK], ACT.Exp, bias=nmx[:, n % 2:n % 2 + 1],
                  accum_out=sme[:, n % 2:n % 2 + 1]).then_inc(e1_d, 1)

            def router(c):
                act.wait_ge(w_t, TJ * (c + 1))
                if c >= 2:
                    act.wait_ge(h_mm, M1 * (c - 1))
                A(wh[:, c % 2, :], feat(c)[0][:, :], ACT.Copy).then_inc(wh_r, 1)
                A(wt[:, c % 2, :], feat(c)[1][0:TAIL3, :], ACT.Copy).then_inc(wh_r, 1)
                act.wait_ge(le_r, 2 * c + 1)
                A(le[:], lg[:], ACT.Exp).then_inc(le_r, 1)

            def hidden(c, m):
                n = M1 * c + HORD.index(m)
                act.wait_ge(h_mm, n + 1)
                q = E * c + m // 4
                if m >= HB:
                    if c:
                        act.wait_ge(g_mm, TJ * c)
                elif q >= 2:
                    act.wait_ge(y_mm, TJ * (q - 1))
                A(hid_buf(c, m), B_H[n % 2][:, :], ACT.Silu, bias=ab1[:, m, c // CPB:c // CPB + 1]).then_inc(h_r, 1)

            def gate(n):
                act.wait_ge(gz_r, n + 1)
                if n >= TJ:
                    act.wait_ge(o_r, n - TJ + 1)
                A(th[:, n % TJ, :], gz[:, n % 2, :], ACT.Tanh, scale=0.5).then_inc(th_r, 1)

            walk(between_steps(), {"zt": ztr, "m": mpiece, "nxf": nxf_, "score": score, "router": router})
            walk(l1_steps(), {"nxf": nxf_, "score": score, "router": router, "hidden": hidden, "gate": gate})

        @block.vector
        def _(dve):
            V = nc.vector
            count = [0]

            def link(ins):
                count[0] += 1
                ins.then_inc(dch, 1)
                dve.wait_ge(dch, count[0])

            def stats(tiles):
                for t, src in tiles:
                    w = src.shape[0]
                    ins = V.bn_stats(st6[0:w, t, :], src)
                link(ins)
                for t, src in tiles:
                    w = src.shape[0]
                    ins = V.bn_aggr(mv[0:w, t, :], st6[0:w, t, :])
                link(ins)

            def rsqrt(n=TJ):
                y, v, t = rs[:, 0, 0:n], rs[:, 1, 0:n], rs[:, 2, 0:n]
                link(V.tensor_scalar(v, mv[:, 0:n, 1], EPS, None, ALU.add))
                link(V.tensor_scalar(t.bitcast(I32), v.bitcast(I32), 1, None, ALU.logical_shift_right))
                link(V.tensor_scalar(y.bitcast(I32), t.bitcast(I32), -1.0, float(0x5F3759DF - 2 ** 31), ALU.mult, ALU.add))
                link(V.tensor_scalar(v, v, 0.5, None, ALU.mult))
                for _ in range(3):
                    link(V.tensor_tensor(t, y, y, ALU.mult))
                    link(V.tensor_tensor(t, t, v, ALU.mult))
                    link(V.scalar_tensor_tensor(y, t, 1.5, y, ALU.subtract, ALU.mult))

            def normalised(dst, t, src, rows=P):
                return V.tensor_scalar(dst, src, mv[0:rows, t, 0:1], rs[0:rows, 0, t:t + 1], ALU.subtract, ALU.mult)

            def norm(c, half):
                for j in (2 * half, 2 * half + 1):
                    n = TJ * c + j
                    if n >= 2:
                        dve.wait_ge(ln_t, 2 * c + half)
                    normalised(lnt[:, j % 2, :], j, x[:, n, :]).then_inc(ln_r, 1)

            def xsplit(c, half):
                o = slice(2 * P * half, 2 * P * half + 2 * P)
                dve.wait_ge(xf_r, KC * (2 * c + half + 1))
                if c:
                    dve.wait_ge(pj_d, NG * c)
                V.tensor_copy(xh[:, :, o], xf[:, :, o]).then_inc(xh_r, 1)
                dve.wait_ge(xh_r, 2 * c + half + 1)
                V.tensor_tensor(xl[:, :, o], xf[:, :, o], xh[:, :, o], ALU.subtract).then_inc(xl_r, 1)

            link(V.memset(mv[:], 1.0))
            dve.wait_ge(ld["ctx"], 16)
            stats([(TJ + t, ctxt[0:P if t < 2 else 64, t, :]) for t in range(3)])
            dve.wait_ge(ld_x[0], 16)
            stats([(j, x[:, j, :]) for j in range(TJ)])
            rsqrt(TJ + 3)
            for t in range(3):
                w = P if t < 2 else 64
                normalised(ctxt[0:w, t, :], TJ + t, ctxt[0:w, t, :], w).then_inc(cl_r, 1)
            dve.wait_ge(ld["small"], 16)
            dve.wait_ge(ss_mm, 1)
            for i in range(0, 8, 2):
                ins = V.scalar_tensor_tensor(ssc[:, i:i + 2, :], B_U[:, B * i:B * (i + 2)].rearrange("p (m b) -> p m b", b=B),
                                             1.0 if i % 4 == 0 else 0.0, sm("bss", i, 2).unsqueeze(2).broadcast_to([P, 2, B]),
                                             ALU.add, ALU.add)
            ins.then_inc(ss_r, 1)
            norm(0, 0)
            norm(0, 1)
            dve.wait_ge(ld["ident"], 16)
            V.tensor_scalar(negI[:], ident[:], -1.0, None, ALU.mult).then_inc(neg_r, 1)
            dve.wait_ge(xkv_r, 2 * KC * B)
            for k in range(KC):
                ins = V.tensor_copy(xkv4[:, k, :, :, :], xkv[:, k, :, P:KP].unsqueeze(2).broadcast_to([P, B, GH, 32]))
            ins.then_inc(x4_r, 1)
            xsplit(0, 0)
            for gi in range(NG):
                dve.wait_ge(kh_r, gi + 1)
                link(V.tensor_scalar(kg[:, gi], kh[:, gi, :, 0:LK], sm("m1"), None, ALU.mult))
                V.scalar_tensor_tensor(kg[:, gi], K_BANK[gi][:, 0:B * KP].rearrange("p (b n) -> p b n", b=B)[:, :, 0:LK],
                                       sm("bk", gi), kg[:, gi], ALU.add, ALU.subtract).then_inc(kg_r, 1)
            dve.wait_ge(kg_r, NG)
            xsplit(0, 1)
            dve.wait_ge(wq_r, 1)
            V.tensor_tensor(wql[:], wq[:], wqh[:], ALU.subtract).then_inc(wq_r, 1)
            dve.wait_ge(zeroed, 1)
            for j in range(GH):
                r = slice(32 * j, 32 * j + 32)
                for dst, o, w in ((LK * j, 0, LK), (LK * GH + 32 * j, P, KT)):
                    ins = V.tensor_copy(ka[r, :, :, dst:dst + w].rearrange("p b g n -> p g b n"), kg[r, :, :, o:o + w])
            ins.then_inc(ka_r, 1)
            dve.wait_ge(ld["bv"], 16)
            dve.wait_ge(zeroed, 5)
            for n in range(2 * B):
                b, tail = n % B, n // B
                src = V_BANK[n]
                dve.wait_ge(v_mm, n + 1)
                if not tail:
                    V.tensor_tensor(vmain[:, b, :, 0:DH], src[:, 0:D].rearrange("p (h d) -> p h d", h=NH),
                                    bv[:].rearrange("p (h d) -> p h d", h=NH), ALU.add).then_inc(v_r, 1)
                else:
                    link(V.tensor_tensor(vtf[:], src[:, 0:D], bv[:], ALU.add))
                    for j in range(GH):
                        r = slice(32 * j, 32 * j + 32)
                        ins = V.tensor_scalar(vtail[r, b, :, 32 * j:32 * j + DH],
                                              vtf[r, :].rearrange("p (g j d) -> p g j d", g=NG, j=GH)[:, :, j, :],
                                              small[r, SM["m26"][0]:SM["m26"][1]], None, ALU.mult)
                    ins.then_inc(v_r, 1)
                    dve.wait_ge(v_r, n + 1)

            def chunk_stats(c, half):
                if half == 0:
                    dve.wait_ge(ld_x[c], 16)
                stats([(j, x[:, TJ * c + j, :]) for j in (2 * half, 2 * half + 1)])
                if half:
                    rsqrt()

            def xt(c, half):
                if half == 0:
                    norm(c, 0)
                    norm(c, 1)
                xsplit(c, half)

            def rows(g, q):
                n = TJ * g + q
                dve.wait_ge(s1_d, n + 1)
                if g >= 2:
                    dve.wait_ge(nm_d, g - 1)
                V.tensor_reduce(nm[:, g % 2, q, :].rearrange("p (h w) -> p h w", w=32)[:, :, DH:DH + 1],
                                pair[:, :, 0:2 * LK].rearrange("p s (a n) -> p s a n", a=2), AXX, ALU.max).then_inc(mx_d, 1)

            def shift(g):
                dve.wait_ge(nm_d, g + 1)
                dve.wait_ge(qh_r, g + 1)
                if g >= 2:
                    dve.wait_ge(st_d, (GH + 1) * (g - 1))
                V.scalar_tensor_tensor(ql[:, g % 2, :], B_P[g % 2][:, :], sm("bq", g % NG), qh[:, g % 2, :],
                                       ALU.add, ALU.subtract).then_inc(ql_r, 1)

            def uz(n):
                dve.wait_ge(uz_d, n + 1)
                heads = B_TOK[:, :].rearrange("p (h w) -> p h w", w=32)
                link(V.reciprocal(rz[:], heads[:, :, DH]))
                if n >= 2:
                    dve.wait_ge(zt_d, n - 1)
                V.tensor_tensor(z[:, n % 2, :].rearrange("p (h d) -> p h d", h=NH), heads[:, :, 0:DH],
                                rz[:].unsqueeze(2).broadcast_to([P, NH, DH]), ALU.mult).then_inc(z_r, 1)

            def wproj(n):
                dve.wait_ge(wp_d, n + 1)
                dve.wait_ge(xb_r, n + 1)
                V.tensor_tensor(x[:, n, :], B_TOK[:, 0:D], x[:, n, :], ALU.add).then_inc(x1_r, 1)

            def prep(n):
                t = PREP[n]
                dve.wait_ge(prep_mm, n + 1)
                src = B_TOK
                if t[0] == "anchor":
                    m0 = 4 * t[1]
                    w = min(4, M1 - m0)
                    ins = V.tensor_tensor(ab1[:, m0:m0 + w, :], src[:, 0:B * w].rearrange("p (m b) -> p m b", m=w),
                                          sm("b1", m0, w).unsqueeze(2).broadcast_to([P, w, B]), ALU.add)
                elif t[0] == "w2":
                    r = 4 * t[1] + 2 * t[2]
                    ins = V.tensor_copy(w2[:, r:r + 2, :], src[:, :].rearrange("p (r n) -> p r n", r=2))
                elif t[0] == "pk":
                    ins = V.tensor_copy(pk[:, t[1]], src[:, 0:B * KP].rearrange("p (b n) -> p b n", b=B))
                elif t[0] == "kq":
                    ins = V.tensor_scalar(kq[:, t[1], :, 0:LK], src[:, 0:B * KP].rearrange("p (b n) -> p b n", b=B)[:, :, 0:LK],
                                          D ** -0.5, None, ALU.mult)
                elif t[0] == "v":
                    v4 = src[:, 0:B * KP].rearrange("p (b n) -> p b n", b=B)
                    link(V.tensor_copy(vf[:, t[1]], v4))
                    ins = V.tensor_copy(vt[:, t[1]], v4[:, :, P:KP])
                elif t[0] == "mr":
                    ins = V.tensor_copy(mr[:, t[1]], src[:, 0:E * LK].rearrange("p (e n) -> p e n", e=E))
                elif t[0] == "b2":
                    w = 2 - t[1]
                    dve.wait_ge(ld["outb"], 16)
                    ins = V.tensor_tensor(b2[:, 2 * t[1]:2 * t[1] + w, :], src[:, 0:w * D].rearrange("p (e n) -> p e n", e=w),
                                          outb[:].unsqueeze(1).broadcast_to([P, w, D]), ALU.add)
                else:
                    ins = V.tensor_tensor(cr[:], src[:, 0:B * E].rearrange("p (b e) -> p b e", b=B),
                                          sm("rb", 0, E).unsqueeze(1).broadcast_to([P, B, E]), ALU.add)
                ins.then_inc(prep_r, 1)

            walk(l0_steps(), {"stats": chunk_stats, "xt": xt, "rows": rows, "shift": shift, "uz": uz, "wp": wproj, "prep": prep})

            def mpiece(n):
                b, i = MP[n]
                w = min(512, W1N - 512 * i)
                o = slice(512 * i, 512 * i + w)
                dve.wait_ge(m_h, m_hi(n))
                src = M_BANK[n % 4]
                if b is None:
                    V.tensor_copy(mt[64:96, 0, o], src[0:32, 0:w])
                    V.tensor_copy(mt[64:96, 1, o], src[32:64, 0:w])
                    V.tensor_tensor(mt[32:64, 0, o], src[0:32, 0:w], mt[0:32, 0, o], ALU.subtract)
                    ins = V.tensor_tensor(mt[32:64, 1, o], src[32:64, 0:w], mt[32:64, 1, o], ALU.subtract)
                else:
                    ins = V.tensor_tensor(ml[:, b, o], src[:, 0:w], mh[:, b, o], ALU.subtract)
                ins.then_inc(m_l, 1)

            def ln_stats(c):
                dve.wait_ge(x1_r, TJ * (c + 1))
                stats([(j, x[:, TJ * c + j, :]) for j in range(TJ)])
                rsqrt()

            def ln(c, half):
                if c == 0 and half == 0:
                    dve.wait_ge(av_d, GR)
                    link(V.memset(pn3[:], 0.0))
                for j in (2 * half, 2 * half + 1):
                    n = TJ * c + j
                    if n >= 2:
                        dve.wait_ge(l_t, n - 1)
                    normalised(lnt1[:, n % 2, :], j, x[:, n, :]).then_inc(l_r, 1)

            def nxsplit(c):
                for k in range(KC):
                    dve.wait_ge(nf_r, KC * c + k + 1)
                    if c >= 2:
                        dve.wait_ge(h_mm, M1 * (c - 1))
                    V.tensor_copy(nxh[:, c % 2, k, :], nxf[:, k, :]).then_inc(nh_r, 1)
                    dve.wait_ge(nh_r, KC * c + k + 1)
                    V.tensor_tensor(nxl[:, c % 2, k, :], nxf[:, k, :], nxh[:, c % 2, k, :], ALU.subtract).then_inc(nl_r, 1)

            def score(n):
                j = n % TJ
                dve.wait_ge(sc_d, n + 1)
                if j == 0 and n:
                    dve.wait_ge(le_r, 2 * (n // TJ))
                link(V.tensor_copy(lg[:, j, :], B_SC[:, LK:SC1]))
                V.tensor_reduce(nmx[:, n % 2:n % 2 + 1], B_SC[:, 0:LK], AXX, ALU.max, negate=True).then_inc(nm1_r, 1)

            def weights(n):
                j, b, i = n % TJ, n // TJ // CPB, n % 2
                dve.wait_ge(e1_d, n + 1)
                link(V.reciprocal(rec[:, i:i + 1], sme[:, i:i + 1]))
                if n >= 2:
                    dve.wait_ge(w_t, n - 1)
                link(V.tensor_scalar(pn[:, i, :], pe_[:, i, 0:P], rec[:, i:i + 1], None, ALU.mult))
                V.tensor_scalar(pn3[:, i, :, 0:KT], pe_[:, i, P:LK].unsqueeze(1).broadcast_to([P, 3, KT]),
                                rec[:, i:i + 1], None, ALU.mult).then_inc(pn_r, 1)
                for e in range(E):
                    ins = V.tensor_tensor_reduce(out=ttr[:], in0=pe_[:, i, :], in1=mr[:, b, e, :], scale=rec[:, i:i + 1],
                                                 scalar=0.0, op0=ALU.mult, op1=ALU.add, accum_out=lw[:, j, e:e + 1])
                    if e < E - 1:
                        link(ins)
                ins.then_inc(lg_r, 1)

            def router(c):
                b = c // CPB
                dve.wait_ge(wh_r, 2 * c + 1)
                V.tensor_tensor(wl[:, c % 2, :], feat(c)[0][:, :], wh[:, c % 2, :], ALU.subtract).then_inc(w_r, 1)
                dve.wait_ge(wh_r, 2 * c + 2)
                V.tensor_tensor(wt[64:96, c % 2, :], feat(c)[1][64:96, :], wt[64:96, c % 2, :], ALU.subtract).then_inc(w_r, 1)
                dve.wait_ge(lg_r, TJ * (c + 1))
                link(V.tensor_tensor(lg[:], lg[:], lw[:], ALU.add))
                link(V.tensor_tensor(lg[:], lg[:], cr[:, b, :].unsqueeze(1).broadcast_to([P, TJ, E]), ALU.add))
                link(V.tensor_reduce(lx[:], lg[:], AXX, ALU.max))
                V.tensor_tensor(lg[:], lg[:], lx[:].unsqueeze(2).broadcast_to([P, TJ, E]), ALU.subtract).then_inc(le_r, 1)
                dve.wait_ge(le_r, 2 * c + 2)
                link(V.tensor_reduce(lx[:], le[:], AXX, ALU.add))
                link(V.reciprocal(lx[:], lx[:]))
                if c >= 2:
                    dve.wait_ge(bs_r, TJ * (c - 1))
                V.scalar_tensor_tensor(pr[:, c % 2], le[:], 0.5, lx[:].unsqueeze(2).broadcast_to([P, TJ, E]),
                                       ALU.mult, ALU.mult).then_inc(pr_r, 1)

            def gate(n):
                if n == 0:
                    dve.wait_ge(ld["gb2"], 16)
                dve.wait_ge(g_mm, n + 1)
                if n >= 2:
                    dve.wait_ge(th_r, n - 1)
                V.tensor_tensor(gz[:, n % 2, :], B_G[:, 0:D], gb2[:], ALU.add).then_inc(gz_r, 1)

            def expert(c, e, j):
                n = TJ * (E * c + e) + j
                dve.wait_ge(y_mm, n + 1)
                if e == 0:
                    dve.wait_ge(bs_r, TJ * c + j + 1)
                    if c:
                        dve.wait_ge(o_r, TJ * (c - 1) + j + 1)
                else:
                    dve.wait_ge(y_r, n - TJ + 1)
                V.scalar_tensor_tensor(acc[:, j, :], B_Y[n % 2][:, 0:D], pr[:, c % 2, j, e:e + 1],
                                       bs[:, j, :] if e == 0 else acc[:, j, :], ALU.mult, ALU.add).then_inc(y_r, 1)

            front_parts = {"ln_stats": ln_stats, "ln": ln, "nxf": nxsplit, "score": score, "weights": weights,
                           "router": router}
            walk(between_steps(), {"uz": uz, "wp": wproj, "m": mpiece, **front_parts})
            walk(l1_steps(), {"gate": gate, "expert": expert, **front_parts})

        @block.tensor
        def _(pe):
            mm = nc.tensor.matmul

            def same(column):
                return column.broadcast_to([P, P])

            def passes(dst, terms, first=True, last=True, free=False):
                for i, (a, b_) in enumerate(terms):
                    ins = mm(dst, a, b_, start=first and i == 0, stop=last and i == len(terms) - 1,
                             skip_group_check=free)
                return ins

            pe.wait_ge(ld["wss"], 16)
            pe.wait_ge(silu_d, 1)
            for m in range(8):
                ins = passes(B_U[:, B * m:B * m + B], [(wss[:, k, m, :], csilu[:, k, :]) for k in range(KC)])
            ins.then_inc(ss_mm, 1)
            pe.wait_ge(ld["ident"], 16)
            for t in range(3):
                pe.wait_ge(cl_r, t + 1)
                w = P if t < 2 else 64
                for k in range(KC):
                    ins = nc.tensor.transpose(B_S[k][:, P * t:P * t + w], ctxt[0:w, t, P * k:P * k + P], ident[0:w, 0:w])
            ins.then_inc(cl_t, 1)

            tok = [None, None]

            def take_tok(freed, value):
                if tok[0] is not None:
                    pe.wait_ge(tok[0], tok[1])
                tok[0], tok[1] = freed, value

            def xt(c, half):
                take_tok(xf_r, KC * (2 * c + half + 1))
                for j in (2 * half, 2 * half + 1):
                    pe.wait_ge(ln_r, TJ * c + j + 1)
                    for k in range(KC):
                        ins = nc.tensor.transpose(B_TOK[:, 2 * P * k + P * (j % 2):2 * P * k + P * (j % 2) + P],
                                                  lnt[:, j % 2, P * k:P * k + P], ident[:])
                ins.then_inc(ln_t, 1)

            xt(0, 0)
            pe.wait_ge(ld["wk"], 16)
            pe.wait_ge(xkv_r, 2 * KC * B)
            for g in range(NG):
                passes(K_BANK[g][:, 0:B * KP],
                       [(wk[:, k, g, :], xkv[:, k, :, :].rearrange("p b n -> p (b n)")) for k in range(KC)]).then_inc(k_mm, 1)
                if g == 0:
                    xt(0, 1)
            pe.wait_ge(ld["wv"], 16)
            pe.wait_ge(x4_r, 1)
            pe.wait_ge(ss_r, 1)
            pe.wait_ge(xf_r, 2 * KC)
            for n in range(2 * B):
                b, tail = n % B, n // B
                passes(V_BANK[n][:, 0:D],
                       [((xkv4[:, k, b, :, :].rearrange("p a n -> p (a n)") if tail else xkv[:, k, b, 0:P]), wv[:, k, :])
                        for k in range(KC)]).then_inc(v_mm, 1)
            tok[0], tok[1] = v_r, 2

            def proj(g):
                c, gi = divmod(g, NG)
                if g == 0:
                    pe.wait_ge(wq_r, 2)
                if g < 2:
                    pe.wait_ge(kg_r, g + 3)
                else:
                    pe.wait_ge(ql_r, g - 1)
                pe.wait_ge(xl_r, 2 * (c + 1))
                h, l = xh, xl
                terms = []
                for k in range(KC):
                    terms += [(wqh[:, k, gi, :], h[:, k, :]), (wqh[:, k, gi, :], l[:, k, :]), (wql[:, k, gi, :], h[:, k, :])]
                passes(B_P[g % 2][:, :], terms, last=False, free=True).then_inc(pj_d, 1)

            def rows(g, q):
                c, gi = divmod(g, NG)
                n = TJ * g + q
                pe.wait_ge(qh_r, g + 1)
                if n == 0:
                    pe.wait_ge(ka_r, 1)
                    pe.wait_ge(v_r, 2 * B)
                else:
                    pe.wait_ge(mx_d, n)
                for s in range(2):
                    ins = mm(B_S[s][:, 0:2 * LK], qh[:, g % 2, P * q:P * q + P],
                             ka[:, c // CPB, gi, 2 * LK * s:2 * LK * (s + 1)], start=True, stop=True)
                ins.then_inc(s1_d, 1)

            def shift(g):
                pe.wait_ge(neg_r, 1)
                for q in range(TJ):
                    pe.wait_ge(mx_d, TJ * g + q + 1)
                    ins = mm(B_P[g % 2][:, P * q:P * q + P], nm[:, g % 2, q, :], negI[:], start=False, stop=q == TJ - 1,
                             skip_group_check=True)
                ins.then_inc(nm_d, 1)

            def keys(g, k):
                c, gi = divmod(g, NG)
                b = c // CPB
                n = (GH + 1) * g + k
                if k == 0:
                    pe.wait_ge(ql_r, g + 1)
                if n == 0:
                    pe.wait_ge(kb_r, 2 * GH)
                    pe.wait_ge(kg_r, 2)
                if n >= 2:
                    pe.wait_ge(ex_d, n - 1)
                if k < GH:
                    a, b_ = ka[:, b, gi, LK * k:LK * k + P], kb[:, b, gi, P * k:P * k + P]
                else:
                    a, b_ = ka[:, b, gi, LK * GH:LK * GH + P], kb[:, b, gi, P * GH:P * GH + P]
                passes(B_ST[n % 2][:, :], [(a, qh[:, g % 2, :]), (b_, ql[:, g % 2, :])]).then_inc(st_d, 1)

            def av(g):
                c, gi = divmod(g, NG)
                b = c // CPB
                if g == 0:
                    pe.wait_ge(v_r, 2 * B)
                    pe.wait_ge(ones_r, 1)
                else:
                    pe.wait_ge(u_r, g)
                for j in range(GH):
                    pe.wait_ge(ex_d, (GH + 1) * g + j + 1)
                    mm(B_U[32 * j:32 * j + 32, :], vmain[:, b, GH * gi + j, :], pt[:, j, :], start=True, stop=False,
                       skip_group_check=True)
                pe.wait_ge(ex_d, (GH + 1) * (g + 1))
                mm(B_U[:, :], vtail[:, b, gi, :], pt[:, GH, :], start=False, stop=True,
                   skip_group_check=True).then_inc(av_d, 1)

            def uz(n):
                c, j = divmod(n, TJ)
                pe.wait_ge(u_r, NG * (c + 1))
                take_tok(z_r, n + 1)
                for gi in range(NG):
                    ins = nc.tensor.transpose(B_TOK[:, P * gi:P * gi + P], u[:, (NG * c + gi) % NU, P * j:P * j + P], ident[:])
                ins.then_inc(uz_d, 1)

            def ztr(n):
                take_tok(zt_r, n + 1)
                for k in range(KC):
                    ins = nc.tensor.transpose(B_TOK[:, P * k:P * k + P], z[:, n % 2, P * k:P * k + P], ident[:])
                ins.then_inc(zt_d, 1)

            def wproj(n):
                if n == 0:
                    pe.wait_ge(ld["wp"], 16)
                take_tok(x1_r, n + 1)
                passes(B_TOK[:, 0:D], [(zt[:, n % 2, k, :], wp[:, k, :]) for k in range(KC)]).then_inc(wp_d, 1)

            def prep(n):
                t = PREP[n]
                if n:
                    pe.wait_ge(prep_r, n)
                take_tok(prep_r, n + 1)
                st, bk_ = stage[0], B_TOK
                if t[0] == "anchor":
                    i = t[1]
                    pe.wait_ge(ld_a[i], 16)
                    for m in range(4 * i, min(4 * i + 4, M1)):
                        o = P * (m - 4 * i)
                        ins = passes(bk_[:, B * (m - 4 * i):B * (m - 4 * i) + B],
                                     [(st[:, k, o:o + P], sm("cond", B * k, B)) for k in range(KC)])
                elif t[0] == "w2":
                    pe.wait_ge(ld_a[4 + t[1]], 16)
                    pe.wait_ge(ld["outw"], 16)
                    for r in range(2):
                        o = P * (2 * t[2] + r)
                        ins = passes(bk_[:, D * r:D * r + D], [(st[:, k, o:o + P], outw[:, k, :]) for k in range(KC)])
                elif t[0] in ("pk", "v"):
                    pe.wait_ge(ld["ctxT"], 16)
                    w = pw[:, 1 if t[0] == "pk" else 2]
                    pe.wait_ge(ld["pwk" if t[0] == "pk" else "pwv"], 16)
                    ins = passes(bk_[:, 0:B * KP], [(w[:, k, P * t[1]:P * t[1] + P], ctxT[:, k].rearrange("p b n -> p (b n)"))
                                                    for k in range(KC)])
                elif t[0] == "kq":
                    pe.wait_ge(ld["pwqT"], 16)
                    ins = passes(bk_[:, 0:B * KP], [(pw[:, 0, k, P * t[1]:P * t[1] + P], pk[:, k].rearrange("p b n -> p (b n)"))
                                                    for k in range(KC)])
                elif t[0] == "mr":
                    for e in range(E):
                        ins = passes(bk_[:, LK * e:LK * e + LK], [(same(sm("rwe", E * k + e)), vf[:, k, t[1], 0:LK]) for k in range(KC)])
                elif t[0] == "b2":
                    pe.wait_ge(ld["outw"], 16)
                    for e in range(2 * t[1], min(2 * t[1] + 2, E)):
                        o = D * (e - 2 * t[1])
                        ins = passes(bk_[:, o:o + D], [(same(sm("eb2", E * k + e)), outw[:, k, :]) for k in range(KC)])
                else:
                    for b in range(B):
                        ins = passes(bk_[:, E * b:E * b + E], [(same(sm("cond", B * k + b)), sm("rwa", E * k, E)) for k in range(KC)])
                ins.then_inc(prep_mm, 1)

            walk(l0_steps(), {"xt": xt, "proj": proj, "rows": rows, "shift": shift, "keys": keys, "av": av,
                              "uz": uz, "zt": ztr, "wp": wproj, "prep": prep})


            def mpiece(n):
                b, i = MP[n]
                w = min(512, W1N - 512 * i)
                if n == 0:
                    pe.wait_ge(ld["w1e"], 16)
                    pe.wait_ge(prep_r, len(PREP))
                    pe.wait_ge(ex_d, (GH + 1) * GR)
                    pe.wait_ge(u_r, GR)
                    pe.wait_ge(ql_r, GR)
                if n >= 4:
                    pe.wait_ge(m_l, n - 3)
                src = M_BANK[n % 4]
                rows_ = P if b is not None else 32 * B
                passes(src[0:rows_, 0:w],
                       [((vt[:, k].rearrange("p b n -> p (b n)") if b is None else vf[:, k, b, 0:P]),
                         w1e[:, k, 512 * i:512 * i + w]) for k in range(KC)]).then_inc(m_mm, 1)

            def nxt(c, half):
                if c and half == 0:
                    pe.wait_ge(w_r, 2 * c)
                    pe.wait_ge(x1_r, TJ * NC)
                elif half == 0:
                    pe.wait_ge(mx_d, TJ * GR)
                for j in (2 * half, 2 * half + 1):
                    n = TJ * c + j
                    pe.wait_ge(l_r, n + 1)
                    for k in range(KC):
                        ins = nc.tensor.transpose(feat(c)[k][:, P * j:P * j + P], lnt1[:, n % 2, P * k:P * k + P], ident[:])
                    ins.then_inc(l_t, 1)

            def score(n):
                c, j = divmod(n, TJ)
                pe.wait_ge(nf_r, KC * (c + 1))
                if n == 0:
                    pe.wait_ge(prep_r, PI[("cr",)] + 1)
                    pe.wait_ge(ql_r, GR)
                if n:
                    pe.wait_ge(e1_d, n)
                passes(B_SC[:, 0:SC1], [(nxf[:, k, P * j:P * j + P], kq[:, k, c // CPB, :]) for k in range(KC)]).then_inc(sc_d, 1)

            def wtr(n):
                c, j = divmod(n, TJ)
                pe.wait_ge(pn_r, n + 1)
                nc.tensor.transpose(feat(c)[0][:, P * j:P * j + P], pn[:, n % 2, :], ident[:])
                nc.tensor.transpose(feat(c)[1][0:TAIL3, P * j:P * j + P], pn3[:, n % 2].rearrange("p a n -> p (a n)"),
                                    ident[:]).then_inc(w_t, 1)

            def hidden(c, m):
                n = M1 * c + HORD.index(m)
                b = c // CPB
                if n == 0:
                    pe.wait_ge(w1_r, 2 * NW1)
                if m == HB:
                    pe.wait_ge(nl_r, KC * (c + 1))
                    pe.wait_ge(w_r, 2 * (c + 1))
                    pe.wait_ge(m_l, len(MP))
                if n >= 2:
                    pe.wait_ge(h_r, n - 1)
                o = slice(P * m, P * m + P)
                h, l = nxh[:, c % 2], nxl[:, c % 2]
                terms = []
                for k in range(KC):
                    terms += [(w1h[:, k, o], h[:, k, :]), (w1h[:, k, o], l[:, k, :]), (w1l[:, k, o], h[:, k, :])]
                terms += [(mh[:, b, o], wh[:, c % 2, :]), (mh[:, b, o], wl[:, c % 2, :]), (ml[:, b, o], wh[:, c % 2, :]),
                          (mt[:, b, o], wt[:, c % 2, :])]
                passes(B_H[n % 2][:, :], terms).then_inc(h_mm, 1)

            def gate(n):
                c, j = divmod(n, TJ)
                if n == 0:
                    pe.wait_ge(ld["gw2"], 16)
                pe.wait_ge(h_r, M1 * c + GB)
                if n:
                    pe.wait_ge(gz_r, n)
                passes(B_G[:, 0:D], [(hg[:, k, P * j:P * j + P], gw2[:, k, :]) for k in range(KC)]).then_inc(g_mm, 1)

            def expert(c, e, j):
                q = E * c + e
                n = TJ * q + j
                pe.wait_ge(h_r, M1 * c + GB + 4 * (e + 1))
                if n >= 2:
                    pe.wait_ge(y_r, n - 1)
                passes(B_Y[n % 2][:, 0:D], [(hid[:, q % 2, r, P * j:P * j + P], w2[:, 4 * e + r, :]) for r in range(4)]).then_inc(y_mm, 1)

            walk(between_steps(), {"uz": uz, "zt": ztr, "wp": wproj, "m": mpiece, "nxt": nxt, "score": score, "wtr": wtr})
            walk(l1_steps(), {"nxt": nxt, "score": score, "wtr": wtr, "hidden": hidden, "gate": gate, "expert": expert})


def laid_out(v):
    f = lambda name: np.ascontiguousarray(v[name])
    chunks = lambda w: w.reshape(w.shape[0] // P, P, -1).transpose(1, 0, 2)
    rep = lambda row, n=P: np.broadcast_to(row, (n,) + row.shape)
    x, ctx_, cond = f("x"), f("ctx_1024"), f("cond_1024")
    zeros = lambda *s: np.zeros(s, x.dtype)
    twice = lambda w: np.repeat(w.reshape(-1, NG, GH, 1, DH), 2, axis=3).reshape(w.shape[0], NG * P)
    wkv, bkv = f("L0_xcond_Wkv"), f("L0_xcond_bkv")
    a = {"x": x.reshape(B * LQ // P, P, D).transpose(1, 0, 2)}
    p = np.arange(P)
    cols = lambda vec: vec.reshape(-1, P).T
    rw, w1 = f("L1_xcond_router_W"), np.concatenate([*f("L1_xcond_e_w1"), f("L1_xcond_gate_w1")], axis=1)
    w1r = np.concatenate([f("L1_xcond_e_b1").ravel(), f("L1_xcond_gate_b1")])
    bss = np.concatenate([f("L0_xcond_bss_q"), f("L0_xcond_bss_kv")])
    a["small"] = np.concatenate([
        chunks(cond.T).reshape(P, -1), cols(bss), cols(twice(f("L0_xcond_bq")[None])[0]), cols(twice(bkv[None, :D])[0]),
        cols(f("L1_xcond_ln_gamma")), cols(f("L1_xcond_ln_beta")), cols(w1r), rep(f("L1_xcond_router_b")),
        (p % 32 < DH).astype(np.float32)[:, None], (p % 32 >= DH).astype(np.float32)[:, None], (p % 32 == DH).astype(np.float32)[:, None],
        (p % 32 < KT).astype(np.float32)[:, None],
        chunks(rw[0:D]).reshape(P, -1), chunks(rw[2 * D:]).reshape(P, -1),
        chunks(rw[D:2 * D]).reshape(P, -1), chunks(f("L1_xcond_e_b2").T).reshape(P, -1)], axis=1)
    a["ident"] = np.eye(P, dtype=np.float32)
    ct = zeros(P, 3, D)
    for b in range(B):
        ct[:, b] = ctx_[b, 0:P]
        ct[32 * b:32 * b + KT, 2] = ctx_[b, P:]
    a["ctx"] = ct
    cT = zeros(P, KC, B, KP)
    for b in range(B):
        cT[:, :, b, 0:LK] = chunks(ctx_[b].T)
    a["ctxT"] = cT
    a["wss"] = chunks(np.concatenate([f("L0_xcond_Wss_q"), f("L0_xcond_Wss_kv")], axis=1)).reshape(P, KC, 8, P)
    a["wq"] = chunks(twice(f("L0_xcond_Wq"))).reshape(P, KC, NG, P)
    a["wk"] = chunks(twice(wkv[:, :D])).reshape(P, KC, NG, P)
    a["wv"], a["bv"] = chunks(wkv[:, D:]), rep(bkv[D:])
    a["wp"], a["bp"] = chunks(f("L0_xcond_Wp")), rep(f("L0_xcond_bp"))
    a["pwqT"], a["pwk"], a["pwv"] = chunks(f("L1_xcond_Wq").T), chunks(f("L1_xcond_Wk")), chunks(f("L1_xcond_Wv"))
    a["w1n"], a["w1e"], a["w1a"] = chunks(w1[0:D]), chunks(w1[D:2 * D]), chunks(w1[2 * D:])
    a["ew2T"] = chunks(f("L1_xcond_e_w2").reshape(E * RH, D).T)
    a["outw"], a["outb"] = chunks(f("L1_xcond_out_w")), rep(f("L1_xcond_out_b"))
    a["gw2"], a["gb2"] = chunks(f("L1_xcond_gate_w2")), rep(f("L1_xcond_gate_b2"))
    return {n: np.ascontiguousarray(a[n].reshape(s)) for n, s in SHAPES.items()}


def kernel(**inputs):
    import concourse.bacc as bacc
    from concourse.bass_utils import run_bass_kernel_spmd

    nc = bacc.Bacc("TRN2", target_bir_lowering=False, num_devices=1)
    arrays = laid_out({k: np.asarray(v) for k, v in inputs.items()})
    dram = {n: nc.dram_tensor(f"in_{n}", s, F32, kind="ExternalInput").ap() for n, s in SHAPES.items()}
    out = nc.dram_tensor("out_x", SHAPES["x"], F32, kind="ExternalOutput").ap()
    build(nc, dram, out)
    r = run_bass_kernel_spmd(nc, [{f"in_{n}": a for n, a in arrays.items()}], core_ids=[0])
    return r.results[0]["out_x"].transpose(1, 0, 2).reshape(B, LQ, D)
```

```python
from contextlib import ExitStack

import numpy as np
import concourse.bass as bass
from concourse import mybir

F32 = mybir.dt.float32
F32R = mybir.dt.float32r
I32 = mybir.dt.int32
ALU = mybir.AluOpType
ACT = mybir.ActivationFunctionType
AXX = mybir.AxisListType.X

P = 128
B, LQ, D = 2, 1024, 256
LK = 154
NH, DH = 16, 16
KC = D // P
CT = 512
NC = B * LQ // CT
CPB = NC // B
TJ = CT // P
GH = 4
NG = NH // GH
NU = NG + 1
GR = NC * NG
KP = 160
KT = LK - P
E, RH = 3, 512
HB = E * RH // P
GB = D // P
M1 = HB + GB
W1N = M1 * P
SC1 = LK + E
EPS = 1e-5
TAIL3 = 96

SM = {}
_at = 0
for _n, _w in (("cond", KC * B), ("bss", 8), ("bq", NG), ("bk", NG), ("gamma", KC), ("beta", KC),
               ("b1", M1), ("rb", E), ("m0", 1), ("m1", 1), ("m16", 1), ("m26", 1), ("rwn", KC * E),
               ("rwa", KC * E), ("rwe", KC * E), ("eb2", KC * E)):
    SM[_n] = (_at, _at + _w)
    _at += _w
SMW = _at

SHAPES = {
    "x": (P, B * LQ // P, D), "small": (P, SMW), "ident": (P, P), "ctx": (P, 3, D),
    "ctxT": (P, KC, B, KP), "wss": (P, KC, 8, P), "wq": (P, KC, NG, P), "wk": (P, KC, NG, P),
    "wv": (P, KC, D), "bv": (P, D), "wp": (P, KC, D), "bp": (P, D),
    "pwqT": (P, KC, D), "pwk": (P, KC, D), "pwv": (P, KC, D),
    "w1n": (P, KC, W1N), "w1e": (P, KC, W1N), "w1a": (P, KC, W1N),
    "ew2T": (P, KC, E * RH), "outw": (P, KC, D),
    "outb": (P, D), "gw2": (P, KC, D), "gb2": (P, D),
}


def build(nc, dram, out):
    ctx = ExitStack()
    with ctx:
        def sem(name):
            return ctx.enter_context(nc.semaphore(name))

        def sb(name, shape, dt=F32, where=ctx):
            return where.enter_context(nc.sbuf_tensor(name, list(shape), dt))

        pair = ctx.enter_context(nc.psum_tensor("pair", [P, 2, 512], F32))
        bank = [ctx.enter_context(nc.psum_tensor(f"bank{i}", [P, 512], F32)) for i in range(6)]
        B_S, B_P, B_ST, B_U, B_TOK = [pair[:, i, :] for i in range(2)], bank[0:2], bank[2:4], bank[4], bank[5]
        B_Y, B_G, B_SC, B_H, B_F = B_S, bank[0], bank[1], bank[2:4], bank[4:6]
        SS_BANK = [B_U, B_P[1]]
        K_BANK = [B_ST[0], B_ST[1], B_P[0], B_P[1]]
        V_BANK = [B_U, B_TOK, B_ST[0], B_ST[1]]
        M_BANK = [B_TOK] * 4 + [(B_H[0], B_H[1], B_G)[n % 3] for n in range(8)]

        x = sb("x_sb", (P, NC * TJ, D))
        small = sb("small_sb", (P, SMW))
        ident = sb("ident_sb", (P, P))
        negI = sb("negI", (P, P), F32R)
        w1h = sb("w1h", (P, KC, W1N), F32R)
        w1l = sb("w1l", (P, KC, W1N), F32R)
        pre0 = ExitStack()
        ctxt = sb("ctx_sb", (P, 3, D), F32, pre0)
        vtf = sb("vtf", (P, D), F32, pre0)
        bv = sb("bv_sb", (P, D), F32, pre0)
        xkv = sb("xkv", (P, KC, B, KP), F32, pre0)
        pre0.close()
        raw = ExitStack()
        w2 = sb("w2", (P, HB, D), F32, raw)
        raw.close()
        w2l = sb("w2l", (P, HB, D), F32R)
        b2 = sb("b2", (P, E, D))
        ab1 = sb("ab1", (P, M1, B))
        kq = sb("kq", (P, KC, B, SC1))
        vf = sb("vf", (P, KC, B, KP))
        vt = sb("vt", (P, KC, B, 32))
        mr = sb("mr", (P, B, E, LK))
        cr = sb("cr", (P, B, E))
        stage = [sb("stage0", (P, KC, 512)), sb("stage1", (P, KC, 256))]
        st6 = sb("st6", (P, TJ + 3, 6))
        mv = sb("mv", (P, TJ + 3, 2))
        rs = sb("rs", (P, 3, TJ + 3))

        def sm(name, i=0, n=1):
            return small[:, SM[name][0] + i:SM[name][0] + i + n]

        ops = ExitStack()
        ctxT = sb("ctxT_sb", (P, KC, B, KP), F32, ops)
        pw = sb("pw", (P, 3, KC, D), F32, ops)
        pk = sb("pk", (P, KC, B, KP), F32, ops)
        outb = sb("outb_sb", (P, D), F32, ops)
        ops.close()
        w1_ = ExitStack()
        w1e = sb("w1e_sb", (P, KC, W1N), F32, w1_)
        w1_.close()
        late = ExitStack()
        acc = sb("acc", (P, TJ, D), F32, late)
        gz = sb("gz", (P, 2, D), F32, late)
        th = sb("th", (P, TJ, D), F32, late)
        late.close()
        sb("place", (P, KC, W1N))

        l0 = ExitStack()
        KAW, KBW = GH * LK + P, GH * P + P
        keys_ = sb("keys", (P, B, NG, KAW + KBW), F32R, l0)
        ka, kb = keys_[:, :, :, 0:KAW], keys_[:, :, :, KAW:KAW + KBW]
        bp = sb("bp_sb", (P, D), F32, l0)
        wp = sb("wp_sb", (P, KC, D), F32, l0)
        wqh = sb("wqh", (P, KC, NG, P), F32R, l0)
        wql = sb("wql", (P, KC, NG, P), F32R, l0)
        ssc = sb("ssc", (P, 8, B), F32, l0)
        vmain = sb("vmain", (P, B, NH, 32), F32, l0)
        vtail = sb("vtail", (P, B, NG, P), F32, l0)
        lnt = sb("lnt", (P, 2, D), F32, l0)
        xh = sb("xh", (P, KC, CT), F32R, l0)
        xl = sb("xl", (P, KC, CT), F32R, l0)
        xf = sb("xf", (P, KC, CT), F32, l0)
        nm = sb("nm", (P, 2, TJ, P), F32R, l0)
        rz = sb("rz", (P, NH), F32, l0)
        bkm = sb("bkm", (P, NG), F32, l0)
        warm = sb("warm", (P, 1), F32, l0)
        pre = ExitStack()
        wss = sb("wss_sb", (P, KC, 8, P), F32, pre)
        wk = sb("wk_sb", (P, KC, NG, P), F32, pre)
        wv = sb("wv_sb", (P, KC, D), F32, pre)
        wq = sb("wq_sb", (P, KC, NG, P), F32, pre)
        xkv4 = sb("xkv4", (P, KC, B, GH, 32), F32, pre)
        kh = sb("kh", (P, NG, B, KP), F32R, pre)
        kg = sb("kg", (P, NG, B, LK), F32R, pre)
        pre.close()
        qh = sb("qh", (P, 2, CT), F32R, l0)
        ql = sb("ql", (P, 2, CT), F32R, l0)
        z = sb("z", (P, 2, D), F32, l0)
        zt = sb("zt", (P, 2, KC, P), F32, l0)
        pt = sb("pt", (P, GH + 1, CT), F32, l0)
        u = sb("u", (P, NU, CT), F32, l0)
        csilu = sb("csilu", (P, KC, B), F32, l0)
        outw = sb("outw_sb", (P, KC, D), F32, l0)
        l0.close()

        l1 = ExitStack()
        m_ = sb("m_ev", (P, B, 3, W1N), F32R, l1)
        mh, ml, mt = m_[:, :, 0, :], m_[:, :, 1, :], m_[0:TAIL3, :, 2, :]
        gw2 = sb("gw2_sb", (P, KC, D), F32, l1)
        gb2 = sb("gb2_sb", (P, D), F32, l1)
        hg = sb("hg", (P, GB, CT), F32, l1)
        lnt1 = sb("lnt1", (P, 2, D), F32, l1)
        wh = sb("wh", (P, 2, CT), F32R, l1)
        wl = sb("wl", (P, 2, CT), F32R, l1)
        wt = sb("wt", (TAIL3, 2, CT), F32R, l1)
        pe_ = sb("pe_", (P, 2, LK), F32, l1)
        nxf = sb("nxf", (P, KC, CT), F32, l1)
        nx0 = sb("nx0", (P, 2, KC, CT), F32R, l1)
        pn = sb("pn", (P, 2, P), F32, l1)
        pn3 = sb("pn3", (P, 2, 3, 32), F32, l1)
        ttr = sb("ttr", (P, LK), F32, l1)
        nmx = sb("nmx", (P, 2), F32, l1)
        sme = sb("sme", (P, 2), F32, l1)
        rec = sb("rec", (P, 2), F32, l1)
        lg = sb("lg", (P, TJ, E), F32, l1)
        lw = sb("lw", (P, TJ, E), F32, l1)
        lx = sb("lx", (P, TJ), F32, l1)
        le = sb("le", (P, TJ, E), F32, l1)
        pr = sb("pr", (P, 2, TJ, E), F32, l1)
        nx1 = sb("nx1", (P, 2, KC, CT), F32R, l1)
        nx = (nx0, nx1)
        w2h = sb("w2h", (P, HB, D), F32R, l1)
        hid = sb("hid", (P, 2, CT), F32, l1)
        hs = sb("hs", (P, 3, 2, CT), F32R, l1)
        l1.close()

        ld = {n: sem(f"ld_{n}") for n in SHAPES if n not in ("x", "wss", "w1n", "w1a", "ew2T")}
        ld_ss = [sem("ld_wss_q"), sem("ld_wss_kv")]
        ld_x = [sem(f"ld_x{c}") for c in range(NC)]
        NW1 = W1N // 256
        PE_PIECES = [("w1a", i) for i in range(4)] + [("ew2T", i) for i in range(3)]
        ld_a, ld_b = [sem(f"ld_piece{i}") for i in range(7)], [sem(f"ld_w1n{i}") for i in range(NW1)]
        stored = sem("stored")
        silu_d, ss_mm, ss_r = sem("silu_done"), sem("ss_mm"), sem("ss_ready")
        zeroed, neg_r, wq_r = sem("zeroed"), sem("neg_ready"), sem("wq_split")
        cl_r, cl_t, xkv_r, x4_r, ones_r = sem("ctx_ln"), sem("ctx_t"), sem("xkv_ready"), sem("xkv4_ready"), sem("ones_ready")
        kg1_r, bkm_r = sem("lo_rows_hi"), sem("bkm_ready")
        k_mm, kh_r, kg_r, v_mm, v_r, ka_r, kb_r = sem("k_mm"), sem("kh_ready"), sem("kg_ready"), sem("v_mm"), sem("v_ready"), sem("ka_ready"), sem("kb_ready")
        prep_mm, prep_r, w1_r = sem("prep_mm"), sem("prep_ready"), sem("w1_split")
        ln_r, ln_t, xf_r, xh_r, xl_r = sem("ln_ready"), sem("ln_taken"), sem("xf_ready"), sem("xh_ready"), sem("xl_ready")
        pj_d, qh_r, ql_r = sem("proj_done"), sem("qh_ready"), sem("ql_ready")
        s1_d, mx_d, nm_d = sem("rowscores_done"), sem("max_done"), sem("shift_added")
        st_d, ex_d, av_d, u_r = sem("keyscores_done"), sem("exp_done"), sem("av_done"), sem("u_ready")
        uz_d, z_r, zt_d, zt_r = sem("uz_done"), sem("z_ready"), sem("zt_done"), sem("zt_ready")
        wp_d, xb_r, x1_r = sem("wp_done"), sem("xb_ready"), sem("x1_ready")
        m_mm, mt_r, m_h, m_l = sem("m_mm"), sem("tail_keys_copied"), sem("m_hi"), sem("m_lo")
        l_r, l_t, nf_r, nh_r, nl_r = sem("l_ready"), sem("l_taken"), sem("nxf_ready"), sem("nxh_ready"), sem("nxl_ready")
        sc_d, nm1_r, e1_d, pn_r, w_t = sem("sc_done"), sem("nmx_ready"), sem("e1_done"), sem("pn_ready"), sem("w_taken")
        wh_r, w_r, lg_r, le_r, pr_r = sem("wh_ready"), sem("w_ready"), sem("lg_ready"), sem("le_ready"), sem("pr_ready")
        h_mm, h_r, g_mm, gz_r, th_r = sem("h_mm"), sem("h_ready"), sem("g_mm"), sem("gz_ready"), sem("th_ready")
        w2_r, hh_r, hl_r = sem("w2_split"), sem("hidden_hi"), sem("hidden_lo")
        y_mm, y_r, f_r, o_r = sem("y_mm"), sem("y_used"), sem("delta_ready"), sem("out_ready")
        rg_r, rs_r = sem("rsqrt_guess"), sem("rsqrt_ready")
        dch, pch = sem("vector_chain"), sem("pool_chain")

        OPS = [("pk", 0), ("v", 0), ("pk", 1), ("v", 1), ("kq", 0), ("b2", 0), ("kq", 1), ("b2", 1)]
        W2P = [[("w2", i, hf) for hf in range(2)] for i in range(3)]
        PREP = OPS + [("anchor", 0), ("mr", 0), ("anchor", 1), ("mr", 1), ("anchor", 2), ("cr",), ("anchor", 3),
                      *W2P[0], *W2P[1], *W2P[2]]
        PI = {t: n for n, t in enumerate(PREP)}

        def tile_steps(n):
            return ("uz", n), ("zt", n), ("wp", n)

        def l0_steps():
            yield from (("proj", 0, 0), ("proj", 0, 1))
            for q in range(TJ):
                yield ("rows", 0, q)
                yield ("val", q)
            yield ("shift", 0)
            yield from (("proj", 1, 0), ("proj", 1, 1))
            yield ("place", 1)
            prep = 0
            for g in range(GR):
                c, gi = divmod(g, NG)
                n, m = g + 1, g + 2
                fill = [()] * 6
                first = list(front1(0))
                if c > 0 and gi < 2:
                    fill = [(s,) for t in (0, 1) for s in tile_steps(TJ * (c - 1) + 2 * gi + t)]
                if c + 1 < NC:
                    if gi == 0:
                        fill[3] += (("stats", c + 1, 0),)
                        fill[5] += (("stats", c + 1, 1),)
                    elif gi == 1:
                        fill[3] += (("rsqrt", c + 1),)
                        fill[5] += (("norm", c + 1, 0),)
                    elif gi == 2:
                        fill[0] += (("xt", c + 1, 0), ("norm", c + 1, 1))
                        fill[1] += (("xt", c + 1, 1), ("split", c + 1, 0))
                        fill[2] += (("split", c + 1, 1),)
                for at, place, i in ((GR - 4, 3, 0), (GR - 2, 0, 1), (GR - 2, 5, 2), (GR - 1, 0, 3), (GR - 1, 2, 4),
                                     (GR - 1, 3, 5), (GR - 1, 5, 6)):
                    if g == at:
                        fill[place] += tuple(first[i])
                for i in () if c and gi < 2 else (2, 5) if gi == 2 else (0, 2, 5):
                    if i == (5 if gi == 2 else 2) and c >= CPB:
                        fill[i] += (("m", 2 * (c - CPB) + gi - 2), ("m_taken", 2 * (c - CPB) + gi - 2))
                    elif prep < len(PREP):
                        fill[i] += (("prep", prep),)
                        prep += 1
                more = n < GR
                order = [("keys", g, 0), more and ("rows", n, 0), ("keys", g, 1), fill[0], ("keys", g, 2),
                         more and ("rows", n, 1), ("keys", g, 3), fill[1], ("keys", g, 4), more and ("rows", n, 2), fill[2]]
                if gi != 2:
                    order += [m < GR and ("proj", m, 0), more and ("rows", n, 3), fill[3], ("av", g), fill[4],
                              more and ("shift", n), m < GR and ("proj", m, 1)]
                else:
                    order += [more and ("rows", n, 3), fill[3], ("av", g), fill[4], more and ("shift", n),
                              m < GR and ("proj", m, 0), m < GR and ("proj", m, 1)]
                order += [fill[5]]
                for step in order:
                    if step and isinstance(step[0], str):
                        yield step
                    elif step:
                        yield from step
            assert prep == len(PREP)

        MP = [(0, i) for i in range(4)] + [(b, i) for i in range(4) for b in (None, 1)]
        MTAIL = MP.index((None, 3))

        NM0 = 4

        def m_hi(n):
            return n + 1 + sum(b is None for b, _ in MP[0:n + 1])

        def front1(c):
            n = TJ * c
            yield (("ln_stats", c),)
            if c:
                yield ()
            yield (("ln", c, 0),)
            yield (("nxt", c, 0), ("ln", c, 1))
            yield (("nxt", c, 1), ("nxf", c))
            if c:
                yield ()
            yield (("score", n), ("score", n + 1))
            yield (("exp", n), ("exp", n + 1))
            yield (("weights", n), ("score", n + 2), ("score", n + 3))
            yield (("wtr", n), ("weights", n + 1))
            yield (("wtr", n + 1), ("exp", n + 2), ("exp", n + 3), *((("weights", n + 2),) if c else ()))
            if c:
                yield (("weights", n + 3),)
                yield (("wtr", n + 2), ("wtr", n + 3), ("wsplit", c))
            else:
                yield (("weights", n + 2),)
                yield ()
                yield (("wtr", n + 2), ("weights", n + 3))
                yield ()
                yield (("wtr", n + 3),)
                yield (("wsplit", c),)
                yield ()
                yield ()
            yield (("router", c),)

        def between_steps():
            first = iter(list(front1(0))[7:])
            tail = [s for j in range(TJ) for s in tile_steps(TJ * (NC - 1) + j)]
            for n in range(len(tail)):
                yield tail[n]
                if 0 < n <= len(MP) - NM0:
                    yield ("m_taken", NM0 + n - 1)
                if n < len(MP) - NM0:
                    yield ("m", NM0 + n)
                yield from next(first, ())

        def l1_steps():
            def products(c, m):
                yield ("part", c, m)
                if m % 4 == 2:
                    yield ("bias", c, m // 4)
                if m % 4 == 3:
                    for j in range(TJ):
                        yield ("sum", c, m // 4, j)
                        if (c, m) == (NC - 1, HB - 1):
                            yield ("final", TJ * c + j)

            for c in range(NC):
                take = front1(c + 1) if c + 1 < NC else iter(())
                for i, m in enumerate(HORD):
                    yield ("hidden", c, m)
                    if m < HB:
                        yield ("hsplit", c, m)
                    if i > GB + 1:
                        yield from products(c, HORD[i - 2])
                    elif i < 2 and c:
                        yield from products(c - 1, HB - 2 + i)
                    if c and 2 <= i < 2 + TJ:
                        yield ("final", TJ * (c - 1) + i - 2)
                    if c == 0 and i < E:
                        yield ("w2_split", i)
                    if 3 <= i < 3 + TJ:
                        yield ("gate", TJ * c + i - 3)
                    yield from next(take, ())
            yield from products(NC - 1, HB - 2)
            yield from products(NC - 1, HB - 1)

        LAST = TJ * (NC - 1)

        def tok_bank(n, step):
            return B_TOK if n < LAST else (B_TOK, B_U)[(3 * (n - LAST) + step) % 2]

        def ln_rows(c, half):
            return (stage[1], B_S[0]) if (c, half) == (0, 1) else (lnt, B_TOK)

        def feat(c):
            return [B_F[0][:, :], B_F[1][:, :]] if c else B_S

        HORD = [HB, HB + 1] + list(range(HB))

        def y_tile(j):
            return B_Y[j // 2][:, D * (j % 2):D * (j % 2) + D]

        def walk(steps, parts):
            for s in steps:
                if s[0] in parts:
                    parts[s[0]](*s[1:])

        block = ctx.enter_context(nc.Block())

        @block.sync
        def _(sp):
            def load(dst, name):
                sp.dma_start(dst, dram[name]).then_inc(ld[name], 16)
            load(small[:], "small")
            for half in (1, 0):
                sp.dma_start(wss[:, :, 4 * half:4 * half + 4, :], dram["wss"][:, :, 4 * half:4 * half + 4, :]).then_inc(ld_ss[half], 16)
                if half:
                    load(wk[:], "wk")
            load(wv[:], "wv")
            load(bv[:], "bv")
            load(wp[:], "wp")
            for c in range(1, NC):
                sp.dma_start(x[:, TJ * c:TJ * c + TJ, :], dram["x"][:, TJ * c:TJ * c + TJ, :]).then_inc(ld_x[c], 16)
            for n, (name, i) in enumerate(PE_PIECES):
                if n == 1:
                    sp.wait_ge(prep_r, len(OPS))
                    load(w1e[:], "w1e")
                if n:
                    pname, pi = PE_PIECES[n - 1]
                    sp.wait_ge(prep_mm, 1 + PI[("anchor", pi) if pname == "w1a" else ("w2", pi, 1)])
                w = min(512, SHAPES[name][2] - 512 * i)
                sp.dma_start(stage[0][:, :, 0:w], dram[name][:, :, 512 * i:512 * i + w]).then_inc(ld_a[n], 16)
            sp.wait_ge(x1_r, TJ * NC)
            load(gw2[:], "gw2")
            load(gb2[:], "gb2")
            for c in range(NC - 1):
                sp.wait_ge(o_r, TJ * c + TJ)
                sp.dma_start(out[:, TJ * c:TJ * c + TJ, :], x[:, TJ * c:TJ * c + TJ, :]).then_inc(stored, 16)
            for n in range(TJ * (NC - 1), TJ * NC):
                sp.wait_ge(o_r, n + 1)
                sp.dma_start(out[:, n, :], x[:, n, :]).then_inc(stored, 16)
            sp.wait_ge(stored, 16 * (NC - 1 + TJ))

        @block.gpsimd
        def _(pool):
            count = [0]

            def link(ins):
                count[0] += 1
                ins.then_inc(pch, 1)
                pool.wait_ge(pch, count[0])

            g_ = nc.gpsimd
            g_.memset(keys_[:].bitcast(F32), 0.0).then_inc(zeroed, 1)
            g_.memset(nm[:].bitcast(F32), 0.0).then_inc(zeroed, 1)
            link(g_.memset(vmain[:], 0.0))
            g_.memset(vmain[:, :, :, DH:DH + 1], 1.0).then_inc(zeroed, 1)
            g_.memset(vtail[:], 0.0).then_inc(zeroed, 1)
            pool.wait_ge(zeroed, 4)
            pool.wait_ge(ld["small"], 16)
            pool.wait_ge(ld["wq"], 16)
            g_.tensor_copy(wqh[:], wq[:]).then_inc(wq_r, 1)
            pool.wait_ge(wq_r, 1)
            g_.tensor_tensor(wql[:], wq[:], wqh[:], ALU.subtract).then_inc(wq_r, 1)
            pool.wait_ge(wq_r, 2)
            pool.wait_ge(kh_r, NG)
            for j in range(GH):
                r = slice(32 * j, 32 * j + 32)
                for dst, o, w in ((P * j, 0, P), (P * GH + 32 * j, P, KT)):
                    g_.tensor_scalar(kb[r, :, :, dst:dst + w].rearrange("p b g n -> p g b n"), kh[r, :, :, o:o + w],
                                     small[r, SM["m0"][0]:SM["m0"][1]], small[r, SM["m16"][0]:SM["m16"][1]],
                                     ALU.mult, ALU.add).then_inc(kb_r, 1)
                    pool.wait_ge(kb_r, 2 * j + (1 if w == P else 2))
            for j in range(GH):
                r = slice(32 * j, 32 * j + 32)
                link(g_.tensor_copy(vtail[r, :, :, 32 * j + DH:32 * j + DH + 1].rearrange("p b g o -> p (b g) o"),
                                    small[r, SM["m26"][0]:SM["m26"][1]].unsqueeze(1).broadcast_to([32, B * NG, 1])))
            g_.tensor_copy(kq[:, :, :, LK:SC1], sm("rwn", 0, KC * E).rearrange("p (k e) -> p k e", k=KC)
                           .unsqueeze(2).broadcast_to([P, KC, B, E])).then_inc(ones_r, 1)
            pool.wait_ge(ones_r, 1)

            def xb(c, half):
                if (c, half) == (0, 0):
                    pool.wait_ge(ld["bp"], 16)
                for j in (2 * half, 2 * half + 1):
                    n = TJ * c + j
                    pool.wait_ge(ln_r, n + 1)
                    g_.tensor_tensor(x[:, n, :], x[:, n, :], bp[:], ALU.add).then_inc(xb_r, 1)

            def newton(n):
                y, v, t = rs[:, 0, 0:TJ], rs[:, 1, 0:TJ], rs[:, 2, 0:TJ]
                pool.wait_ge(rg_r, n)
                for i in range(3):
                    link(g_.tensor_tensor(t, y, y, ALU.mult))
                    link(g_.tensor_tensor(t, t, v, ALU.mult))
                    link(g_.tensor_scalar(t, t, 1.5, None, ALU.subtract))
                    ins = g_.tensor_tensor(y, t, y, ALU.mult)
                    if i < 2:
                        link(ins)
                ins.then_inc(rs_r, 1)

            def piece(i):
                o = slice(256 * i, 256 * i + 256)
                pool.wait_ge(ld_b[i], 16)
                g_.tensor_copy(w1h[:, :, o], stage[1][:]).then_inc(w1_r, 1)
                pool.wait_ge(w1_r, 2 * i + 1)
                g_.tensor_tensor(w1l[:, :, o], stage[1][:], w1h[:, :, o], ALU.subtract).then_inc(w1_r, 1)
                if i + 1 < NW1:
                    pool.wait_ge(w1_r, 2 * i + 2)
                    pool.dma_start(stage[1][:], dram["w1n"][:, :, 256 * (i + 1):256 * (i + 2)]).then_inc(ld_b[i + 1], 16)

            def av(g):
                if g < NW1:
                    piece(g)

            pool.wait_ge(ln_t, 2)
            pool.dma_start(stage[1][:], dram["w1n"][:, :, 0:256]).then_inc(ld_b[0], 16)
            xb(0, 0)
            xb(0, 1)
            walk(l0_steps(), {"xt": xb, "av": av, "rsqrt": newton, "ln_stats": lambda c: newton(NC + c)})

            pool.wait_ge(m_h, m_hi(MTAIL))
            for b in range(B):
                pool.dma_start(mt[64:96, b, :], mt[32 * b:32 * b + 32, b, :]).then_inc(mt_r, 16)

            def hsplit(c, m):
                q = HB * c + m
                pool.wait_ge(hh_r, q + 1)
                g_.tensor_tensor(hs[:, q % 3, 1, :], hid[:, q % 2, :], hs[:, q % 3, 0, :], ALU.subtract).then_inc(hl_r, 1)

            def final(n):
                pool.wait_ge(f_r, n + 1)
                g_.tensor_tensor(x[:, n, :], x[:, n, :], acc[:, n % TJ, :], ALU.add).then_inc(o_r, 1)

            walk(l1_steps(), {"hsplit": hsplit, "final": final, "ln_stats": lambda c: newton(NC + c)})

        @block.scalar
        def _(act):
            def load(dst, name):
                act.dma_start(dst, dram[name]).then_inc(ld[name], 16)
            load(ctxt[:], "ctx")
            act.dma_start(x[:, 0:TJ, :], dram["x"][:, 0:TJ, :]).then_inc(ld_x[0], 16)
            load(ident[:], "ident")
            load(wq[:], "wq")
            A = nc.scalar.activation
            act.wait_ge(ld["small"], 16)
            A(csilu[:], small[:, 0:KC * B].rearrange("p (k b) -> p k b", k=KC), ACT.Silu).then_inc(silu_d, 1)
            load(bp[:], "bp")
            load(ctxT[:], "ctxT")
            load(pw[:, 0], "pwqT")
            load(pw[:, 1], "pwk")
            load(pw[:, 2], "pwv")
            load(outw[:], "outw")
            load(outb[:], "outb")

            act.wait_ge(ss_r, 1)
            act.wait_ge(cl_t, 1)
            for k in range(KC):
                for b in range(B):
                    for dst, o, w in ((0, P * b, P), (P, B * P + 32 * b, 32)):
                        A(xkv[:, k, b, dst:dst + w], B_S[k][:, o:o + w], ACT.Identity, bias=ssc[:, 6 + k, b:b + 1],
                          scale=ssc[:, 4 + k, b:b + 1]).then_inc(xkv_r, 1)

            def xt(c, half):
                b = c // CPB
                act.wait_ge(ln_t, 2 * c + half + 1)
                if c:
                    act.wait_ge(xl_r, 2 * (c - 1) + half + 1)
                o = 2 * P * half
                for k in range(KC):
                    A(xf[:, k, o:o + 2 * P], ln_rows(c, half)[1][:, 2 * P * k:2 * P * k + 2 * P], ACT.Identity, bias=ssc[:, 2 + k, b:b + 1],
                      scale=ssc[:, k, b:b + 1]).then_inc(xf_r, 1)

            act.wait_ge(bkm_r, 1)
            for gi in range(NG):
                act.wait_ge(k_mm, gi + 1)
                A(kg[:, gi], K_BANK[gi][:, 0:B * KP].rearrange("p (b n) -> p b n", b=B)[:, :, 0:LK], ACT.Identity,
                  bias=bkm[:, gi:gi + 1], scale=sm("m1")).then_inc(kg1_r, 1)
                A(kh[:, gi], K_BANK[gi][:, 0:B * KP].rearrange("p (b n) -> p b n", b=B), ACT.Identity,
                  bias=sm("bk", gi)).then_inc(kh_r, 1)
                if gi == 1:
                    act.wait_ge(ss_r, 2)
                    xt(0, 0)
                    xt(0, 1)
            A(warm[:], sm("bq"), ACT.Exp)

            def proj(g, k):
                if k < KC - 1:
                    return
                act.wait_ge(pj_d, g + 1)
                if g >= 2:
                    act.wait_ge(st_d, (GH + 1) * (g - 1))
                A(qh[:, g % 2, :], B_P[g % 2][:, :], ACT.Identity, bias=sm("bq", g % NG)).then_inc(qh_r, 1)

            def keys(g, k):
                n = (GH + 1) * g + k
                act.wait_ge(st_d, n + 1)
                if k == 0 and g:
                    act.wait_ge(av_d, g)
                if n == 0:
                    act.wait_ge(v_r, 2 * B)
                A(pt[:, k, :], B_ST[n % 2][:, :], ACT.Exp, scale=DH ** -0.5).then_inc(ex_d, 1)

            def av(g):
                c = g // NG
                act.wait_ge(av_d, g + 1)
                if g == 0:
                    act.wait_ge(ka_r, B)
                if g >= NU:
                    act.wait_ge(uz_d, TJ * ((g - NU) // NG + 1))
                A(u[:, g % NU, :], B_U[:, :], ACT.Copy).then_inc(u_r, 1)

            def ztr(n):
                act.wait_ge(zt_d, n + 1)
                if n >= 2:
                    act.wait_ge(wp_d, n - 1)
                A(zt[:, n % 2, :, :], tok_bank(n, 1)[:, 0:D].rearrange("p (k n) -> p k n", k=KC), ACT.Copy).then_inc(zt_r, 1)

            def mpiece(n):
                b, i = MP[n]
                w = min(512, W1N - 512 * i)
                act.wait_ge(m_mm, n + 1)
                src = M_BANK[n]
                o = slice(512 * i, 512 * i + w)
                if b is None:
                    A(mt[0:32, 0, o], src[0:32, 0:w], ACT.Copy).then_inc(m_h, 1)
                    A(mt[32:64, 1, o], src[32:64, 0:w], ACT.Copy).then_inc(m_h, 1)
                else:
                    A(mh[:, b, o], src[:, 0:w], ACT.Copy).then_inc(m_h, 1)

            def nxf_(c):
                act.wait_ge(l_t, TJ * (c + 1))
                if c:
                    act.wait_ge(sc_d, TJ * c)
                for k in range(KC):
                    if c:
                        act.wait_ge(nl_r, KC * (c - 1) + k + 1)
                    A(nxf[:, k, :], feat(c)[k], ACT.Identity, bias=sm("beta", k), scale=sm("gamma", k)).then_inc(nf_r, 1)

            def exp(n):
                act.wait_ge(nm1_r, n - n % 2 + 2)
                if n >= 2:
                    act.wait_ge(lg_r, n - 1)
                A(pe_[:, n % 2, :], B_SC[:, SC1 * (n % 2):SC1 * (n % 2) + LK], ACT.Exp, bias=nmx[:, n % 2:n % 2 + 1],
                  accum_out=sme[:, n % 2:n % 2 + 1]).then_inc(e1_d, 1)

            def wsplit(c):
                act.wait_ge(w_t, TJ * (c + 1))
                if c == 0:
                    act.wait_ge(av_d, GR)
                if c >= 2:
                    act.wait_ge(h_mm, M1 * (c - 1))
                A(wh[:, c % 2, :], feat(c)[0][:, :], ACT.Copy).then_inc(wh_r, 1)
                A(wt[:, c % 2, :], feat(c)[1][0:TAIL3, :], ACT.Copy).then_inc(wh_r, 1)

            def router(c):
                act.wait_ge(le_r, 2 * c + 1)
                A(le[:], lg[:], ACT.Exp).then_inc(le_r, 1)

            def hidden(c, m):
                n = M1 * c + HORD.index(m)
                act.wait_ge(h_mm, n + 1)
                if m >= HB:
                    if c:
                        act.wait_ge(g_mm, TJ * c)
                    dst = hg[:, m - HB, :]
                else:
                    q = HB * c + m
                    if q >= 2:
                        act.wait_ge(hl_r, q - 1)
                    dst = hid[:, q % 2, :]
                A(dst, B_H[n % 2][:, :], ACT.Silu, bias=ab1[:, m, c // CPB:c // CPB + 1]).then_inc(h_r, 1)

            def gate(n):
                act.wait_ge(gz_r, n + 1)
                if n >= TJ:
                    act.wait_ge(o_r, n - TJ + 1)
                A(th[:, n % TJ, :], gz[:, n % 2, :], ACT.Tanh, scale=0.5).then_inc(th_r, 1)

            first = {"m_taken": mpiece, "nxf": nxf_, "exp": exp, "wsplit": wsplit, "router": router}
            walk(l0_steps(), {"xt": xt, "proj": proj, "keys": keys, "av": av, "zt": ztr, **first})
            walk(between_steps(), {"zt": ztr, **first})
            walk(l1_steps(), {"nxf": nxf_, "exp": exp, "wsplit": wsplit, "router": router, "hidden": hidden, "gate": gate})

        @block.vector
        def _(dve):
            V = nc.vector
            count = [0]

            def link(ins):
                count[0] += 1
                ins.then_inc(dch, 1)
                dve.wait_ge(dch, count[0])

            def stats(tiles):
                for t, src in tiles:
                    w = src.shape[0]
                    ins = V.bn_stats(st6[0:w, t, :], src)
                link(ins)
                for t, src in tiles:
                    w = src.shape[0]
                    ins = V.bn_aggr(mv[0:w, t, :], st6[0:w, t, :])
                link(ins)

            def guess(at=0, n=TJ):
                y, v, t = rs[:, 0, at:at + n], rs[:, 1, at:at + n], rs[:, 2, at:at + n]
                link(V.tensor_scalar(v, mv[:, at:at + n, 1], EPS, None, ALU.add))
                link(V.tensor_scalar(t.bitcast(I32), v.bitcast(I32), 1, None, ALU.logical_shift_right))
                V.tensor_scalar(y.bitcast(I32), t.bitcast(I32), -1.0, float(0x5F3759DF - 2 ** 31), ALU.mult, ALU.add)
                return V.tensor_scalar(v, v, 0.5, None, ALU.mult)

            def rsqrt(at, n):
                y, v, t = rs[:, 0, at:at + n], rs[:, 1, at:at + n], rs[:, 2, at:at + n]
                link(guess(at, n))
                for _ in range(3):
                    link(V.tensor_tensor(t, y, y, ALU.mult))
                    link(V.tensor_tensor(t, t, v, ALU.mult))
                    link(V.scalar_tensor_tensor(y, t, 1.5, y, ALU.subtract, ALU.mult))

            def normalised(dst, t, src, rows=P):
                return V.tensor_scalar(dst, src, mv[0:rows, t, 0:1], rs[0:rows, 0, t:t + 1], ALU.subtract, ALU.mult)

            def norm(c, half):
                if c and half == 0:
                    dve.wait_ge(rs_r, c)
                for j in (2 * half, 2 * half + 1):
                    n = TJ * c + j
                    if c:
                        dve.wait_ge(ln_t, 2 * c + half)
                    normalised(ln_rows(c, half)[0][:, j % 2, :], j, x[:, n, :]).then_inc(ln_r, 1)

            def xsplit(c, half):
                o = slice(2 * P * half, 2 * P * half + 2 * P)
                dve.wait_ge(xf_r, KC * (2 * c + half + 1))
                if c:
                    dve.wait_ge(pj_d, NG * c)
                V.tensor_copy(xh[:, :, o], xf[:, :, o]).then_inc(xh_r, 1)
                dve.wait_ge(xh_r, 2 * c + half + 1)
                V.tensor_tensor(xl[:, :, o], xf[:, :, o], xh[:, :, o], ALU.subtract).then_inc(xl_r, 1)

            link(V.memset(mv[:], 1.0))
            dve.wait_ge(ld["ctx"], 16)
            stats([(TJ + t, ctxt[0:P if t < 2 else 64, t, :]) for t in range(3)])
            rsqrt(TJ, 3)
            for t in range(3):
                w = P if t < 2 else 64
                normalised(ctxt[0:w, t, :], TJ + t, ctxt[0:w, t, :], w).then_inc(cl_r, 1)

            def adaln(half):
                dve.wait_ge(ss_mm, 2 - half)
                for i in (4 * half, 4 * half + 2):
                    ins = V.scalar_tensor_tensor(ssc[:, i:i + 2, :], SS_BANK[half][:, B * i:B * (i + 2)].rearrange("p (m b) -> p m b", b=B),
                                                 1.0 if i % 4 == 0 else 0.0, sm("bss", i, 2).unsqueeze(2).broadcast_to([P, 2, B]),
                                                 ALU.add, ALU.add)
                ins.then_inc(ss_r, 1)

            dve.wait_ge(ld["small"], 16)
            V.tensor_scalar(bkm[:], sm("bk", 0, NG), sm("m1"), None, ALU.mult).then_inc(bkm_r, 1)
            adaln(1)
            dve.wait_ge(ld_x[0], 16)
            stats([(j, x[:, j, :]) for j in range(TJ)])
            rsqrt(0, TJ)
            norm(0, 0)
            norm(0, 1)
            adaln(0)
            dve.wait_ge(ld["ident"], 16)
            V.tensor_scalar(negI[:], ident[:], -1.0, None, ALU.mult).then_inc(neg_r, 1)
            dve.wait_ge(xkv_r, 2 * KC * B)
            for k in range(KC):
                ins = V.tensor_copy(xkv4[:, k, :, :, :], xkv[:, k, :, P:KP].unsqueeze(2).broadcast_to([P, B, GH, 32]))
            ins.then_inc(x4_r, 1)
            for gi in range(NG):
                dve.wait_ge(kh_r, gi + 1)
                dve.wait_ge(kg1_r, gi + 1)
                V.scalar_tensor_tensor(kg[:, gi], K_BANK[gi][:, 0:B * KP].rearrange("p (b n) -> p b n", b=B)[:, :, 0:LK],
                                       sm("bk", gi), kg[:, gi], ALU.add, ALU.subtract).then_inc(kg_r, 1)
                if gi == 1:
                    xsplit(0, 0)
                    xsplit(0, 1)
            dve.wait_ge(kg_r, NG)
            dve.wait_ge(zeroed, 1)

            def place(b):
                for j in range(GH):
                    r = slice(32 * j, 32 * j + 32)
                    for dst, o, w in ((LK * j, 0, LK), (LK * GH + 32 * j, P, KT)):
                        ins = V.tensor_copy(ka[r, b, :, dst:dst + w], kg[r, :, b, o:o + w])
                ins.then_inc(ka_r, 1)

            place(0)
            def val(n):
                b, tail = n % B, n // B
                src = V_BANK[n]
                if n == 0:
                    dve.wait_ge(ld["bv"], 16)
                    dve.wait_ge(zeroed, 4)
                dve.wait_ge(v_mm, n + 1)
                if not tail:
                    V.tensor_tensor(vmain[:, b, :, 0:DH], src[:, 0:D].rearrange("p (h d) -> p h d", h=NH),
                                    bv[:].rearrange("p (h d) -> p h d", h=NH), ALU.add).then_inc(v_r, 1)
                else:
                    link(V.tensor_tensor(vtf[:], src[:, 0:D], bv[:], ALU.add))
                    for j in range(GH):
                        r = slice(32 * j, 32 * j + 32)
                        ins = V.tensor_scalar(vtail[r, b, :, 32 * j:32 * j + DH],
                                              vtf[r, :].rearrange("p (g j d) -> p g j d", g=NG, j=GH)[:, :, j, :],
                                              small[r, SM["m26"][0]:SM["m26"][1]], None, ALU.mult)
                    ins.then_inc(v_r, 1)
                    dve.wait_ge(v_r, n + 1)

            def chunk_stats(c, half):
                if half == 0:
                    dve.wait_ge(ld_x[c], 16)
                stats([(j, x[:, TJ * c + j, :]) for j in (2 * half, 2 * half + 1)])

            def chunk_rsqrt(c):
                guess().then_inc(rg_r, 1)

            def rows(g, q):
                n = TJ * g + q
                dve.wait_ge(s1_d, n + 1)
                if g >= 2:
                    dve.wait_ge(nm_d, g - 1)
                V.tensor_reduce(nm[:, g % 2, q, :].rearrange("p (h w) -> p h w", w=32)[:, :, DH:DH + 1],
                                pair[:, :, 0:2 * LK].rearrange("p s (a n) -> p s a n", a=2), AXX, ALU.max).then_inc(mx_d, 1)

            def shift(g):
                dve.wait_ge(nm_d, g + 1)
                dve.wait_ge(qh_r, g + 1)
                if g >= 2:
                    dve.wait_ge(st_d, (GH + 1) * (g - 1))
                V.scalar_tensor_tensor(ql[:, g % 2, :], B_P[g % 2][:, :], sm("bq", g % NG), qh[:, g % 2, :],
                                       ALU.add, ALU.subtract).then_inc(ql_r, 1)

            def uz(n):
                dve.wait_ge(uz_d, n + 1)
                heads = tok_bank(n, 0)[:, :].rearrange("p (h w) -> p h w", w=32)
                link(V.reciprocal(rz[:], heads[:, :, DH]))
                if n >= 2:
                    dve.wait_ge(zt_d, n - 1)
                V.tensor_tensor(z[:, n % 2, :].rearrange("p (h d) -> p h d", h=NH), heads[:, :, 0:DH],
                                rz[:].unsqueeze(2).broadcast_to([P, NH, DH]), ALU.mult).then_inc(z_r, 1)

            def wproj(n):
                dve.wait_ge(wp_d, n + 1)
                dve.wait_ge(xb_r, n + 1)
                V.tensor_tensor(x[:, n, :], tok_bank(n, 2)[:, 0:D], x[:, n, :], ALU.add).then_inc(x1_r, 1)

            def prep(n):
                t = PREP[n]
                dve.wait_ge(prep_mm, n + 1)
                src = B_TOK
                if t[0] == "anchor":
                    m0 = 4 * t[1]
                    w = min(4, M1 - m0)
                    ins = V.tensor_tensor(ab1[:, m0:m0 + w, :], src[:, 0:B * w].rearrange("p (m b) -> p m b", m=w),
                                          sm("b1", m0, w).unsqueeze(2).broadcast_to([P, w, B]), ALU.add)
                elif t[0] == "w2":
                    r = 4 * t[1] + 2 * t[2]
                    ins = V.tensor_copy(w2[:, r:r + 2, :], src[:, :].rearrange("p (r n) -> p r n", r=2))
                elif t[0] == "pk":
                    ins = V.tensor_copy(pk[:, t[1]], src[:, 0:B * KP].rearrange("p (b n) -> p b n", b=B))
                elif t[0] == "kq":
                    ins = V.tensor_scalar(kq[:, t[1], :, 0:LK], src[:, 0:B * KP].rearrange("p (b n) -> p b n", b=B)[:, :, 0:LK],
                                          D ** -0.5, None, ALU.mult)
                elif t[0] == "v":
                    v4 = src[:, 0:B * KP].rearrange("p (b n) -> p b n", b=B)
                    link(V.tensor_copy(vf[:, t[1]], v4))
                    ins = V.tensor_copy(vt[:, t[1]], v4[:, :, P:KP])
                elif t[0] == "mr":
                    ins = V.tensor_copy(mr[:, t[1]], src[:, 0:E * LK].rearrange("p (e n) -> p e n", e=E))
                elif t[0] == "b2":
                    w = 2 - t[1]
                    dve.wait_ge(ld["outb"], 16)
                    ins = V.tensor_tensor(b2[:, 2 * t[1]:2 * t[1] + w, :], src[:, 0:w * D].rearrange("p (e n) -> p e n", e=w),
                                          outb[:].unsqueeze(1).broadcast_to([P, w, D]), ALU.add)
                else:
                    ins = V.tensor_tensor(cr[:], src[:, 0:B * E].rearrange("p (b e) -> p b e", b=B),
                                          sm("rb", 0, E).unsqueeze(1).broadcast_to([P, B, E]), ALU.add)
                ins.then_inc(prep_r, 1)

            def mpiece(n):
                b, i = MP[n]
                w = min(512, W1N - 512 * i)
                o = slice(512 * i, 512 * i + w)
                dve.wait_ge(m_h, m_hi(n))
                src = M_BANK[n]
                if b is None:
                    V.tensor_tensor(mt[32:64, 0, o], src[0:32, 0:w], mt[0:32, 0, o], ALU.subtract)
                    ins = V.tensor_tensor(mt[0:32, 1, o], src[32:64, 0:w], mt[32:64, 1, o], ALU.subtract)
                else:
                    ins = V.tensor_tensor(ml[:, b, o], src[:, 0:w], mh[:, b, o], ALU.subtract)
                ins.then_inc(m_l, 1)

            def ln_stats(c):
                dve.wait_ge(x1_r, TJ * (c + 1))
                stats([(j, x[:, TJ * c + j, :]) for j in range(TJ)])
                guess().then_inc(rg_r, 1)

            def ln(c, half):
                if c == 0 and half == 0:
                    dve.wait_ge(pj_d, GR)
                if half == 0:
                    dve.wait_ge(rs_r, NC + c)
                for j in (2 * half, 2 * half + 1):
                    n = TJ * c + j
                    if n >= 2:
                        dve.wait_ge(l_t, n - 1)
                    normalised(lnt1[:, n % 2, :], j, x[:, n, :]).then_inc(l_r, 1)

            def nxsplit(c):
                for k in range(KC):
                    dve.wait_ge(nf_r, KC * c + k + 1)
                    if c >= 2:
                        dve.wait_ge(h_mm, M1 * (c - 1))
                    V.tensor_copy(nx[c % 2][:, 0, k, :], nxf[:, k, :]).then_inc(nh_r, 1)
                    dve.wait_ge(nh_r, KC * c + k + 1)
                    V.tensor_tensor(nx[c % 2][:, 1, k, :], nxf[:, k, :], nx[c % 2][:, 0, k, :], ALU.subtract).then_inc(nl_r, 1)

            def score(n):
                j = n % TJ
                dve.wait_ge(sc_d, n - n % 2 + 2)
                if j == 0 and n:
                    dve.wait_ge(le_r, 2 * (n // TJ))
                o = SC1 * (n % 2)
                link(V.tensor_copy(lg[:, j, :], B_SC[:, o + LK:o + SC1]))
                V.tensor_reduce(nmx[:, n % 2:n % 2 + 1], B_SC[:, o:o + LK], AXX, ALU.max, negate=True).then_inc(nm1_r, 1)

            def weights(n):
                if n == 0:
                    link(V.memset(pn3[:], 0.0))
                j, b, i = n % TJ, n // TJ // CPB, n % 2
                dve.wait_ge(e1_d, n + 1)
                link(V.reciprocal(rec[:, i:i + 1], sme[:, i:i + 1]))
                if n >= 2:
                    dve.wait_ge(w_t, n - 1)
                link(V.tensor_scalar(pn[:, i, :], pe_[:, i, 0:P], rec[:, i:i + 1], None, ALU.mult))
                V.tensor_scalar(pn3[:, i, :, 0:KT], pe_[:, i, P:LK].unsqueeze(1).broadcast_to([P, 3, KT]),
                                rec[:, i:i + 1], None, ALU.mult).then_inc(pn_r, 1)
                for e in range(E):
                    ins = V.tensor_tensor_reduce(out=ttr[:], in0=pe_[:, i, :], in1=mr[:, b, e, :], scale=rec[:, i:i + 1],
                                                 scalar=0.0, op0=ALU.mult, op1=ALU.add, accum_out=lw[:, j, e:e + 1])
                    if e < E - 1:
                        link(ins)
                ins.then_inc(lg_r, 1)

            def wsplit(c):
                dve.wait_ge(wh_r, 2 * c + 1)
                V.tensor_tensor(wl[:, c % 2, :], feat(c)[0][:, :], wh[:, c % 2, :], ALU.subtract).then_inc(w_r, 1)
                dve.wait_ge(wh_r, 2 * c + 2)
                V.tensor_tensor(wt[64:96, c % 2, :], feat(c)[1][64:96, :], wt[64:96, c % 2, :], ALU.subtract).then_inc(w_r, 1)

            def router(c):
                b = c // CPB
                dve.wait_ge(lg_r, TJ * (c + 1))
                link(V.tensor_tensor(lg[:], lg[:], lw[:], ALU.add))
                link(V.tensor_tensor(lg[:], lg[:], cr[:, b, :].unsqueeze(1).broadcast_to([P, TJ, E]), ALU.add))
                link(V.tensor_reduce(lx[:], lg[:], AXX, ALU.max))
                V.tensor_tensor(lg[:], lg[:], lx[:].unsqueeze(2).broadcast_to([P, TJ, E]), ALU.subtract).then_inc(le_r, 1)
                dve.wait_ge(le_r, 2 * c + 2)
                link(V.tensor_reduce(lx[:], le[:], AXX, ALU.add))
                link(V.reciprocal(lx[:], lx[:]))
                V.scalar_tensor_tensor(pr[:, c % 2], le[:], 0.5, lx[:].unsqueeze(2).broadcast_to([P, TJ, E]),
                                       ALU.mult, ALU.mult).then_inc(pr_r, 1)

            def gate(n):
                if n == 0:
                    dve.wait_ge(ld["gb2"], 16)
                dve.wait_ge(g_mm, n + 1)
                if n >= 2:
                    dve.wait_ge(th_r, n - 1)
                V.tensor_tensor(gz[:, n % 2, :], B_G[:, 0:D], gb2[:], ALU.add).then_inc(gz_r, 1)

            def w2_split(e):
                o = slice(4 * e, 4 * e + 4)
                dve.wait_ge(x1_r, TJ * NC)
                V.tensor_copy(w2h[:, o, :], w2[:, o, :]).then_inc(w2_r, 1)
                dve.wait_ge(w2_r, 2 * e + 1)
                V.tensor_tensor(w2l[:, o, :], w2[:, o, :], w2h[:, o, :], ALU.subtract).then_inc(w2_r, 1)

            def hsplit(c, m):
                q = HB * c + m
                dve.wait_ge(h_r, M1 * c + HORD.index(m) + 1)
                if q >= 3:
                    dve.wait_ge(y_mm, q - 2)
                V.tensor_copy(hs[:, q % 3, 0, :], hid[:, q % 2, :]).then_inc(hh_r, 1)

            def bias(c, e):
                for j in range(TJ):
                    p_ = pr[:, c % 2, j, e:e + 1]
                    if e == 0:
                        if c:
                            dve.wait_ge(o_r, TJ * (c - 1) + j + 1)
                        ins = V.tensor_scalar(acc[:, j, :], b2[:, e, :], p_, None, ALU.mult)
                    else:
                        ins = V.scalar_tensor_tensor(acc[:, j, :], b2[:, e, :], p_, acc[:, j, :], ALU.mult, ALU.add)
                link(ins)

            def expert_sum(c, e, j):
                dve.wait_ge(y_mm, HB * c + 4 * e + 4)
                V.scalar_tensor_tensor(acc[:, j, :], y_tile(j), pr[:, c % 2, j, e:e + 1], acc[:, j, :],
                                       ALU.mult, ALU.add).then_inc(y_r, 1)

            def final(n):
                c, j = divmod(n, TJ)
                dve.wait_ge(y_r, TJ * (E * c + E - 1) + j + 1)
                dve.wait_ge(th_r, n + 1)
                V.scalar_tensor_tensor(acc[:, j, :], th[:, j, :], 1.0, acc[:, j, :], ALU.add, ALU.mult).then_inc(f_r, 1)

            front_parts = {"ln_stats": ln_stats, "ln": ln, "nxf": nxsplit, "score": score, "weights": weights, "wsplit": wsplit,
                           "router": router}
            out_parts = {"uz": uz, "wp": wproj, "m_taken": mpiece}
            walk(l0_steps(), {"val": val, "place": place, "stats": chunk_stats, "rsqrt": chunk_rsqrt, "norm": norm, "split": xsplit, "rows": rows, "shift": shift, "prep": prep,
                              **out_parts, **front_parts})
            walk(between_steps(), {**out_parts, **front_parts})
            walk(l1_steps(), {"gate": gate, "w2_split": w2_split, "hsplit": hsplit, "bias": bias, "sum": expert_sum, "final": final, **front_parts})

        @block.tensor
        def _(pe):
            mm = nc.tensor.matmul

            def same(column):
                return column.broadcast_to([P, P])

            def passes(dst, terms, first=True, last=True, free=False):
                for i, (a, b_) in enumerate(terms):
                    ins = mm(dst, a, b_, start=first and i == 0, stop=last and i == len(terms) - 1,
                             skip_group_check=free)
                return ins

            def ss(half):
                for m in range(4 * half, 4 * half + 4):
                    ins = passes(SS_BANK[half][:, B * m:B * m + B], [(wss[:, k, m, :], csilu[:, k, :]) for k in range(KC)])
                ins.then_inc(ss_mm, 1)

            pe.wait_ge(ld_ss[1], 16)
            pe.wait_ge(silu_d, 1)
            ss(1)
            pe.wait_ge(ld["ident"], 16)
            for t in range(3):
                pe.wait_ge(cl_r, t + 1)
                w = P if t < 2 else 64
                for k in range(KC):
                    ins = nc.tensor.transpose(B_S[k][:, P * t:P * t + w], ctxt[0:w, t, P * k:P * k + P], ident[0:w, 0:w])
            ins.then_inc(cl_t, 1)

            tok = [None, None]

            def take_tok(freed, value):
                if tok[0] is not None:
                    pe.wait_ge(tok[0], tok[1])
                tok[0], tok[1] = freed, value

            def xt(c, half):
                rows_, bank_ = ln_rows(c, half)
                if (c, half) != (0, 1):
                    take_tok(xf_r, KC * (2 * c + half + 1))
                for j in (2 * half, 2 * half + 1):
                    pe.wait_ge(ln_r, TJ * c + j + 1)
                    for k in range(KC):
                        ins = nc.tensor.transpose(bank_[:, 2 * P * k + P * (j % 2):2 * P * k + P * (j % 2) + P],
                                                  rows_[:, j % 2, P * k:P * k + P], ident[:])
                ins.then_inc(ln_t, 1)

            pe.wait_ge(ld_ss[0], 16)
            ss(0)
            pe.wait_ge(ld["wk"], 16)
            pe.wait_ge(xkv_r, 2 * KC * B)
            for g in range(NG):
                passes(K_BANK[g][:, 0:B * KP],
                       [(wk[:, k, g, :], xkv[:, k, :, :].rearrange("p b n -> p (b n)")) for k in range(KC)]).then_inc(k_mm, 1)
                if g == 1:
                    xt(0, 0)
                    xt(0, 1)

            def val(n):
                b, tail = n % B, n // B
                if n == 0:
                    pe.wait_ge(ld["wv"], 16)
                    pe.wait_ge(x4_r, 1)
                    pe.wait_ge(ss_r, 2)
                elif n == 1:
                    take_tok(v_r, 2)
                else:
                    pe.wait_ge(kg_r, n - 1)
                passes(V_BANK[n][:, 0:D],
                       [((xkv4[:, k, b, :, :].rearrange("p a n -> p (a n)") if tail else xkv[:, k, b, 0:P]), wv[:, k, :])
                        for k in range(KC)]).then_inc(v_mm, 1)

            def proj(g, k):
                c, gi = divmod(g, NG)
                if g == 0:
                    pe.wait_ge(wq_r, 2)
                if g < 2:
                    pe.wait_ge(kg_r, g + 3)
                else:
                    pe.wait_ge(ql_r, g - 1)
                pe.wait_ge(xl_r, 2 * (c + 1))
                terms = [(wqh[:, k, gi, :], xh[:, k, :]), (wqh[:, k, gi, :], xl[:, k, :]), (wql[:, k, gi, :], xh[:, k, :])]
                ins = passes(B_P[g % 2][:, :], terms, first=k == 0, last=False, free=True)
                if k == KC - 1:
                    ins.then_inc(pj_d, 1)

            def rows(g, q):
                c, gi = divmod(g, NG)
                n = TJ * g + q
                pe.wait_ge(qh_r, g + 1)
                if gi == 0 and q == 0 and c % CPB == 0:
                    pe.wait_ge(ka_r, c // CPB + 1)
                if n:
                    pe.wait_ge(mx_d, n)
                for s in range(2):
                    ins = mm(B_S[s][:, 0:2 * LK], qh[:, g % 2, P * q:P * q + P],
                             ka[:, c // CPB, gi, 2 * LK * s:2 * LK * (s + 1)], start=True, stop=True)
                ins.then_inc(s1_d, 1)

            def shift(g):
                pe.wait_ge(neg_r, 1)
                for q in range(TJ):
                    pe.wait_ge(mx_d, TJ * g + q + 1)
                    ins = mm(B_P[g % 2][:, P * q:P * q + P], nm[:, g % 2, q, :], negI[:], start=False, stop=q == TJ - 1,
                             skip_group_check=True)
                ins.then_inc(nm_d, 1)

            def keys(g, k):
                c, gi = divmod(g, NG)
                b = c // CPB
                n = (GH + 1) * g + k
                if k == 0:
                    pe.wait_ge(ql_r, g + 1)
                if n == 0:
                    pe.wait_ge(kb_r, 2 * GH)
                    pe.wait_ge(v_r, 2 * B)
                if n >= 2:
                    pe.wait_ge(ex_d, n - 1)
                if k < GH:
                    a, b_ = ka[:, b, gi, LK * k:LK * k + P], kb[:, b, gi, P * k:P * k + P]
                else:
                    a, b_ = ka[:, b, gi, LK * GH:LK * GH + P], kb[:, b, gi, P * GH:P * GH + P]
                passes(B_ST[n % 2][:, :], [(a, qh[:, g % 2, :]), (b_, ql[:, g % 2, :])]).then_inc(st_d, 1)

            def av(g):
                c, gi = divmod(g, NG)
                b = c // CPB
                if g == 0:
                    pe.wait_ge(v_r, 2 * B)
                    pe.wait_ge(ones_r, 1)
                else:
                    pe.wait_ge(u_r, g)
                for j in range(GH):
                    pe.wait_ge(ex_d, (GH + 1) * g + j + 1)
                    mm(B_U[32 * j:32 * j + 32, :], vmain[:, b, GH * gi + j, :], pt[:, j, :], start=True, stop=False,
                       skip_group_check=True)
                pe.wait_ge(ex_d, (GH + 1) * (g + 1))
                mm(B_U[:, :], vtail[:, b, gi, :], pt[:, GH, :], start=False, stop=True,
                   skip_group_check=True).then_inc(av_d, 1)

            def uz(n):
                c, j = divmod(n, TJ)
                pe.wait_ge(u_r, NG * (c + 1))
                if n <= LAST:
                    take_tok(z_r, n + 1)
                dst = tok_bank(n, 0)
                for gi in range(NG):
                    ins = nc.tensor.transpose(dst[:, P * gi:P * gi + P], u[:, (NG * c + gi) % NU, P * j:P * j + P], ident[:])
                ins.then_inc(uz_d, 1)

            def ztr(n):
                if n < LAST:
                    take_tok(zt_r, n + 1)
                else:
                    pe.wait_ge(z_r, n + 1)
                    pe.wait_ge(x1_r, n)
                dst = tok_bank(n, 1)
                for k in range(KC):
                    ins = nc.tensor.transpose(dst[:, P * k:P * k + P], z[:, n % 2, P * k:P * k + P], ident[:])
                ins.then_inc(zt_d, 1)

            def wproj(n):
                if n == 0:
                    pe.wait_ge(ld["wp"], 16)
                if n < LAST:
                    take_tok(x1_r, n + 1)
                else:
                    pe.wait_ge(zt_r, n + 1)
                passes(tok_bank(n, 2)[:, 0:D], [(zt[:, n % 2, k, :], wp[:, k, :]) for k in range(KC)]).then_inc(wp_d, 1)

            def prep(n):
                t = PREP[n]
                if n:
                    pe.wait_ge(prep_r, n)
                take_tok(prep_r, n + 1)
                st, bk_ = stage[0], B_TOK
                if t[0] == "anchor":
                    i = t[1]
                    pe.wait_ge(ld_a[i], 16)
                    for m in range(4 * i, min(4 * i + 4, M1)):
                        o = P * (m - 4 * i)
                        ins = passes(bk_[:, B * (m - 4 * i):B * (m - 4 * i) + B],
                                     [(st[:, k, o:o + P], sm("cond", B * k, B)) for k in range(KC)])
                elif t[0] == "w2":
                    pe.wait_ge(ld_a[4 + t[1]], 16)
                    pe.wait_ge(ld["outw"], 16)
                    for r in range(2):
                        o = P * (2 * t[2] + r)
                        ins = passes(bk_[:, D * r:D * r + D], [(st[:, k, o:o + P], outw[:, k, :]) for k in range(KC)])
                elif t[0] in ("pk", "v"):
                    pe.wait_ge(ld["ctxT"], 16)
                    w = pw[:, 1 if t[0] == "pk" else 2]
                    pe.wait_ge(ld["pwk" if t[0] == "pk" else "pwv"], 16)
                    ins = passes(bk_[:, 0:B * KP], [(w[:, k, P * t[1]:P * t[1] + P], ctxT[:, k].rearrange("p b n -> p (b n)"))
                                                    for k in range(KC)])
                elif t[0] == "kq":
                    pe.wait_ge(ld["pwqT"], 16)
                    ins = passes(bk_[:, 0:B * KP], [(pw[:, 0, k, P * t[1]:P * t[1] + P], pk[:, k].rearrange("p b n -> p (b n)"))
                                                    for k in range(KC)])
                elif t[0] == "mr":
                    for e in range(E):
                        ins = passes(bk_[:, LK * e:LK * e + LK], [(same(sm("rwe", E * k + e)), vf[:, k, t[1], 0:LK]) for k in range(KC)])
                elif t[0] == "b2":
                    pe.wait_ge(ld["outw"], 16)
                    for e in range(2 * t[1], min(2 * t[1] + 2, E)):
                        o = D * (e - 2 * t[1])
                        ins = passes(bk_[:, o:o + D], [(same(sm("eb2", E * k + e)), outw[:, k, :]) for k in range(KC)])
                else:
                    for b in range(B):
                        ins = passes(bk_[:, E * b:E * b + E], [(same(sm("cond", B * k + b)), sm("rwa", E * k, E)) for k in range(KC)])
                ins.then_inc(prep_mm, 1)

            def mpiece(n):
                b, i = MP[n]
                w = min(512, W1N - 512 * i)
                if n == 0:
                    pe.wait_ge(ld["w1e"], 16)
                    pe.wait_ge(prep_r, len(OPS))
                if n < NM0:
                    take_tok(m_l, n + 1)
                if n == NM0:
                    pe.wait_ge(ex_d, (GH + 1) * GR)
                    pe.wait_ge(u_r, GR)
                    pe.wait_ge(ql_r, GR)
                if n >= NM0 + 3:
                    pe.wait_ge(m_l, n - 2)
                src = M_BANK[n]
                rows_ = P if b is not None else 32 * B
                passes(src[0:rows_, 0:w],
                       [((vt[:, k].rearrange("p b n -> p (b n)") if b is None else vf[:, k, b, 0:P]),
                         w1e[:, k, 512 * i:512 * i + w]) for k in range(KC)]).then_inc(m_mm, 1)

            def nxt(c, half):
                if c and half == 0:
                    pe.wait_ge(w_r, 2 * c)
                    pe.wait_ge(x1_r, TJ * NC)
                elif half == 0:
                    pe.wait_ge(mx_d, TJ * GR)
                for j in (2 * half, 2 * half + 1):
                    n = TJ * c + j
                    pe.wait_ge(l_r, n + 1)
                    for k in range(KC):
                        ins = nc.tensor.transpose(feat(c)[k][:, P * j:P * j + P], lnt1[:, n % 2, P * k:P * k + P], ident[:])
                    ins.then_inc(l_t, 1)

            def score(n):
                c, j = divmod(n, TJ)
                pe.wait_ge(nf_r, KC * (c + 1))
                if n == 0:
                    pe.wait_ge(prep_r, len(OPS))
                    pe.wait_ge(ql_r, GR)
                if n >= 2:
                    pe.wait_ge(e1_d, n - n % 2)
                passes(B_SC[:, SC1 * (n % 2):SC1 * (n % 2) + SC1], [(nxf[:, k, P * j:P * j + P], kq[:, k, c // CPB, :]) for k in range(KC)]).then_inc(sc_d, 1)

            def wtr(n):
                c, j = divmod(n, TJ)
                pe.wait_ge(pn_r, n + 1)
                nc.tensor.transpose(feat(c)[0][:, P * j:P * j + P], pn[:, n % 2, :], ident[:])
                nc.tensor.transpose(feat(c)[1][0:TAIL3, P * j:P * j + P], pn3[:, n % 2].rearrange("p a n -> p (a n)"),
                                    ident[:]).then_inc(w_t, 1)

            def hidden(c, m):
                n = M1 * c + HORD.index(m)
                b = c // CPB
                if n == 0:
                    pe.wait_ge(w1_r, 2 * NW1)
                if m == HB:
                    pe.wait_ge(nl_r, KC * (c + 1))
                    pe.wait_ge(w_r, 2 * (c + 1))
                    pe.wait_ge(m_l, MTAIL + 1 if b == 0 else len(MP))
                    pe.wait_ge(mt_r, 16 * B)
                if n >= 2:
                    pe.wait_ge(h_r, n - 1)
                o = slice(P * m, P * m + P)
                h, l = nx[c % 2][:, 0], nx[c % 2][:, 1]
                terms = []
                for k in range(KC):
                    terms += [(w1h[:, k, o], h[:, k, :]), (w1h[:, k, o], l[:, k, :]), (w1l[:, k, o], h[:, k, :])]
                terms += [(mh[:, b, o], wh[:, c % 2, :]), (mh[:, b, o], wl[:, c % 2, :]), (ml[:, b, o], wh[:, c % 2, :]),
                          (mt[:, b, o], wt[:, c % 2, :])]
                passes(B_H[n % 2][:, :], terms).then_inc(h_mm, 1)

            def gate(n):
                c, j = divmod(n, TJ)
                if n == 0:
                    pe.wait_ge(ld["gw2"], 16)
                pe.wait_ge(h_r, M1 * c + GB)
                if n:
                    pe.wait_ge(gz_r, n)
                passes(B_G[:, 0:D], [(hg[:, k, P * j:P * j + P], gw2[:, k, :]) for k in range(KC)]).then_inc(g_mm, 1)

            def part(c, m):
                q = HB * c + m
                e, r = divmod(m, 4)
                pe.wait_ge(hl_r, q + 1)
                if c == 0 and r == 0:
                    pe.wait_ge(w2_r, 2 * e + 2)
                for j in range(TJ):
                    if r == 0 and q and j % 2 == 0:
                        pe.wait_ge(y_r, TJ * (E * c + e - 1) + j + 2)
                    hi, lo = hs[:, q % 3, 0, P * j:P * j + P], hs[:, q % 3, 1, P * j:P * j + P]
                    ins = passes(y_tile(j), [(hi, w2h[:, m, :]), (lo, w2h[:, m, :]), (hi, w2l[:, m, :])],
                                 first=r == 0 and j % 2 == 0, last=r == 3, free=True)
                ins.then_inc(y_mm, 1)

            rows_parts = {"uz": uz, "zt": ztr, "wp": wproj, "m": mpiece}
            front_parts = {"nxt": nxt, "score": score, "wtr": wtr}
            walk(l0_steps(), {"xt": xt, "val": val, "proj": proj, "rows": rows, "shift": shift, "keys": keys, "av": av, "prep": prep,
                              **rows_parts, **front_parts})
            walk(between_steps(), {**rows_parts, **front_parts})
            walk(l1_steps(), {"nxt": nxt, "score": score, "wtr": wtr, "hidden": hidden, "gate": gate, "part": part})


def laid_out(v):
    f = lambda name: np.ascontiguousarray(v[name])
    chunks = lambda w: w.reshape(w.shape[0] // P, P, -1).transpose(1, 0, 2)
    rep = lambda row, n=P: np.broadcast_to(row, (n,) + row.shape)
    x, ctx_, cond = f("x"), f("ctx_1024"), f("cond_1024")
    zeros = lambda *s: np.zeros(s, x.dtype)
    twice = lambda w: np.repeat(w.reshape(-1, NG, GH, 1, DH), 2, axis=3).reshape(w.shape[0], NG * P)
    wkv, bkv = f("L0_xcond_Wkv"), f("L0_xcond_bkv")
    a = {"x": x.reshape(B * LQ // P, P, D).transpose(1, 0, 2)}
    p = np.arange(P)
    cols = lambda vec: vec.reshape(-1, P).T
    rw, w1 = f("L1_xcond_router_W"), np.concatenate([*f("L1_xcond_e_w1"), f("L1_xcond_gate_w1")], axis=1)
    w1r = np.concatenate([f("L1_xcond_e_b1").ravel(), f("L1_xcond_gate_b1")])
    bss = np.concatenate([f("L0_xcond_bss_q"), f("L0_xcond_bss_kv")])
    a["small"] = np.concatenate([
        chunks(cond.T).reshape(P, -1), cols(bss), cols(twice(f("L0_xcond_bq")[None])[0]), cols(twice(bkv[None, :D])[0]),
        cols(f("L1_xcond_ln_gamma")), cols(f("L1_xcond_ln_beta")), cols(w1r), rep(f("L1_xcond_router_b")),
        (p % 32 < DH).astype(np.float32)[:, None], (p % 32 >= DH).astype(np.float32)[:, None], (p % 32 == DH).astype(np.float32)[:, None],
        (p % 32 < KT).astype(np.float32)[:, None],
        chunks(rw[0:D]).reshape(P, -1), chunks(rw[2 * D:]).reshape(P, -1),
        chunks(rw[D:2 * D]).reshape(P, -1), chunks(f("L1_xcond_e_b2").T).reshape(P, -1)], axis=1)
    a["ident"] = np.eye(P, dtype=np.float32)
    ct = zeros(P, 3, D)
    for b in range(B):
        ct[:, b] = ctx_[b, 0:P]
        ct[32 * b:32 * b + KT, 2] = ctx_[b, P:]
    a["ctx"] = ct
    cT = zeros(P, KC, B, KP)
    for b in range(B):
        cT[:, :, b, 0:LK] = chunks(ctx_[b].T)
    a["ctxT"] = cT
    a["wss"] = chunks(np.concatenate([f("L0_xcond_Wss_q"), f("L0_xcond_Wss_kv")], axis=1)).reshape(P, KC, 8, P)
    a["wq"] = chunks(twice(f("L0_xcond_Wq"))).reshape(P, KC, NG, P)
    a["wk"] = chunks(twice(wkv[:, :D])).reshape(P, KC, NG, P)
    a["wv"], a["bv"] = chunks(wkv[:, D:]), rep(bkv[D:])
    a["wp"], a["bp"] = chunks(f("L0_xcond_Wp")), rep(f("L0_xcond_bp"))
    a["pwqT"], a["pwk"], a["pwv"] = chunks(f("L1_xcond_Wq").T), chunks(f("L1_xcond_Wk")), chunks(f("L1_xcond_Wv"))
    a["w1n"], a["w1e"], a["w1a"] = chunks(w1[0:D]), chunks(w1[D:2 * D]), chunks(w1[2 * D:])
    a["ew2T"] = chunks(f("L1_xcond_e_w2").reshape(E * RH, D).T)
    a["outw"], a["outb"] = chunks(f("L1_xcond_out_w")), rep(f("L1_xcond_out_b"))
    a["gw2"], a["gb2"] = chunks(f("L1_xcond_gate_w2")), rep(f("L1_xcond_gate_b2"))
    return {n: np.ascontiguousarray(a[n].reshape(s)) for n, s in SHAPES.items()}


def kernel(**inputs):
    import concourse.bacc as bacc
    from concourse.bass_utils import run_bass_kernel_spmd

    nc = bacc.Bacc("TRN2", target_bir_lowering=False, num_devices=1)
    arrays = laid_out({k: np.asarray(v) for k, v in inputs.items()})
    dram = {n: nc.dram_tensor(f"in_{n}", s, F32, kind="ExternalInput").ap() for n, s in SHAPES.items()}
    out = nc.dram_tensor("out_x", SHAPES["x"], F32, kind="ExternalOutput").ap()
    build(nc, dram, out)
    r = run_bass_kernel_spmd(nc, [{f"in_{n}": a for n, a in arrays.items()}], core_ids=[0])
    return r.results[0]["out_x"].transpose(1, 0, 2).reshape(B, LQ, D)
```
